# Optimizing a Trainium2 kernel written in Bass

```python
import numpy as np
import jax
import jax.numpy as jnp

def _softmax(x, axis=-1):
    return jax.nn.softmax(x, axis=axis)

def _gelu(x):
    return jax.nn.gelu(x, approximate=True)

def _silu(x):
    return jax.nn.silu(x)

def _sigmoid(x):
    return jax.nn.sigmoid(x)

def _layernorm(x, axis=-1, eps=1e-05):
    m = jnp.mean(x, axis=axis, keepdims=True)
    v = jnp.var(x, axis=axis, keepdims=True)
    return (x - m) / jnp.sqrt(v + eps)

def _scatter_add(tgt, idx, src, axis=0):
    return tgt.at[idx].add(src)

def _segment_sum(src, seg, n):
    return jax.ops.segment_sum(src, seg, n)
kernel_name = 'mk_vit_tower_d1_tok_img512_r4_bd225f'

def setup_inputs(seed: int=0):
    np.random.seed(seed)
    _w = jnp.asarray

    def _rec_inputs():
        import jax
        import jax.numpy as jnp
        _rk = jax.random.key(seed)
        x = -0.000190493 + 0.999948 * jax.random.normal(jax.random.fold_in(_rk, 1), (128, 2, 104, 104), jnp.float32)
        return x
    x = _rec_inputs()

    def _L0_tok_setup():
        import jax, jax.numpy as jnp
        import numpy as np
        HP = 4
        PATCH = 8
        EPS = 1e-07

        def _shifts(x):
            h, w = (x.shape[2], x.shape[3])
            pad2 = ((0, 0), (0, 0))
            left_up = jnp.pad(x[:, :, HP:, :w - HP], pad2 + ((0, HP), (HP, 0)))
            right_up = jnp.pad(x[:, :, HP:, HP:], pad2 + ((0, HP), (0, HP)))
            left_down = jnp.pad(x[:, :, :h - HP, :w - HP], pad2 + ((HP, 0), (HP, 0)))
            right_down = jnp.pad(x[:, :, :h - HP, HP:], pad2 + ((HP, 0), (0, HP)))
            return (left_up, right_up, left_down, right_down)
        key = jax.random.key(seed)
        k1, k2, k3, k4 = jax.random.split(key, 4)
        B, C, S = (128, 2, 104)
        embed_dim = 128
        x = jax.random.normal(k1, (B, C, S, S), dtype=jnp.float32)
        gamma = 1.0 + 0.05 * jax.random.normal(k2, (10, S, S), dtype=jnp.float32)
        beta = 0.05 * jax.random.normal(k3, (10, S, S), dtype=jnp.float32)
        W = 0.02 * jax.random.normal(k4, (embed_dim, 10, PATCH, PATCH), dtype=jnp.float32)
        b = jnp.zeros((embed_dim,), dtype=jnp.float32)
        return {'x': x, 'gamma': gamma, 'beta': beta, 'W': W, 'b': b}
    _L0_tok_all = _L0_tok_setup()
    _L0_tok_in = {k: v for k, v in _L0_tok_all.items() if k in ('gamma', 'beta', 'W', 'b')}
    del _L0_tok_all

    def _L0_attn_setup():
        import jax, jax.numpy as jnp
        import numpy as np
        D_IN = 128
        D_MODEL = 64
        D_STATE = 128
        D_CONV = 4
        D_INNER = 128
        DT_RANK = 16
        B, L = (8, 512)

        def _mamba(x, in_w, conv_w, conv_b, xproj_w, dt_w, dt_b, A_log, Dp, outp_w):
            Bb, Ls, _ = x.shape
            xz = x @ in_w.T
            u, z = jnp.split(xz, 2, axis=-1)
            up = jnp.pad(u, ((0, 0), (D_CONV - 1, 0), (0, 0)))
            u = conv_b + sum((up[:, k:k + Ls, :] * conv_w[:, k] for k in range(D_CONV)))
            u = jax.nn.silu(u)
            dbl = u @ xproj_w.T
            delta = jax.nn.softplus(dbl[..., :DT_RANK] @ dt_w.T + dt_b)
            Bm = dbl[..., DT_RANK:DT_RANK + D_STATE]
            Cm = dbl[..., DT_RANK + D_STATE:]
            A = -jnp.exp(A_log)

            def step(h, inp):
                d_t, b_t, c_t, u_t = inp
                h = jnp.exp(d_t[..., None] * A) * h + d_t[..., None] * b_t[:, None, :] * u_t[..., None]
                y = jnp.einsum('bds,bs->bd', h, c_t)
                return (h, y)
            h0 = jnp.zeros((Bb, D_INNER, D_STATE), x.dtype)
            xs = (jnp.swapaxes(delta, 0, 1), jnp.swapaxes(Bm, 0, 1), jnp.swapaxes(Cm, 0, 1), jnp.swapaxes(u, 0, 1))
            _, ys = jax.lax.scan(step, h0, xs)
            y = jnp.swapaxes(ys, 0, 1) + u * Dp
            y = y * jax.nn.silu(z)
            return y @ outp_w.T
        key = jax.random.key(seed)
        ks = iter(jax.random.split(key, 64))
        w = lambda *s: jax.random.normal(next(ks), s, jnp.float32) * 0.02
        d = {'x': jax.random.normal(next(ks), (B, L, D_IN), jnp.float32), 'mlp_w': w(D_MODEL, D_IN), 'mlp_b': w(D_MODEL), 'mlpres_w': w(D_MODEL, D_IN), 'mlpres_b': w(D_MODEL), 'fl_w': w(D_MODEL, D_MODEL), 'fl_b': w(D_MODEL), 'bl_w': w(D_MODEL, D_MODEL), 'bl_b': w(D_MODEL), 'out_w': w(D_IN, D_MODEL), 'out_b': w(D_IN)}
        for p in ('f_', 'b_'):
            d[p + 'in_w'] = w(2 * D_INNER, D_MODEL)
            d[p + 'conv_w'] = w(D_INNER, D_CONV)
            d[p + 'conv_b'] = w(D_INNER)
            d[p + 'xproj_w'] = w(DT_RANK + 2 * D_STATE, D_INNER)
            d[p + 'dt_w'] = w(D_INNER, DT_RANK)
            d[p + 'dt_b'] = jnp.full((D_INNER,), -4.6, jnp.float32)
            d[p + 'Alog'] = jnp.log(jnp.arange(1, D_STATE + 1, dtype=jnp.float32)) * jnp.ones((D_INNER, 1), jnp.float32)
            d[p + 'D'] = jnp.ones((D_INNER,), jnp.float32)
            d[p + 'outp_w'] = w(D_MODEL, D_INNER)
        return d
    _L0_attn_all = _L0_attn_setup()
    _L0_attn_in = {k: v for k, v in _L0_attn_all.items() if k in ('mlp_w', 'mlp_b', 'mlpres_w', 'mlpres_b', 'fl_w', 'fl_b', 'bl_w', 'bl_b', 'out_w', 'out_b', 'f_in_w', 'f_conv_w', 'f_conv_b', 'f_xproj_w', 'f_dt_w', 'f_dt_b', 'f_Alog', 'f_D', 'f_outp_w', 'b_in_w', 'b_conv_w', 'b_conv_b', 'b_xproj_w', 'b_dt_w', 'b_dt_b', 'b_Alog', 'b_D', 'b_outp_w')}
    del _L0_attn_all

    def _L0_ffn_setup():
        import jax, jax.numpy as jnp
        import numpy as np
        B, S, D, F, E = (4, 512, 128, 512, 8)
        key = jax.random.key(seed)
        k = jax.random.split(key, 5)
        x = jax.random.normal(k[0], (B, S, D), dtype=jnp.float32)
        Ws = jax.random.normal(k[1], (D, E), dtype=jnp.float32) * 0.02
        bs = jnp.zeros((E,), dtype=jnp.float32)
        W1 = jax.random.normal(k[2], (E, D, F), dtype=jnp.float32) * 0.02
        b1 = jnp.zeros((E, F), dtype=jnp.float32)
        W2 = jax.random.normal(k[3], (E, F, D), dtype=jnp.float32) * 0.02
        b2 = jnp.zeros((E, D), dtype=jnp.float32)
        return {'x': x, 'Ws': Ws, 'bs': bs, 'W1': W1, 'b1': b1, 'W2': W2, 'b2': b2}
    _L0_ffn_all = _L0_ffn_setup()
    _L0_ffn_in = {k: v for k, v in _L0_ffn_all.items() if k in ('Ws', 'bs', 'W1', 'b1', 'W2', 'b2')}
    del _L0_ffn_all
    return {'x': x, 'L0_tok_gamma': _L0_tok_in['gamma'], 'L0_tok_beta': _L0_tok_in['beta'], 'L0_tok_W': _L0_tok_in['W'], 'L0_tok_b': _L0_tok_in['b'], 'L0_attn_mlp_w': _L0_attn_in['mlp_w'], 'L0_attn_mlp_b': _L0_attn_in['mlp_b'], 'L0_attn_mlpres_w': _L0_attn_in['mlpres_w'], 'L0_attn_mlpres_b': _L0_attn_in['mlpres_b'], 'L0_attn_fl_w': _L0_attn_in['fl_w'], 'L0_attn_fl_b': _L0_attn_in['fl_b'], 'L0_attn_bl_w': _L0_attn_in['bl_w'], 'L0_attn_bl_b': _L0_attn_in['bl_b'], 'L0_attn_out_w': _L0_attn_in['out_w'], 'L0_attn_out_b': _L0_attn_in['out_b'], 'L0_attn_f_in_w': _L0_attn_in['f_in_w'], 'L0_attn_f_conv_w': _L0_attn_in['f_conv_w'], 'L0_attn_f_conv_b': _L0_attn_in['f_conv_b'], 'L0_attn_f_xproj_w': _L0_attn_in['f_xproj_w'], 'L0_attn_f_dt_w': _L0_attn_in['f_dt_w'], 'L0_attn_f_dt_b': _L0_attn_in['f_dt_b'], 'L0_attn_f_Alog': _L0_attn_in['f_Alog'], 'L0_attn_f_D': _L0_attn_in['f_D'], 'L0_attn_f_outp_w': _L0_attn_in['f_outp_w'], 'L0_attn_b_in_w': _L0_attn_in['b_in_w'], 'L0_attn_b_conv_w': _L0_attn_in['b_conv_w'], 'L0_attn_b_conv_b': _L0_attn_in['b_conv_b'], 'L0_attn_b_xproj_w': _L0_attn_in['b_xproj_w'], 'L0_attn_b_dt_w': _L0_attn_in['b_dt_w'], 'L0_attn_b_dt_b': _L0_attn_in['b_dt_b'], 'L0_attn_b_Alog': _L0_attn_in['b_Alog'], 'L0_attn_b_D': _L0_attn_in['b_D'], 'L0_attn_b_outp_w': _L0_attn_in['b_outp_w'], 'L0_ffn_Ws': _L0_ffn_in['Ws'], 'L0_ffn_bs': _L0_ffn_in['bs'], 'L0_ffn_W1': _L0_ffn_in['W1'], 'L0_ffn_b1': _L0_ffn_in['b1'], 'L0_ffn_W2': _L0_ffn_in['W2'], 'L0_ffn_b2': _L0_ffn_in['b2']}

def reference(x, L0_tok_gamma, L0_tok_beta, L0_tok_W, L0_tok_b, L0_attn_mlp_w, L0_attn_mlp_b, L0_attn_mlpres_w, L0_attn_mlpres_b, L0_attn_fl_w, L0_attn_fl_b, L0_attn_bl_w, L0_attn_bl_b, L0_attn_out_w, L0_attn_out_b, L0_attn_f_in_w, L0_attn_f_conv_w, L0_attn_f_conv_b, L0_attn_f_xproj_w, L0_attn_f_dt_w, L0_attn_f_dt_b, L0_attn_f_Alog, L0_attn_f_D, L0_attn_f_outp_w, L0_attn_b_in_w, L0_attn_b_conv_w, L0_attn_b_conv_b, L0_attn_b_xproj_w, L0_attn_b_dt_w, L0_attn_b_dt_b, L0_attn_b_Alog, L0_attn_b_D, L0_attn_b_outp_w, L0_ffn_Ws, L0_ffn_bs, L0_ffn_W1, L0_ffn_b1, L0_ffn_W2, L0_ffn_b2):
    import jax
    import jax.numpy as jnp

    def _L0_tok_ref(x, gamma, beta, W, b):
        import jax, jax.numpy as jnp
        import numpy as np
        HP = 4
        PATCH = 8
        EPS = 1e-07

        def _shifts(x):
            h, w = (x.shape[2], x.shape[3])
            pad2 = ((0, 0), (0, 0))
            left_up = jnp.pad(x[:, :, HP:, :w - HP], pad2 + ((0, HP), (HP, 0)))
            right_up = jnp.pad(x[:, :, HP:, HP:], pad2 + ((0, HP), (0, HP)))
            left_down = jnp.pad(x[:, :, :h - HP, :w - HP], pad2 + ((HP, 0), (HP, 0)))
            right_down = jnp.pad(x[:, :, :h - HP, HP:], pad2 + ((HP, 0), (0, HP)))
            return (left_up, right_up, left_down, right_down)
        lu, ru, ld, rd = _shifts(x)
        concat = jnp.concatenate((x, lu, ru, ld, rd), axis=1)
        mean = jnp.mean(concat, axis=(1, 2, 3), keepdims=True)
        var = jnp.var(concat, axis=(1, 2, 3), keepdims=True)
        normed = (concat - mean) * jax.lax.rsqrt(var + EPS)
        normed = normed * gamma[None] + beta[None]
        y = jax.lax.conv_general_dilated(normed, W, window_strides=(PATCH, PATCH), padding='VALID', dimension_numbers=('NCHW', 'OIHW', 'NCHW'))
        y = y + b[None, :, None, None]
        B, E = (y.shape[0], y.shape[1])
        y = y.reshape(B, E, -1).transpose(0, 2, 1)
        return y

    def _L0_attn_ref(x, mlp_w, mlp_b, mlpres_w, mlpres_b, fl_w, fl_b, bl_w, bl_b, out_w, out_b, f_in_w, f_conv_w, f_conv_b, f_xproj_w, f_dt_w, f_dt_b, f_Alog, f_D, f_outp_w, b_in_w, b_conv_w, b_conv_b, b_xproj_w, b_dt_w, b_dt_b, b_Alog, b_D, b_outp_w):
        import jax, jax.numpy as jnp
        import numpy as np
        D_IN = 128
        D_MODEL = 64
        D_STATE = 128
        D_CONV = 4
        D_INNER = 128
        DT_RANK = 16
        B, L = (8, 512)

        def _mamba(x, in_w, conv_w, conv_b, xproj_w, dt_w, dt_b, A_log, Dp, outp_w):
            Bb, Ls, _ = x.shape
            xz = x @ in_w.T
            u, z = jnp.split(xz, 2, axis=-1)
            up = jnp.pad(u, ((0, 0), (D_CONV - 1, 0), (0, 0)))
            u = conv_b + sum((up[:, k:k + Ls, :] * conv_w[:, k] for k in range(D_CONV)))
            u = jax.nn.silu(u)
            dbl = u @ xproj_w.T
            delta = jax.nn.softplus(dbl[..., :DT_RANK] @ dt_w.T + dt_b)
            Bm = dbl[..., DT_RANK:DT_RANK + D_STATE]
            Cm = dbl[..., DT_RANK + D_STATE:]
            A = -jnp.exp(A_log)

            def step(h, inp):
                d_t, b_t, c_t, u_t = inp
                h = jnp.exp(d_t[..., None] * A) * h + d_t[..., None] * b_t[:, None, :] * u_t[..., None]
                y = jnp.einsum('bds,bs->bd', h, c_t)
                return (h, y)
            h0 = jnp.zeros((Bb, D_INNER, D_STATE), x.dtype)
            xs = (jnp.swapaxes(delta, 0, 1), jnp.swapaxes(Bm, 0, 1), jnp.swapaxes(Cm, 0, 1), jnp.swapaxes(u, 0, 1))
            _, ys = jax.lax.scan(step, h0, xs)
            y = jnp.swapaxes(ys, 0, 1) + u * Dp
            y = y * jax.nn.silu(z)
            return y @ outp_w.T
        nrm = jnp.sqrt(jnp.sum(x * x, axis=1, keepdims=True))
        x_norm = x / jnp.maximum(nrm, 1e-12)
        x_up = x_norm @ mlp_w.T + mlp_b
        x_f = _mamba(x_up @ fl_w.T + fl_b, f_in_w, f_conv_w, f_conv_b, f_xproj_w, f_dt_w, f_dt_b, f_Alog, f_D, f_outp_w)
        x_b = x_up @ bl_w.T + bl_b
        x_b = jnp.flip(_mamba(jnp.flip(x_b, axis=1), b_in_w, b_conv_w, b_conv_b, b_xproj_w, b_dt_w, b_dt_b, b_Alog, b_D, b_outp_w), axis=1)
        z = jax.nn.leaky_relu(x_norm @ mlpres_w.T + mlpres_b, negative_slope=0.01)
        x_fusion = (x_f + x_b) * z
        return x_fusion @ out_w.T + out_b + x

    def _L0_ffn_ref(x, Ws, bs, W1, b1, W2, b2):
        import jax, jax.numpy as jnp
        import numpy as np
        B, S, D, F, E = (4, 512, 128, 512, 8)
        Bb, Ss, Dd = x.shape
        xt = x.reshape(-1, Dd)
        logits = xt @ Ws + bs
        probs = jax.nn.softmax(logits, axis=-1)
        prob_max = jnp.max(probs, axis=-1)
        routes = jnp.argmax(probs, axis=-1)
        onehot = jax.nn.one_hot(routes, W1.shape[0], dtype=xt.dtype)

        def expert_ffn(w1, bb1, w2, bb2):
            h = jax.nn.gelu(xt @ w1 + bb1, approximate=False)
            return h @ w2 + bb2
        y = jax.vmap(expert_ffn)(W1, b1, W2, b2)
        out = jnp.einsum('te,etd->td', onehot, y)
        out = out * prob_max[:, None]
        return out.reshape(Bb, Ss, Dd)
    h = _L0_tok_ref(x, L0_tok_gamma, L0_tok_beta, L0_tok_W, L0_tok_b)
    h = h + _L0_attn_ref(_layernorm(h, axis=-1), L0_attn_mlp_w, L0_attn_mlp_b, L0_attn_mlpres_w, L0_attn_mlpres_b, L0_attn_fl_w, L0_attn_fl_b, L0_attn_bl_w, L0_attn_bl_b, L0_attn_out_w, L0_attn_out_b, L0_attn_f_in_w, L0_attn_f_conv_w, L0_attn_f_conv_b, L0_attn_f_xproj_w, L0_attn_f_dt_w, L0_attn_f_dt_b, L0_attn_f_Alog, L0_attn_f_D, L0_attn_f_outp_w, L0_attn_b_in_w, L0_attn_b_conv_w, L0_attn_b_conv_b, L0_attn_b_xproj_w, L0_attn_b_dt_w, L0_attn_b_dt_b, L0_attn_b_Alog, L0_attn_b_D, L0_attn_b_outp_w)
    h = h + _L0_ffn_ref(_layernorm(h, axis=-1), L0_ffn_Ws, L0_ffn_bs, L0_ffn_W1, L0_ffn_b1, L0_ffn_W2, L0_ffn_b2)
    return h

_drawn_inputs = setup_inputs


def setup_inputs(seed=0):
    import zlib

    import numpy as np

    out = dict(_drawn_inputs(seed))
    spreads = {'L0_tok_b': (0.0, 0.1),
     'L0_attn_f_dt_b': (-4.599999904632568, 0.6),
     'L0_attn_f_D': (1.0, 0.6),
     'L0_attn_b_dt_b': (-4.599999904632568, 0.6),
     'L0_attn_b_D': (1.0, 0.6),
     'L0_ffn_bs': (0.0, 0.8),
     'L0_ffn_b1': (0.0, 0.8),
     'L0_ffn_b2': (0.0, 0.71)}
    factors = {'L0_attn_mlp_w': 8.0,
     'L0_attn_mlp_b': 8.0,
     'L0_attn_mlpres_w': 8.0,
     'L0_attn_mlpres_b': 8.0,
     'L0_attn_fl_w': 8.0,
     'L0_attn_fl_b': 8.0,
     'L0_attn_bl_w': 8.0,
     'L0_attn_bl_b': 8.0,
     'L0_attn_out_w': 8.0,
     'L0_attn_out_b': 3.743,
     'L0_attn_f_in_w': 8.0,
     'L0_attn_f_conv_w': 8.0,
     'L0_attn_f_conv_b': 8.0,
     'L0_attn_f_outp_w': 8.0,
     'L0_attn_b_in_w': 8.0,
     'L0_attn_b_conv_w': 8.0,
     'L0_attn_b_conv_b': 8.0,
     'L0_attn_b_outp_w': 8.0,
     'L0_ffn_Ws': 4.623,
     'L0_ffn_W1': 8.0,
     'L0_ffn_W2': 8.0,
     'L0_attn_f_xproj_w': 64.0,
     'L0_attn_f_dt_w': 64.0,
     'L0_attn_f_Alog': 62.636,
     'L0_attn_b_xproj_w': 64.0,
     'L0_attn_b_dt_w': 64.0,
     'L0_attn_b_Alog': 64.0}
    for name, (base, spread) in spreads.items():
        noise = np.random.default_rng([zlib.crc32(name.encode()), seed]).standard_normal(out[name].shape)
        drawn = base * np.exp(spread * noise) if base else spread * noise
        out[name] = jnp.asarray(drawn.astype(out[name].dtype))
    for name, factor in factors.items():
        out[name] = (out[name] * factor).astype(out[name].dtype)
    return out
```

```python
from contextlib import ExitStack

import numpy as np

import concourse.bass as bass
from concourse import mybir

BATCH, CH, SIDE, PATCH, HALF = 128, 2, 104, 8, 4
GRID = SIDE // PATCH
L = GRID * GRID
D = 128
DM = 64
RANK = 16
KCONV = 4
IMGS = 4
GROUPS = BATCH // IMGS
T = IMGS * L
SHIFTS = 5
AREA = SHIFTS * CH * SIDE * SIDE
E, F = 8, 512
FC = F // 128
BANK = 512
PIECES = ((0, BANK), (BANK, T))
CHUNKS = [(c, min(c + 128, T)) for c in range(0, T, 128)]
NC = len(CHUNKS)
SHIFT_OF = (None, (4, -4), (4, 4), (-4, -4), (-4, 4))

UNIT = 32
UNITS = GROUPS * 2 * (D // UNIT)
BODY = 2 * UNIT
AHEAD = 4
RATE_LOG_CAP = 78.0
STEPS = 1 + 4 * (SHIFTS - 1)
HRING, PRING = 8, 4
YBASE = 6 * BANK
ABASE = (0, 2 * BANK)
UBASE = 4 * BANK


def keep_count():
    n = np.ones((SIDE, SIDE), np.float32)
    for dr, dc in SHIFT_OF[1:]:
        r, c = np.arange(SIDE) - dr, np.arange(SIDE) - dc
        n += ((r >= 0) & (r < SIDE))[:, None] & ((c >= 0) & (c < SIDE))[None, :]
    return n


PADDED = AREA - CH * int(keep_count().sum())


def build(nc, a, out):
    f32, bf16 = mybir.dt.float32, mybir.dt.bfloat16
    ALU, ACT = mybir.AluOpType, mybir.ActivationFunctionType
    X = mybir.AxisListType.X

    def dram(name, rows, cols, dt=f32):
        return nc.dram_tensor(name, [rows, cols], dt).ap()

    R2 = GROUPS * 2 * D
    delta_d = dram("delta_parts", 3 * R2, T, bf16)
    du_d = dram("du_parts", 3 * R2, T, bf16)
    B_d, C_d = dram("B_rows", R2, T), dram("C_rows", R2, T)
    uD_d, sz_d, y_d = dram("uD_rows", R2, T), dram("silu_z", R2, T), dram("y_rows", R2, T)
    zf_d = dram("branch_z", GROUPS * DM, T)
    hx_d = dram("residual", GROUPS * D, T)

    with ExitStack() as whole:
        psum = whole.enter_context(nc.psum_tensor("psum", [128, 8 * BANK], f32))
        slot = [psum[:, 2 * BANK * s:2 * BANK * s + T] for s in range(4)]
        A_all = whole.enter_context(nc.sbuf_tensor("A_all", [D, 2, D], f32))
        ones = whole.enter_context(nc.sbuf_tensor("ones", [128, 128], f32))
        eps_ln = whole.enter_context(nc.sbuf_tensor("eps_ln", [128, 1], f32))
        prepare(nc, a, locals())
        scan(nc, a, locals())
        experts(nc, a, locals(), out)


def imgs(ap):
    return ap.rearrange("p (b t) -> p b t", b=IMGS)


def prepare(nc, a, env):
    f32, bf16, ALU, ACT, X = (env[k] for k in ("f32", "bf16", "ALU", "ACT", "X"))
    psum, slot, ones, A_all, eps_ln = (env[k] for k in ("psum", "slot", "ones", "A_all", "eps_ln"))
    R2 = env["R2"]
    used = []
    with ExitStack() as ctx:
        def sb(name, shape, dt=f32):
            return ctx.enter_context(nc.sbuf_tensor(name, shape, dt))

        def sem(name):
            handle = nc.alloc_semaphore(name=name)
            used.append(handle)
            return handle

        gamma, beta = sb("gamma", [128, SHIFTS, L]), sb("beta", [128, SHIFTS, L])
        count = sb("count", [128, L])
        Wtok = sb("Wtok", [128, SHIFTS, D])
        mlpT, presT = sb("mlpT", [D, DM]), sb("presT", [D, DM])
        flT, inT = sb("flT", [DM, 2, D]), sb("inT", [DM, 2, 2 * D])
        xpT, dtT = sb("xpT", [D, 2, RANK + 2 * D]), sb("dtT", [RANK, 2, D])
        convw = sb("convw", [D, 2, KCONV])
        cols = sb("cols", [D, 7])
        cols64 = sb("cols64", [DM, 4])
        Alog = sb("Alog", [D, 2, D])
        G0, B0 = sb("G0", [D, L]), sb("B0", [D, L])

        img = sb("img", [128, T])
        xw, xc, sqw = sb("xw", [128, T]), sb("xc", [128, T]), sb("sqw", [128, T])
        s1, s2 = sb("s1", [128, IMGS]), sb("s2", [128, IMGS])
        negmean, m2, var, lnv, rstd = (sb(n, [128, IMGS]) for n in ("negmean", "m2", "var", "lnv", "rstd"))
        patches = sb("patches", [128, SHIFTS, T])
        tcen, h0 = sb("tcen", [D, T]), sb("h0", [D, T])
        hc, sq, lnr, rs, xln, hx, xn = (sb(n, [D, T]) for n in ("hc", "sq", "lnr", "rs", "xln", "hx", "xn"))
        ss, nrm, inv = (sb(n, [D, IMGS]) for n in ("ss", "nrm", "inv"))
        xup, zpre, zf = (sb(n, [DM, T]) for n in ("xup", "zpre", "zf"))
        xin = sb("xin", [DM, 2, T])
        upad = sb("upad", [D, 2, IMGS, L + KCONV - 1])
        sz, conv, u, uD = (sb(n, [D, 2, T]) for n in ("sz", "conv", "u", "uD"))
        dtl = sb("dtl", [RANK, 2, T])
        Bs, Cs, pre = (sb(n, [D, 2, T]) for n in ("Bs", "Cs", "pre"))
        mag, ex, w1, lg, rw, off, delta, du = (sb(n, [D, T]) for n in
                                               ("mag", "ex", "w1", "lg", "rw", "off", "delta", "du"))
        rem, rem2 = sb("rem", [D, T]), sb("rem2", [D, T])
        dparts, uparts = sb("dparts", [D, 2, 3, T], bf16), sb("uparts", [D, 2, 3, T], bf16)

        weights = sem("weights")
        consts = sem("consts")
        carrier, sp_carrier = sem("carrier"), sem("sp_carrier")
        A_exp, A_cut, folded, folded_ps = sem("A_exp"), sem("A_cut"), sem("folded"), sem("folded_ps")
        names = ("img_loaded xw_done sum1_done sum1_ps negmean_done xc_done xcw_done sqw_done sum2_done sum2_ps "
                 "m2_done var_done lnv_done rstd_done patch_steps token_ps tcen_done h0_done lnmean_ps "
                 "hc_done sq_done lnvar_ps lnr_done rs_done xln_done sq3_done ss_done nrm_done nrmc_done inv_done xn_done "
                 "hx_done hx_stored up_ps pres_ps xup_done zpre_done zf_done zf_stored").split()
        S = {n: sem(n) for n in names}
        both = ("fl_ps xin_done inu_ps inz_ps upad_done sz_done sz_stored conv_steps u_done uD_done uD_stored "
                "dt_ps B_ps dtl_done Bs_done B_stored C_ps Cs_done C_stored pre_ps pre_done mag_done ex_done w1_done "
                "lg_done rw_done off_done cor_done base_done delta_done du_done first_done dsplit d_stored usplit u_stored").split()
        S2 = [{n: sem(f"{n}_{d}") for n in both} for d in "fb"]

        block = ctx.enter_context(nc.Block())

        @block.sync
        def _(sp):
            for n in 'h0_done hx_done hx_stored patch_steps ss_done token_ps xc_done zf_done zf_stored'.split():
                sp.sem_inc(S[n], 1)
            for n in 'B_stored C_stored Cs_done base_done conv_steps cor_done d_stored du_done off_done pre_done sz_stored uD_done uD_stored u_done u_stored usplit'.split():
                for s in S2:
                    sp.sem_inc(s[n], 1)
            n = 0
            for dst, src in (
                (gamma[:], a["gamma"]), (beta[:], a["beta"]), (count[:], a["count"]), (Wtok[:], a["Wtok"]),
                (mlpT[:], a["mlpT"]), (presT[:], a["presT"]), (flT[:], a["flT"]), (inT[:], a["inT"]),
                (xpT[:], a["xpT"]), (dtT[:], a["dtT"]), (convw[:], a["convw"]), (cols[:], a["cols"]),
                (cols64[:], a["cols64"]), (Alog[:], a["Alog"]),
            ):
                sp.dma_start(dst, src).then_inc(weights, 16)
                n += 16
            assert n == 14 * 16
            with sp.Fori(0, GROUPS) as i:
                sp.wait_ge(S["patch_steps"], i * STEPS + 1)
                sp.sem_inc(sp_carrier, 1)
                sp.wait_ge(S["xc_done"], i + 1)
                sp.sem_inc(sp_carrier, 1)
                sp.dma_start(img[:], a["images"][:, bass.ds(i * T, T)]).then_inc(S["img_loaded"], 16)
                sp.wait_ge(S["hx_done"], i + 1 + 1)
                sp.sem_inc(sp_carrier, 1)
                sp.dma_start(env["hx_d"][bass.ds(i * D, D), :], hx[:]).then_inc(S["hx_stored"], 16)
                sp.wait_ge(S["zf_done"], i + 1 + 1)
                sp.sem_inc(sp_carrier, 1)
                sp.dma_start(env["zf_d"][bass.ds(i * DM, DM), :], zf[:]).then_inc(S["zf_stored"], 16)
                for d in range(2):
                    s = S2[d]
                    sp.wait_ge(s["uD_done"], i + 1 + 1)
                    sp.sem_inc(sp_carrier, 1)
                    sp.dma_start(env["uD_d"][bass.ds(i * (2 * D) + d * D, D), :], uD[:, d, :]).then_inc(s["uD_stored"], 16)
                for d in range(2):
                    s = S2[d]
                    sp.wait_ge(s["dsplit"], 5 * i + 5)
                    sp.sem_inc(sp_carrier, 1)
                    for q in range(3):
                        sp.dma_start(env["delta_d"][bass.ds(i * (2 * D) + (d * D + q * R2), D), :], dparts[:, d, q, :])\
                          .then_inc(s["d_stored"], 16)
                    sp.wait_ge(s["usplit"], 5 * i + 5 + 1)
                    sp.sem_inc(sp_carrier, 1)
                    for q in range(3):
                        sp.dma_start(env["du_d"][bass.ds(i * (2 * D) + (d * D + q * R2), D), :], uparts[:, d, q, :])\
                          .then_inc(s["u_stored"], 16)
            sp.wait_ge(S["hx_stored"], 16 * GROUPS + 1)
            sp.wait_ge(S["zf_stored"], 16 * GROUPS + 1)
            for d in range(2):
                for n in ("sz_stored", "uD_stored", "B_stored", "C_stored"):
                    sp.wait_ge(S2[d][n], 16 * GROUPS + 1)
                for n in ("d_stored", "u_stored"):
                    sp.wait_ge(S2[d][n], 48 * GROUPS + 1)

        @block.tensor
        def _(pe):
            def product(dst, lhsT, rhs, done, start=True, stop=True):
                for lo, hi in PIECES:
                    last = nc.tensor.matmul(dst[:, lo:hi], lhsT, rhs[:, lo:hi], start=start, stop=stop)
                if done is not None:
                    last.then_inc(done, 1)

            pe.wait_ge(weights, 14 * 16)
            pe.wait_ge(consts, 4)
            for n, src in enumerate((gamma, beta)):
                for s in range(SHIFTS):
                    last = nc.tensor.matmul(psum[:, n * BANK:n * BANK + L], Wtok[:, s, :], src[:, s, :],
                                            start=s == 0, stop=s == SHIFTS - 1)
            last.then_inc(folded_ps, 1)
            pe.wait_ge(folded, 2)
            with pe.Fori(0, GROUPS) as i:
                pe.wait_ge(S["sum1_done"], i + 1)
                for d in range(2):
                    pe.wait_ge(S2[d]["pre_done"], i + 1)
                    pe.wait_ge(S2[d]["Cs_done"], i + 1)
                nc.tensor.matmul(slot[3][:, 0:IMGS], ones[:], s1[:], start=True, stop=True).then_inc(S["sum1_ps"], 1)
                pe.wait_ge(S["patch_steps"], i * STEPS + STEPS + 1)
                for s in range(SHIFTS):
                    product(slot[0], Wtok[:, s, :], patches[:, s, :], S["token_ps"] if s == SHIFTS - 1 else None,
                            start=s == 0, stop=s == SHIFTS - 1)
                pe.wait_ge(S["sum2_done"], i + 1)
                nc.tensor.matmul(slot[3][:, 0:IMGS], ones[:], s2[:], start=True, stop=True).then_inc(S["sum2_ps"], 1)
                pe.wait_ge(S["h0_done"], i + 1 + 1)
                product(slot[1], ones[:], h0, S["lnmean_ps"])
                pe.wait_ge(S["sq_done"], i + 1)
                product(slot[2], ones[:], sq, S["lnvar_ps"])
                pe.wait_ge(S["xn_done"], i + 1)
                product(slot[0][0:DM], mlpT[:], xn, S["up_ps"])
                product(slot[1][0:DM], presT[:], xn, S["pres_ps"])
                pe.wait_ge(S["xup_done"], i + 1)
                pe.wait_ge(S["var_done"], i + 1)
                pe.wait_ge(S["lnr_done"], i + 1)
                product(slot[2], flT[:, 0, :], xup, S2[0]["fl_ps"])
                product(slot[3], flT[:, 1, :], xup, S2[1]["fl_ps"])
                pe.wait_ge(S["zpre_done"], i + 1)
                for d in range(2):
                    s, lo, hi = S2[d], slot[2 * d], slot[2 * d + 1]
                    pe.wait_ge(s["xin_done"], i + 1)
                    if d == 1:
                        pe.wait_ge(S2[0]["xin_done"], i + 1)
                    product(lo, inT[:, d, 0:D], xin[:, d, :], s["inu_ps"])
                    product(hi, inT[:, d, D:2 * D], xin[:, d, :], s["inz_ps"])
                for d in range(2):
                    s, lo, hi = S2[d], slot[2 * d], slot[2 * d + 1]
                    pe.wait_ge(s["u_done"], i + 1 + 1)
                    pe.wait_ge(s["sz_done"], i + 1)
                    product(lo[0:RANK], xpT[:, d, 0:RANK], u[:, d, :], s["dt_ps"])
                    product(hi, xpT[:, d, RANK:RANK + D], u[:, d, :], s["B_ps"])
                    pe.wait_ge(s["dtl_done"], i + 1)
                    product(lo, xpT[:, d, RANK + D:RANK + 2 * D], u[:, d, :], s["C_ps"])
                    pe.wait_ge(s["Bs_done"], i + 1)
                    product(hi, dtT[:, d, :], dtl[:, d, :], s["pre_ps"])

        @block.scalar
        def _(act):
            act.wait_ge(weights, 14 * 16)
            act.wait_ge(A_cut, 1)
            nc.scalar.activation(A_all[:], Alog[:], ACT.Exp).then_inc(A_exp, 1)
            with act.Fori(0, GROUPS) as i:
                act.wait_ge(S["var_done"], i + 1)
                act.activation(lnv[:], var[:], ACT.Ln).then_inc(S["lnv_done"], 1)
                act.wait_ge(S["lnv_done"], i + 1)
                act.wait_ge(S["h0_done"], i + 1)
                act.activation(rstd[:], lnv[:], ACT.Exp, scale=-0.5).then_inc(S["rstd_done"], 1)
                act.wait_ge(S["hc_done"], i + 1)
                act.wait_ge(S["ss_done"], i + 1)
                act.activation(sq[:], hc[:], ACT.Square).then_inc(S["sq_done"], 1)
                act.wait_ge(S["lnvar_ps"], i + 1)
                act.activation(lnr[:], slot[2], ACT.Ln, bias=eps_ln[:], scale=1.0 / D).then_inc(S["lnr_done"], 1)
                act.wait_ge(S["lnr_done"], i + 1)
                act.activation(rs[:], lnr[:], ACT.Exp, scale=-0.5).then_inc(S["rs_done"], 1)
                act.wait_ge(S["xln_done"], i + 1)
                act.activation(sq[:], xln[:], ACT.Square).then_inc(S["sq3_done"], 1)
                act.wait_ge(S["ss_done"], i + 1 + 1)
                act.activation(nrm[:], ss[:], ACT.Sqrt).then_inc(S["nrm_done"], 1)
                act.wait_ge(S["up_ps"], i + 1)
                act.activation(xup[:], slot[0][0:DM], ACT.Identity, bias=cols64[:, 0:1]).then_inc(S["xup_done"], 1)
                act.wait_ge(S["pres_ps"], i + 1)
                act.wait_ge(S["zf_done"], i + 1)
                act.activation(zpre[:], slot[1][0:DM], ACT.Identity, bias=cols64[:, 1:2]).then_inc(S["zpre_done"], 1)
                for d in range(2):
                    s = S2[d]
                    act.wait_ge(s["fl_ps"], i + 1)
                    dst = imgs(xin[:, d, :])
                    act.activation(dst[:, :, ::-1] if d else dst, imgs(slot[2 + d][0:DM]), ACT.Identity,
                                   bias=cols64[:, 2 + d:3 + d]).then_inc(s["xin_done"], 1)
                for d in range(2):
                    s = S2[d]
                    act.wait_ge(s["inu_ps"], i + 1)
                    act.wait_ge(s["conv_steps"], 4 * i + 1)
                    act.activation(upad[:, d, :, KCONV - 1:], imgs(slot[2 * d]), ACT.Copy).then_inc(s["upad_done"], 1)
                    act.wait_ge(s["inz_ps"], i + 1)
                    act.wait_ge(s["sz_stored"], 16 * i + 1)
                    act.activation(sz[:, d, :], slot[2 * d + 1], ACT.Silu).then_inc(s["sz_done"], 1)
                    act.wait_ge(s["sz_done"], i + 1)
                    act.dma_start(env["sz_d"][bass.ds(i * (2 * D) + d * D, D), :], sz[:, d, :]).then_inc(s["sz_stored"], 16)
                for d in range(2):
                    s = S2[d]
                    act.wait_ge(s["conv_steps"], 4 * i + 4 + 1)
                    act.wait_ge(s["uD_done"], i + 1)
                    act.wait_ge(s["du_done"], i + 1)
                    act.activation(u[:, d, :], conv[:, d, :], ACT.Silu).then_inc(s["u_done"], 1)
                for d in range(2):
                    s = S2[d]
                    act.wait_ge(s["dt_ps"], i + 1)
                    act.activation(dtl[:, d, :], slot[2 * d][0:RANK], ACT.Copy).then_inc(s["dtl_done"], 1)
                    act.wait_ge(s["B_ps"], i + 1)
                    act.wait_ge(s["B_stored"], 16 * i + 1)
                    act.activation(Bs[:, d, :], slot[2 * d + 1], ACT.Copy).then_inc(s["Bs_done"], 1)
                    act.wait_ge(s["Bs_done"], i + 1)
                    act.dma_start(env["B_d"][bass.ds(i * (2 * D) + d * D, D), :], Bs[:, d, :]).then_inc(s["B_stored"], 16)
                    act.wait_ge(s["C_ps"], i + 1)
                    act.wait_ge(s["C_stored"], 16 * i + 1)
                    act.activation(Cs[:, d, :], slot[2 * d], ACT.Copy).then_inc(s["Cs_done"], 1)
                    act.wait_ge(s["Cs_done"], i + 1 + 1)
                    act.dma_start(env["C_d"][bass.ds(i * (2 * D) + d * D, D), :], Cs[:, d, :]).then_inc(s["C_stored"], 16)
                    act.wait_ge(s["pre_ps"], i + 1)
                    act.wait_ge(s["base_done"], i + 1)
                    act.activation(pre[:, d, :], slot[2 * d + 1], ACT.Identity,
                                   bias=cols[:, 2 + 3 * d:3 + 3 * d]).then_inc(s["pre_done"], 1)
                for d in range(2):
                    s = S2[d]
                    act.wait_ge(s["mag_done"], i + 1)
                    act.wait_ge(S2[1 - d]["off_done"], i + d + 1)
                    act.activation(ex[:], mag[:], ACT.Exp, scale=-1.0).then_inc(s["ex_done"], 1)
                    act.wait_ge(s["w1_done"], i + 1)
                    act.wait_ge(S2[1 - d]["base_done"], i + d + 1)
                    act.activation(lg[:], w1[:], ACT.Ln).then_inc(s["lg_done"], 1)
                    act.wait_ge(s["lg_done"], i + 1)
                    act.wait_ge(S2[1 - d]["cor_done"], i + d + 1)
                    act.activation(rw[:], lg[:], ACT.Exp, scale=-1.0).then_inc(s["rw_done"], 1)

        @block.gpsimd
        def _(pool):
            pool.wait_ge(weights, 14 * 16)
            pool.memset(patches[:], 0.0).then_inc(consts, 1)
            pool.wait_ge(consts, 4)
            with pool.Fori(0, GROUPS) as i:
                pool.wait_ge(S["img_loaded"], 16 * i + 16)
                pool.wait_ge(S["token_ps"], i + 1)
                pool.tensor_tensor(imgs(patches[:, 0, :]), imgs(img[:]),
                                   gamma[:, 0:1, :].broadcast_to([128, IMGS, L]), ALU.mult).then_inc(S["patch_steps"], 1)
                step = 1
                for s in range(1, SHIFTS):
                    dr, dc = SHIFT_OF[s]
                    for qr in range(2):
                        for qc in range(2):
                            p = 64 * qr + 32 * qc
                            oi = (1 if qr == 0 else 0) if dr > 0 else (-1 if qr == 1 else 0)
                            oj = (1 if qc == 0 else 0) if dc > 0 else (-1 if qc == 1 else 0)
                            i0, i1 = max(0, -oi), min(GRID, GRID - oi)
                            j0, j1 = max(0, -oj), min(GRID, GRID - oj)
                            grid = lambda ap: ap.rearrange("p (b i j) -> p b i j", i=GRID, j=GRID)
                            dst = grid(patches[p:p + 32, s, :])[:, :, i0:i1, j0:j1]
                            src = grid(img[p:p + 32, :])[:, :, i0 + oi:i1 + oi, j0 + oj:j1 + oj]
                            gam = grid(gamma[p:p + 32, s, :])[:, :, i0:i1, j0:j1]
                            pool.wait_ge(S["patch_steps"], i * STEPS + step + 1)
                            pool.tensor_tensor(dst, src, gam.broadcast_to([32, IMGS, i1 - i0, j1 - j0]),
                                               ALU.mult).then_inc(S["patch_steps"], 1)
                            step += 1
                pool.wait_ge(S["xln_done"], i + 1)
                pool.wait_ge(S["hx_stored"], 16 * i + 1)
                pool.tensor_tensor(hx[:], h0[:], xln[:], ALU.add).then_inc(S["hx_done"], 1)
                for d in range(2):
                    s = S2[d]
                    pool.wait_ge(s["u_done"], i + 1 + 1)
                    pool.wait_ge(s["uD_stored"], 16 * i + 1)
                    pool.sem_inc(carrier, 1)
                    pool.tensor_scalar(uD[:, d, :], u[:, d, :], cols[:, 3 + 3 * d:4 + 3 * d], None,
                                       ALU.mult).then_inc(s["uD_done"], 1)
                for d in range(2):
                    s = S2[d]
                    pool.wait_ge(s["du_done"], i + 1 + 1)
                    pool.wait_ge(s["u_stored"], 48 * i + 1)
                    up = uparts[:, d]
                    pool.sem_inc(carrier, 1)
                    pool.tensor_scalar(up[:, 0, :], du[:], 1.0, None, ALU.mult).then_inc(s["usplit"], 1)
                    pool.wait_ge(s["usplit"], 5 * i + 1 + 1)
                    pool.tensor_tensor(rem2[:], du[:], up[:, 0, :], ALU.subtract).then_inc(s["usplit"], 1)
                    pool.wait_ge(s["usplit"], 5 * i + 2 + 1)
                    pool.sem_inc(carrier, 1)
                    pool.tensor_scalar(up[:, 1, :], rem2[:], 1.0, None, ALU.mult).then_inc(s["usplit"], 1)
                    pool.wait_ge(s["usplit"], 5 * i + 3 + 1)
                    pool.tensor_tensor(rem2[:], rem2[:], up[:, 1, :], ALU.subtract).then_inc(s["usplit"], 1)
                    pool.wait_ge(s["usplit"], 5 * i + 4 + 1)
                    pool.sem_inc(carrier, 1)
                    pool.tensor_scalar(up[:, 2, :], rem2[:], 1.0, None, ALU.mult).then_inc(s["usplit"], 1)

        @block.vector
        def _(dve):
            dve.memset(ones[:], 1.0).then_inc(consts, 1)
            dve.memset(eps_ln[:], 1e-5).then_inc(consts, 1)
            dve.memset(upad[:], 0.0).then_inc(consts, 1)
            dve.wait_ge(consts, 4)
            dve.wait_ge(weights, 14 * 16)
            dve.tensor_scalar(Alog[:], Alog[:], RATE_LOG_CAP, None, ALU.min).then_inc(A_cut, 1)
            dve.wait_ge(A_exp, 1)
            dve.tensor_scalar(A_all[:], A_all[:], -1.0, None, ALU.mult).then_inc(A_cut, 1)
            dve.wait_ge(folded_ps, 1)
            dve.tensor_copy(G0[:], psum[:, 0:L]).then_inc(folded, 1)
            dve.tensor_scalar(B0[:], psum[:, BANK:BANK + L], cols[:, 0:1], None, ALU.add).then_inc(folded, 1)
            dve.wait_ge(folded, 2)
            dve.wait_ge(A_cut, 2)
            cnt = count[:].unsqueeze(1).broadcast_to([128, IMGS, L])
            with dve.Fori(0, GROUPS) as i:
                dve.wait_ge(S["img_loaded"], 16 * i + 16)
                dve.tensor_tensor(imgs(xw[:]), imgs(img[:]), cnt, ALU.mult).then_inc(S["xw_done"], 1)
                dve.wait_ge(S["xw_done"], i + 1)
                dve.tensor_reduce(s1[:], imgs(xw[:]), X, ALU.add).then_inc(S["sum1_done"], 1)
                dve.wait_ge(S["sum1_ps"], i + 1)
                dve.tensor_scalar(negmean[:], slot[3][:, 0:IMGS], -1.0 / AREA, None, ALU.mult).then_inc(S["negmean_done"], 1)
                dve.wait_ge(S["negmean_done"], i + 1)
                dve.tensor_tensor(imgs(xc[:]), imgs(img[:]), negmean[:].unsqueeze(2).broadcast_to([128, IMGS, L]),
                                  ALU.add).then_inc(S["xc_done"], 1)
                dve.wait_ge(S["xc_done"], i + 1 + 1)
                dve.tensor_tensor(imgs(xw[:]), imgs(xc[:]), cnt, ALU.mult).then_inc(S["xcw_done"], 1)
                dve.wait_ge(S["xcw_done"], i + 1)
                dve.tensor_tensor(sqw[:], xw[:], xc[:], ALU.mult).then_inc(S["sqw_done"], 1)
                dve.wait_ge(S["sqw_done"], i + 1)
                dve.tensor_reduce(s2[:], imgs(sqw[:]), X, ALU.add).then_inc(S["sum2_done"], 1)
                pad = PADDED / AREA
                dve.scalar_tensor_tensor(m2[:], negmean[:], pad, negmean[:], ALU.mult, ALU.mult).then_inc(S["m2_done"], 1)
                dve.wait_ge(S["m2_done"], 2 * i + 1)
                dve.tensor_scalar(m2[:], m2[:], 1e-7, None, ALU.add).then_inc(S["m2_done"], 1)
                dve.wait_ge(S["m2_done"], 2 * i + 2)
                dve.wait_ge(S["sum2_ps"], i + 1)
                dve.scalar_tensor_tensor(var[:], slot[3][:, 0:IMGS], 1.0 / AREA, m2[:], ALU.mult, ALU.add)\
                   .then_inc(S["var_done"], 1)
                dve.wait_ge(S["token_ps"], i + 1 + 1)
                for b in range(IMGS):
                    part = slice(b * L, (b + 1) * L)
                    dve.scalar_tensor_tensor(tcen[:, part], G0[:], negmean[:, b:b + 1], slot[0][:, part],
                                             ALU.mult, ALU.add).then_inc(S["tcen_done"], 1)
                dve.wait_ge(S["rstd_done"], i + 1)
                dve.wait_ge(S["tcen_done"], IMGS * i + IMGS)
                dve.wait_ge(S["hx_done"], i + 1)
                for b in range(IMGS):
                    part = slice(b * L, (b + 1) * L)
                    last = dve.scalar_tensor_tensor(h0[:, part], tcen[:, part], rstd[:, b:b + 1], B0[:],
                                                    ALU.mult, ALU.add)
                last.then_inc(S["h0_done"], 1)
                dve.wait_ge(S["lnmean_ps"], i + 1)
                dve.wait_ge(S["h0_done"], i + 1 + 1)
                dve.scalar_tensor_tensor(hc[:], slot[1], -1.0 / D, h0[:], ALU.mult, ALU.add).then_inc(S["hc_done"], 1)
                dve.wait_ge(S["rs_done"], i + 1)
                dve.wait_ge(S["hc_done"], i + 1)
                dve.tensor_tensor(xln[:], hc[:], rs[:], ALU.mult).then_inc(S["xln_done"], 1)
                dve.wait_ge(S["sq3_done"], i + 1)
                dve.tensor_reduce(ss[:], imgs(sq[:]), X, ALU.add).then_inc(S["ss_done"], 1)
                dve.wait_ge(S["nrm_done"], i + 1)
                dve.tensor_scalar(inv[:], nrm[:], 1e-12, None, ALU.max).then_inc(S["nrmc_done"], 1)
                dve.wait_ge(S["nrmc_done"], i + 1)
                dve.reciprocal(inv[:], inv[:]).then_inc(S["inv_done"], 1)
                dve.wait_ge(S["inv_done"], i + 1)
                dve.wait_ge(S["xln_done"], i + 1)
                dve.tensor_tensor(imgs(xn[:]), imgs(xln[:]), inv[:].unsqueeze(2).broadcast_to([D, IMGS, L]),
                                  ALU.mult).then_inc(S["xn_done"], 1)
                dve.wait_ge(S["zpre_done"], i + 1)
                dve.wait_ge(S["zf_stored"], 16 * i + 1)
                dve.scalar_tensor_tensor(zf[:], zpre[:], 0.01, zpre[:], ALU.mult, ALU.max).then_inc(S["zf_done"], 1)
                for d in range(2):
                    s = S2[d]
                    dve.wait_ge(s["upad_done"], i + 1)
                    dve.wait_ge(s["u_done"], i + 1)
                    c = imgs(conv[:, d, :])
                    dve.tensor_scalar(c, upad[:, d, :, 0:L], convw[:, d, 0:1], cols[:, 1 + 3 * d:2 + 3 * d],
                                      ALU.mult, ALU.add).then_inc(s["conv_steps"], 1)
                    for k in range(1, KCONV):
                        dve.wait_ge(s["conv_steps"], 4 * i + k + 1)
                        dve.scalar_tensor_tensor(c, upad[:, d, :, k:k + L], convw[:, d, k:k + 1], c,
                                                 ALU.mult, ALU.add).then_inc(s["conv_steps"], 1)
                for d in range(2):
                    s = S2[d]
                    dve.wait_ge(s["pre_done"], i + 1 + 1)
                    dve.scalar_tensor_tensor(mag[:], pre[:, d, :], -1.0, pre[:, d, :], ALU.mult, ALU.max)\
                       .then_inc(s["mag_done"], 1)
                    dve.wait_ge(s["ex_done"], i + 1)
                    dve.tensor_scalar(w1[:], ex[:], 1.0, None, ALU.add).then_inc(s["w1_done"], 1)
                    dve.wait_ge(s["w1_done"], i + 1)
                    dve.scalar_tensor_tensor(off[:], w1[:], -1.0, ex[:], ALU.add, ALU.subtract).then_inc(s["off_done"], 1)
                    dve.wait_ge(s["rw_done"], i + 1)
                    dve.wait_ge(s["off_done"], i + 1 + 1)
                    dve.tensor_tensor(off[:], off[:], rw[:], ALU.mult).then_inc(s["cor_done"], 1)
                    dve.scalar_tensor_tensor(rem[:], pre[:, d, :], 0.0, lg[:], ALU.max, ALU.add).then_inc(s["base_done"], 1)
                    dve.wait_ge(s["cor_done"], i + 1 + 1)
                    dve.wait_ge(s["base_done"], i + 1 + 1)
                    dve.tensor_tensor(delta[:], rem[:], off[:], ALU.subtract).then_inc(s["delta_done"], 1)
                    dve.wait_ge(s["delta_done"], i + 1)
                    if d:
                        dve.wait_ge(S2[0]["usplit"], 5 * i + 5 + 1)
                    else:
                        dve.wait_ge(S2[1]["usplit"], 5 * i + 1)
                    dve.tensor_tensor(du[:], delta[:], u[:, d, :], ALU.mult).then_inc(s["du_done"], 1)
                    dve.wait_ge(s["du_done"], i + 1 + 1)
                    dve.memset(imgs(delta[:])[:, :, 0:1], 0.0).then_inc(s["first_done"], 1)
                    dve.wait_ge(s["first_done"], i + 1)
                    dve.wait_ge(s["d_stored"], 48 * i + 1)
                    dp = dparts[:, d]
                    dve.tensor_copy(dp[:, 0, :], delta[:]).then_inc(s["dsplit"], 1)
                    dve.wait_ge(s["dsplit"], 5 * i + 1)
                    dve.tensor_tensor(rem[:], delta[:], dp[:, 0, :], ALU.subtract).then_inc(s["dsplit"], 1)
                    dve.wait_ge(s["dsplit"], 5 * i + 2)
                    dve.tensor_copy(dp[:, 1, :], rem[:]).then_inc(s["dsplit"], 1)
                    dve.wait_ge(s["dsplit"], 5 * i + 3)
                    dve.tensor_tensor(rem[:], rem[:], dp[:, 1, :], ALU.subtract).then_inc(s["dsplit"], 1)
                    dve.wait_ge(s["dsplit"], 5 * i + 4)
                    dve.tensor_copy(dp[:, 2, :], rem[:]).then_inc(s["dsplit"], 1)

    nc.clear_and_free_semaphores(used)
    nc.all_engine_barrier()


def scan(nc, a, env):
    f32, bf16, ALU, ACT = (env[k] for k in ("f32", "bf16", "ALU", "ACT"))
    psum, A_all, R2 = env["psum"], env["A_all"], env["R2"]
    with ExitStack() as ctx:
        def sb(name, shape, dt=f32):
            return ctx.enter_context(nc.sbuf_tensor(name, shape, dt))

        def sem(name):
            return env["whole"].enter_context(nc.semaphore(name))

        spread32 = sb("spread32", [3 * UNIT, UNIT, 128])
        spread = sb("spread", [3 * UNIT, UNIT, 128], bf16)
        window = sb("window", [128, 2 * UNIT - 1])
        delta = sb("delta_in", [3 * UNIT, 2, T], bf16)
        du = sb("du_in", [3 * UNIT, 2, T], bf16)
        A = sb("A_in", [D, 2, UNIT])
        B, C = sb("B_in", [D, 2, T]), sb("C_in", [D, 2, T])
        H = sb("H", [D, HRING, T])
        P = sb("P", [D, PRING, T])
        ysb = sb("ysb", [UNIT, 2, T])

        sp_carrier = sem("sp_carrier2")
        spread_loaded, spread_cast, window_zero, window_done = (
            sem(n) for n in ("spread_loaded", "spread_cast", "window_zero", "window_done"))
        parts_loaded, A_loaded, B_loaded, C_loaded = (
            [sem(f"{n}_loaded{k}") for k in range(2)] for n in ("parts", "A", "B", "C"))
        decay_bcast = sem("decay_bcast")
        du_bcast = sem("du_bcast")
        decay_exp = sem("decay_exp")
        input_mult = sem("input_mult")
        out_mult = sem("out_mult")
        scanned = sem("scanned")
        reduced = sem("reduced")
        y_out = sem("y_out")
        y_stored = [sem(f"y_stored{k}") for k in range(2)]

        block = ctx.enter_context(nc.Block())

        @block.sync
        def _(sp):
            sp.dma_start(spread32[:], a["spread"]).then_inc(spread_loaded, 16)
            with sp.Fori(0, GROUPS) as g:
                for d in range(2):
                    with sp.Fori(0, 2) as h:
                        for k in range(2):
                            v = g * 8 + (h * 2 + (d * 4 + k))
                            free = g * (8 * UNIT) + (h * (2 * UNIT) + (d * 4 + k + 1) * UNIT)
                            sp.wait_ge(decay_bcast, free)
                            sp.sem_inc(sp_carrier, 1)
                            for q in range(3):
                                for src, dst in ((env["delta_d"], delta), (env["du_d"], du)):
                                    sp.dma_start(dst[q * UNIT:(q + 1) * UNIT, k, :],
                                                 src[bass.ds(v * UNIT + q * R2, UNIT), :]).then_inc(parts_loaded[k], 16)
                            sp.wait_ge(decay_exp, free)
                            sp.sem_inc(sp_carrier, 1)
                            sp.dma_start(A[:, k, :], A_all[:, d, bass.ds(h * (2 * UNIT) + k * UNIT, UNIT)])\
                              .then_inc(A_loaded[k], 16)
                            sp.wait_ge(input_mult, free)
                            sp.sem_inc(sp_carrier, 1)
                            sp.dma_start(B[:, k, :], env["B_d"][bass.ds(g * (2 * D) + d * D, D), :]).then_inc(B_loaded[k], 16)
                            sp.wait_ge(out_mult, free)
                            sp.sem_inc(sp_carrier, 1)
                            sp.dma_start(C[:, k, :], env["C_d"][bass.ds(g * (2 * D) + d * D, D), :]).then_inc(C_loaded[k], 16)

        @block.tensor
        def _(pe):
            nc.tensor.sem_inc(decay_bcast, BODY)
            nc.tensor.sem_inc(reduced, PRING)
            pe.wait_ge(spread_cast, 1)
            pe.wait_ge(window_done, 1)

            def spread_row(base, parts, j, done):
                for lo, hi in PIECES:
                    last = nc.tensor.matmul(psum[:, base + lo:base + hi], spread[:, j % UNIT, :],
                                            parts[:, j // UNIT % 2, lo:hi], start=True, stop=True)
                last.then_inc(done, 1)

            def spread_du(i, j):
                if j % UNIT == 0:
                    pe.wait_ge(parts_loaded[j // UNIT % 2], i * 96 + 96 * (j // BODY + 1))
                pe.wait_ge(input_mult, i * BODY + (j + BODY))
                spread_row(UBASE, du, j, du_bcast)

            def spread_delta(i, j):
                pe.wait_ge(scanned, i * BODY + (j + 1))
                spread_row(ABASE[j % 2], delta, j, decay_bcast)

            def reduce(i, j):
                c = j % UNIT
                pe.wait_ge(out_mult, i * BODY + (j + 1 + BODY))
                if c == 0:
                    pe.wait_ge(y_out, i * 2 + (j // UNIT + 1))
                for lo, hi in PIECES:
                    last = nc.tensor.matmul(psum[0:UNIT, YBASE + lo:YBASE + hi], window[:, UNIT - 1 - c:2 * UNIT - 1 - c],
                                            P[:, j % PRING, lo:hi], start=c == 0, stop=c == UNIT - 1)
                last.then_inc(reduced, 1)

            def body(i, ahead):
                for j in range(BODY):
                    if j + AHEAD < BODY or ahead:
                        spread_du(i, j + AHEAD)
                    reduce(i, j)
                    if j + AHEAD < BODY or ahead:
                        spread_delta(i, j + AHEAD)

            for j in range(AHEAD):
                spread_du(0, j)
                spread_delta(0, j)
            with pe.Fori(0, UNITS // 2 - 1) as i:
                body(i, True)
            body(UNITS // 2 - 1, False)

        @block.scalar
        def _(act):
            nc.scalar.sem_inc(decay_exp, BODY)
            nc.scalar.sem_inc(y_out, 1)
            for k in range(2):
                nc.scalar.sem_inc(y_stored[k], 16)
            act.wait_ge(spread_loaded, 16)
            act.activation(spread[:], spread32[:], ACT.Copy).then_inc(spread_cast, 1)

            def decay(n0, body0, j):
                c, k = j % UNIT, j // UNIT % 2
                if c == 0:
                    act.wait_ge(A_loaded[k], body0 * 16 + 16 * (j // BODY + 1))
                act.wait_ge(decay_bcast, n0 + (j + 1 + BODY))
                row = imgs(psum[:, ABASE[j % 2]:ABASE[j % 2] + T])[:, :, 1:]
                act.activation(row, row, ACT.Exp, scale=A[:, k, c:c + 1]).then_inc(decay_exp, 1)

            def body(i, ahead):
                n0 = i * BODY
                for j in range(BODY):
                    if j + AHEAD < BODY or ahead:
                        decay(n0, i, j + AHEAD)
                    if j % UNIT == UNIT - 1:
                        k = j // UNIT
                        act.wait_ge(reduced, n0 + (j + 1 + PRING))
                        act.wait_ge(y_stored[k], i * 16 + 16)
                        act.activation(ysb[:, k, :], psum[0:UNIT, YBASE:YBASE + T], ACT.Copy).then_inc(y_out, 1)
                        act.wait_ge(y_out, i * 2 + (k + 2))
                        act.dma_start(env["y_d"][bass.ds(i * BODY + k * UNIT, UNIT), :], ysb[:, k, :]).then_inc(y_stored[k], 16)

            for j in range(AHEAD):
                decay(0, 0, j)
            with act.Fori(0, UNITS // 2 - 1) as i:
                body(i, True)
            body(UNITS // 2 - 1, False)
            for k in range(2):
                act.wait_ge(y_stored[k], 16 * (UNITS // 2 + 1))

        @block.vector
        def _(dve):
            nc.vector.sem_inc(input_mult, BODY)
            nc.vector.sem_inc(scanned, 2)
            dve.memset(window[:], 0.0).then_inc(window_zero, 1)
            dve.wait_ge(window_zero, 1)
            dve.memset(window[:, UNIT - 1:UNIT], 1.0).then_inc(window_done, 1)

            def inputs(n0, body0, j):
                c, k = j % UNIT, j // UNIT % 2
                if c == 0:
                    dve.wait_ge(B_loaded[k], body0 * 16 + 16 * (j // BODY + 1))
                dve.wait_ge(du_bcast, n0 + (j + 1))
                dve.wait_ge(out_mult, n0 + (j + 1 + BODY - HRING))
                dve.tensor_tensor(H[:, j % HRING, :], psum[:, UBASE:UBASE + T], B[:, k, :],
                                  ALU.mult).then_inc(input_mult, 1)

            def body(i, ahead):
                n0 = i * BODY
                for j in range(BODY):
                    if j + 1 < BODY or ahead:
                        inputs(n0, i, j + 1)
                    dve.wait_ge(decay_exp, n0 + (j + 1 + BODY))
                    dve.wait_ge(input_mult, n0 + (j + 1 + BODY))
                    h = H[:, j % HRING, :]
                    dve.tensor_tensor_scan(h, psum[:, ABASE[j % 2]:ABASE[j % 2] + T], h, 0.0, ALU.mult, ALU.add)\
                       .then_inc(scanned, 1)

            inputs(0, 0, 0)
            with dve.Fori(0, UNITS // 2 - 1) as i:
                body(i, True)
            body(UNITS // 2 - 1, False)

        @block.gpsimd
        def _(pool):
            nc.gpsimd.sem_inc(out_mult, BODY)
            with pool.Fori(0, UNITS // 2) as i:
                n0 = i * BODY
                for j in range(BODY):
                    k = j // UNIT
                    if j % UNIT == 0:
                        pool.wait_ge(C_loaded[k], i * 16 + 16)
                    pool.wait_ge(scanned, n0 + (j + 3))
                    pool.wait_ge(reduced, n0 + (j + 1))
                    pool.tensor_tensor(P[:, j % PRING, :], H[:, j % HRING, :], C[:, k, :], ALU.mult)\
                        .then_inc(out_mult, 1)


def experts(nc, a, env, out):
    f32, ALU, ACT, X = (env[k] for k in ("f32", "ALU", "ACT", "X"))
    psum, slot, ones, eps_ln = (env[k] for k in ("psum", "slot", "ones", "eps_ln"))
    with ExitStack() as ctx:
        def sb(name, shape, dt=f32):
            return ctx.enter_context(nc.sbuf_tensor(name, shape, dt))

        def sem(name):
            return env["whole"].enter_context(nc.semaphore(name))

        outpT, outT = sb("outpT", [D, 2, DM]), sb("outT", [DM, D])
        Ws, bs = sb("Ws", [D, E]), sb("bs", [128, NC, E])
        W1, W2 = sb("W1", [D, E, F]), sb("W2", [128, E, FC, D])
        b1, b2, outb = sb("b1", [128, E, FC]), sb("b2", [D, E]), sb("outb", [D, 1])
        ident, rank = sb("ident", [128, 128]), sb("rank", [128, NC, E])
        pick = sb("pick", [E, E, 128])
        y, uD, sz = (sb(n, [D, 2, T]) for n in ("y_r", "uD_r", "sz_r"))
        zf, hx = sb("zf_r", [DM, T]), sb("hx_r", [D, T])
        gated, back, mix, fus = sb("gated", [D, 2, T]), sb("back", [DM, T]), sb("mix", [DM, T]), sb("fus", [DM, T])
        h1, hc, sq, lnr, rs, xt = (sb(n, [D, T]) for n in ("h1", "hc2", "sq2", "lnr2", "rs2", "xt"))
        lg, eq, gate = (sb(n, [128, NC, E]) for n in ("logits", "eq", "gate"))
        top, tot, pm = (sb(n, [128, NC]) for n in ("top", "tot", "pm"))
        gateT = sb("gateT", [E, T])
        gb = sb("gb", [128, E, T])
        hid = sb("hid", [128, 4, T])
        tmp, acc = sb("tmp", [D, 2, T]), sb("acc", [D, T])

        sp_carrier = sem("sp_carrier3")
        weights = sem("weights3")
        names = ("loaded yu_done gated_done outp_ps back_done mix_done fus_done mixed_ps h1_done mean_ps hc_done sq_done "
                 "var_ps lnr_done rs_done xt_done cleared logits_ps router first_done reduced_max gateexp_done gateT_ps gateT_done "
                 "gb_ps gb_done hid_ps hid_done y_ps tmp_done acc_done stored").split()
        S = {n: sem(n + "3") for n in names}
        block = ctx.enter_context(nc.Block())

        @block.sync
        def _(sp):
            for n in 'fus_done gated_done h1_done hid_done mix_done outp_ps stored tmp_done'.split():
                sp.sem_inc(S[n], 1)
            for dst, src in (
                (outpT[:], a["outpT"]), (outT[:], a["outT"]), (Ws[:], a["Ws"]), (W1[:], a["W1"]), (W2[:], a["W2"]),
                (b1[:], a["b1"]), (b2[:], a["b2"]), (outb[:], a["outb"]), (ident[:], a["ident"]),
                (rank[:], a["rank"]), (pick[:], a["pick"]),
            ):
                sp.dma_start(dst, src).then_inc(weights, 16)
            for c in range(NC):
                sp.dma_start(bs[:, c, :], a["bs"].broadcast_to([128, E])).then_inc(weights, 16)
            with sp.Fori(0, GROUPS) as i:
                sp.wait_ge(S["gated_done"], i + 1)
                sp.sem_inc(sp_carrier, 1)
                sp.wait_ge(S["fus_done"], i + 1)
                sp.sem_inc(sp_carrier, 1)
                sp.wait_ge(S["h1_done"], i + 1)
                sp.sem_inc(sp_carrier, 1)
                for d in range(2):
                    for dst, src in ((y, env["y_d"]), (uD, env["uD_d"]), (sz, env["sz_d"])):
                        sp.dma_start(dst[:, d, :], src[bass.ds(i * (2 * D) + d * D, D), :]).then_inc(S["loaded"], 16)
                sp.dma_start(zf[:], env["zf_d"][bass.ds(i * DM, DM), :]).then_inc(S["loaded"], 16)
                sp.dma_start(hx[:], env["hx_d"][bass.ds(i * D, D), :]).then_inc(S["loaded"], 16)
                sp.wait_ge(S["acc_done"], E * i + E)
                sp.sem_inc(sp_carrier, 1)
                sp.dma_start(out[:, bass.ds(i * T, T)], acc[:]).then_inc(S["stored"], 16)
            sp.wait_ge(S["stored"], 16 * GROUPS + 1)

        LOADED = 16 * 8
        WEIGHTS = 16 * (11 + NC)

        @block.gpsimd
        def _(pool):
            with pool.Fori(0, GROUPS) as i:
                pool.wait_ge(S["loaded"], LOADED * i + LOADED)
                pool.wait_ge(S["outp_ps"], i + 1)
                pool.tensor_tensor(gated[:], y[:], uD[:], ALU.add).then_inc(S["yu_done"], 1)
                pool.wait_ge(S["yu_done"], i + 1)
                pool.tensor_tensor(gated[:], gated[:], sz[:], ALU.mult).then_inc(S["gated_done"], 1)

        @block.tensor
        def _(pe):
            def product(dst, lhsT, rhs, done, start=True, stop=True):
                for lo, hi in PIECES:
                    last = nc.tensor.matmul(dst[:, lo:hi], lhsT, rhs[:, lo:hi], start=start, stop=stop)
                if done is not None:
                    last.then_inc(done, 1)

            pe.wait_ge(weights, WEIGHTS)
            pe.wait_ge(S["cleared"], 1)
            with pe.Fori(0, GROUPS) as i:
                pe.wait_ge(S["gated_done"], i + 1 + 1)
                pe.wait_ge(S["hid_done"], 32 * i + 1)
                pe.wait_ge(S["tmp_done"], E * i + 1)
                product(slot[0][0:DM], outpT[:, 0, :], gated[:, 0, :], None)
                product(slot[1][0:DM], outpT[:, 1, :], gated[:, 1, :], S["outp_ps"])
                pe.wait_ge(S["fus_done"], i + 1 + 1)
                product(slot[2], outT[:], fus, S["mixed_ps"])
                pe.wait_ge(S["h1_done"], i + 1 + 1)
                product(slot[3], ones[:], h1, S["mean_ps"])
                pe.wait_ge(S["sq_done"], i + 1)
                product(slot[0], ones[:], sq, S["var_ps"])
                pe.wait_ge(S["xt_done"], i + 1)
                for c, (lo, hi) in enumerate(CHUNKS):
                    last = nc.tensor.matmul(slot[1][0:hi - lo, c * E:(c + 1) * E], xt[:, lo:hi], Ws[:], start=True, stop=True)
                last.then_inc(S["logits_ps"], 1)
                pe.wait_ge(S["router"], 9 * i + 9)
                for c, (lo, hi) in enumerate(CHUNKS):
                    last = nc.tensor.transpose(slot[2][0:E, lo:hi], gate[0:hi - lo, c, :], ident[0:hi - lo, 0:hi - lo])
                last.then_inc(S["gateT_ps"], 1)
                pe.wait_ge(S["gateT_done"], i + 1)
                for e in range(E):
                    if e >= 2:
                        pe.wait_ge(S["gb_done"], i * E + (e - 1))
                    product(slot[e % 2], pick[:, e, :], gateT, S["gb_ps"])

                def down(n):
                    e, f = divmod(n, FC)
                    pe.wait_ge(S["hid_done"], i * 32 + (n + 1) + 1)
                    if f == 0 and e >= 2:
                        pe.wait_ge(S["tmp_done"], i * E + (e - 1) + 1)
                    product(slot[2 + e % 2], W2[:, e, f, :], hid[:, n % 4, :], S["y_ps"], start=f == 0, stop=f == FC - 1)

                for n in range(E * FC):
                    e, f = divmod(n, FC)
                    if n < 2:
                        pe.wait_ge(S["gb_done"], i * E + (E - 1 + n))
                    else:
                        pe.wait_ge(S["hid_done"], i * 32 + (n - 1) + 1)
                    product(slot[n % 2], W1[:, e, f * 128:(f + 1) * 128], xt, S["hid_ps"])
                    if n >= 1:
                        down(n - 1)
                down(E * FC - 1)

        @block.scalar
        def _(act):
            act.wait_ge(weights, WEIGHTS)
            with act.Fori(0, GROUPS) as i:
                act.wait_ge(S["outp_ps"], i + 1 + 1)
                act.wait_ge(S["mix_done"], i + 1)
                act.activation(imgs(back[:])[:, :, ::-1], imgs(slot[1][0:DM]), ACT.Copy).then_inc(S["back_done"], 1)
                act.wait_ge(S["hc_done"], i + 1)
                act.activation(sq[:], hc[:], ACT.Square).then_inc(S["sq_done"], 1)
                act.wait_ge(S["var_ps"], i + 1)
                act.activation(lnr[:], slot[0], ACT.Ln, bias=eps_ln[:], scale=1.0 / D).then_inc(S["lnr_done"], 1)
                act.wait_ge(S["lnr_done"], i + 1)
                act.activation(rs[:], lnr[:], ACT.Exp, scale=-0.5).then_inc(S["rs_done"], 1)
                act.wait_ge(S["router"], 9 * i + 2)
                act.activation(lg[:], lg[:], ACT.Exp).then_inc(S["gateexp_done"], 1)
                act.wait_ge(S["gateT_ps"], i + 1)
                act.activation(gateT[:], slot[2][0:E], ACT.Copy).then_inc(S["gateT_done"], 1)
                act.wait_ge(S["tmp_done"], E * i + 1)
                for e in range(E):
                    act.wait_ge(S["gb_ps"], i * E + (e + 1))
                    act.activation(gb[:, e, :], slot[e % 2], ACT.Copy).then_inc(S["gb_done"], 1)
                for n in range(E * FC):
                    e, f = divmod(n, FC)
                    act.wait_ge(S["hid_ps"], i * 32 + (n + 1))
                    if n >= 4:
                        act.wait_ge(S["y_ps"], i * 32 + (n - 3))
                    act.activation(hid[:, n % 4, :], slot[n % 2], ACT.Gelu, bias=b1[:, e, f:f + 1]).then_inc(S["hid_done"], 1)

        @block.vector
        def _(dve):
            dve.memset(slot[1][:, 0:NC * E], 0.0).then_inc(S["cleared"], 1)
            dve.wait_ge(weights, WEIGHTS)
            with dve.Fori(0, GROUPS) as i:
                dve.wait_ge(S["back_done"], i + 1)
                dve.tensor_tensor(mix[:], slot[0][0:DM], back[:], ALU.add).then_inc(S["mix_done"], 1)
                dve.wait_ge(S["mix_done"], i + 1 + 1)
                dve.wait_ge(S["loaded"], LOADED * i + LOADED)
                dve.tensor_tensor(fus[:], mix[:], zf[:], ALU.mult).then_inc(S["fus_done"], 1)
                dve.wait_ge(S["mixed_ps"], i + 1)
                dve.scalar_tensor_tensor(h1[:], slot[2], outb[:], hx[:], ALU.add, ALU.add).then_inc(S["h1_done"], 1)
                dve.wait_ge(S["mean_ps"], i + 1)
                dve.wait_ge(S["h1_done"], i + 1 + 1)
                dve.scalar_tensor_tensor(hc[:], slot[3], -1.0 / D, h1[:], ALU.mult, ALU.add).then_inc(S["hc_done"], 1)
                dve.wait_ge(S["rs_done"], i + 1)
                dve.wait_ge(S["hc_done"], i + 1)
                dve.tensor_tensor(xt[:], hc[:], rs[:], ALU.mult).then_inc(S["xt_done"], 1)
                r = S["router"]
                dve.wait_ge(S["logits_ps"], i + 1)
                dve.tensor_tensor(lg[:].rearrange("p c e -> p (c e)"), slot[1][:, 0:NC * E],
                                  bs[:].rearrange("p c e -> p (c e)"), ALU.add).then_inc(r, 1)
                dve.wait_ge(r, 9 * i + 1)
                dve.tensor_reduce(top[:], lg[:], X, ALU.max).then_inc(S["reduced_max"], 1)
                dve.wait_ge(S["reduced_max"], 2 * i + 1)
                spread_of = lambda v: v[:].unsqueeze(2).broadcast_to([128, NC, E])
                dve.tensor_tensor(lg[:], lg[:], spread_of(top), ALU.subtract).then_inc(r, 1)
                dve.wait_ge(S["gateexp_done"], i + 1)
                dve.tensor_reduce(tot[:], lg[:], X, ALU.add).then_inc(r, 1)
                dve.wait_ge(r, 9 * i + 3)
                dve.reciprocal(tot[:], tot[:]).then_inc(r, 1)
                dve.wait_ge(r, 9 * i + 4)
                dve.tensor_tensor(lg[:], lg[:], spread_of(tot), ALU.mult).then_inc(r, 1)
                dve.wait_ge(r, 9 * i + 5)
                dve.tensor_reduce(pm[:], lg[:], X, ALU.max).then_inc(r, 1)
                dve.wait_ge(r, 9 * i + 6)
                dve.tensor_tensor(eq[:], lg[:], spread_of(pm), ALU.is_equal).then_inc(r, 1)
                dve.wait_ge(r, 9 * i + 7)
                dve.tensor_tensor(eq[:], eq[:], rank[:], ALU.mult).then_inc(r, 1)
                dve.wait_ge(r, 9 * i + 8)
                dve.tensor_reduce(top[:], eq[:], X, ALU.max).then_inc(S["reduced_max"], 1)
                dve.wait_ge(S["reduced_max"], 2 * i + 2)
                dve.tensor_tensor(eq[:], eq[:], spread_of(top), ALU.is_equal).then_inc(S["first_done"], 1)
                dve.wait_ge(S["first_done"], i + 1)
                dve.tensor_tensor(gate[:], eq[:], spread_of(pm), ALU.mult).then_inc(r, 1)
                for e in range(E):
                    dve.wait_ge(S["y_ps"], i * 32 + (4 * e + 4))
                    dve.wait_ge(S["gb_done"], i * E + E)
                    dve.scalar_tensor_tensor(tmp[:, e % 2, :], slot[2 + e % 2], b2[:, e:e + 1], gb[:, e, :],
                                             ALU.add, ALU.mult).then_inc(S["tmp_done"], 1)
                    dve.wait_ge(S["tmp_done"], i * E + (e + 1) + 1)
                    if e == 0:
                        dve.wait_ge(S["stored"], 16 * i + 1)
                        dve.tensor_tensor(acc[:], h1[:], tmp[:, 0, :], ALU.add).then_inc(S["acc_done"], 1)
                    else:
                        dve.wait_ge(S["acc_done"], i * E + e)
                        dve.tensor_tensor(acc[:], acc[:], tmp[:, e % 2, :], ALU.add).then_inc(S["acc_done"], 1)


def patch_rows(x):
    n = x.shape[0]
    x = x.reshape(n, CH, GRID, 2, HALF, GRID, 2, HALF)
    return x.transpose(3, 6, 1, 4, 7, 0, 2, 5).reshape(128, n, L)


def swap_halves(rows):
    return rows.reshape((2, 2, 32) + rows.shape[1:])[::-1, ::-1].reshape(rows.shape)


def layout(v):
    def shifts_first(t):
        rows = patch_rows(t.reshape(SHIFTS, CH, SIDE, SIDE))
        return np.concatenate([rows[:, :1], swap_halves(rows[:, 1:])], axis=1)

    W = v["L0_tok_W"].reshape(D, SHIFTS, CH, 2, HALF, 2, HALF).transpose(3, 5, 2, 4, 6, 1, 0).reshape(128, SHIFTS, D)
    W = np.concatenate([W[:, :1], swap_halves(W[:, 1:])], axis=1)
    at = lambda n: v["L0_attn_" + n]
    both = lambda n: np.stack([at("f_" + n), at("b_" + n)])
    ffn = lambda n: v["L0_ffn_" + n]
    spread = np.tile(np.eye(UNIT, dtype=np.float32), (3, 1))[:, :, None] * np.ones((1, 1, 128), np.float32)
    pick = np.eye(E, dtype=np.float32)[:, :, None] * np.ones((1, 1, 128), np.float32)
    arrays = {
        "images": patch_rows(v["x"]).reshape(128, BATCH * L),
        "gamma": shifts_first(v["L0_tok_gamma"]), "beta": shifts_first(v["L0_tok_beta"]),
        "count": patch_rows(np.broadcast_to(keep_count(), (1, CH, SIDE, SIDE)))[:, 0],
        "Wtok": W, "mlpT": at("mlp_w").T, "presT": at("mlpres_w").T,
        "flT": np.pad(np.stack([at("fl_w").T, at("bl_w").T], axis=1), ((0, 0), (0, 0), (0, D - DM))),
        "inT": both("in_w").transpose(2, 0, 1), "xpT": both("xproj_w").transpose(2, 0, 1),
        "dtT": both("dt_w").transpose(2, 0, 1), "convw": both("conv_w").transpose(1, 0, 2),
        "cols": np.stack([v["L0_tok_b"], at("f_conv_b"), at("f_dt_b"), at("f_D"),
                          at("b_conv_b"), at("b_dt_b"), at("b_D")], axis=1),
        "cols64": np.stack([at("mlp_b"), at("mlpres_b"), at("fl_b"), at("bl_b")], axis=1),
        "Alog": both("Alog").transpose(2, 0, 1),
        "spread": spread,
        "outpT": both("outp_w").transpose(2, 0, 1), "outT": at("out_w").T, "outb": at("out_b")[:, None],
        "Ws": ffn("Ws"), "bs": ffn("bs")[None], "W1": ffn("W1").transpose(1, 0, 2),
        "W2": ffn("W2").reshape(E, FC, 128, D).transpose(2, 0, 1, 3),
        "b1": ffn("b1").reshape(E, FC, 128).transpose(2, 0, 1), "b2": ffn("b2").T,
        "ident": np.eye(128, dtype=np.float32),
        "rank": np.broadcast_to(np.arange(E, 0, -1, dtype=np.float32), (128, NC, E)),
        "pick": pick,
    }
    return {n: np.ascontiguousarray(x) for n, x in arrays.items()}


def kernel(**inputs):
    import concourse.bacc as bacc
    from concourse.bass_utils import run_bass_kernel_spmd

    nc = bacc.Bacc("TRN2", target_bir_lowering=False, num_devices=1)
    arrays = layout({n: np.asarray(x) for n, x in inputs.items()})
    args = {n: nc.dram_tensor(n + "_in", x.shape, mybir.dt.from_np(x.dtype), kind="ExternalInput").ap()
            for n, x in arrays.items()}
    out = nc.dram_tensor("out", (D, BATCH * L), mybir.dt.float32, kind="ExternalOutput").ap()
    build(nc, args, out)
    r = run_bass_kernel_spmd(nc, [{n + "_in": x for n, x in arrays.items()}], core_ids=[0])
    return np.ascontiguousarray(r.results[0]["out"].reshape(D, BATCH, L).transpose(1, 2, 0))
```

```python
from contextlib import ExitStack

import numpy as np

import concourse.bass as bass
from concourse import mybir

BATCH, CH, SIDE, PATCH, HALF = 128, 2, 104, 8, 4
GRID = SIDE // PATCH
L = GRID * GRID
D = 128
DM = 64
RANK = 16
KCONV = 4
IMGS = 4
GROUPS = BATCH // IMGS
T = IMGS * L
SHIFTS = 5
AREA = SHIFTS * CH * SIDE * SIDE
E, F = 8, 512
FC = F // 128
BANK = 512
PIECES = ((0, BANK), (BANK, T))
CHUNKS = [(c, min(c + 128, T)) for c in range(0, T, 128)]
NC = len(CHUNKS)
SHIFT_OF = (None, (4, -4), (4, 4), (-4, -4), (-4, 4))

UNIT = 32
UNITS = GROUPS * 2 * (D // UNIT)
BODY = 2 * UNIT
AHEAD = 4
RATE_LOG_CAP = 78.0
STEPS = 1 + 4 * (SHIFTS - 1)
CENTRE, DELTA, SPLIT = 7, 4, 5
HRING, PRING = 8, 4
YBASE = 6 * BANK
ABASE = (0, 2 * BANK)
UBASE = 4 * BANK


def keep_count():
    n = np.ones((SIDE, SIDE), np.float32)
    for dr, dc in SHIFT_OF[1:]:
        r, c = np.arange(SIDE) - dr, np.arange(SIDE) - dc
        n += ((r >= 0) & (r < SIDE))[:, None] & ((c >= 0) & (c < SIDE))[None, :]
    return n


PADDED = AREA - CH * int(keep_count().sum())


def build(nc, a, out):
    f32, bf16 = mybir.dt.float32, mybir.dt.bfloat16
    ALU, ACT = mybir.AluOpType, mybir.ActivationFunctionType
    X = mybir.AxisListType.X

    def dram(name, rows, cols, dt=f32):
        return nc.dram_tensor(name, [rows, cols], dt).ap()

    R2 = GROUPS * 2 * D
    delta_d = dram("delta_parts", 3 * R2, T, bf16)
    du_d = dram("du_parts", 3 * R2, T, bf16)
    B_d, C_d = dram("B_rows", R2, T), dram("C_rows", R2, T)
    uD_d, sz_d, y_d = dram("uD_rows", R2, T), dram("silu_z", R2, T), dram("y_rows", R2, T)
    zf_d = dram("branch_z", GROUPS * DM, T)
    hx_d = dram("residual", GROUPS * D, T)

    with ExitStack() as whole:
        psum = whole.enter_context(nc.psum_tensor("psum", [128, 8 * BANK], f32))
        slot = [psum[:, 2 * BANK * s:2 * BANK * s + T] for s in range(4)]
        A_all = whole.enter_context(nc.sbuf_tensor("A_all", [D, 2, D], f32))
        ones = whole.enter_context(nc.sbuf_tensor("ones", [128, 128], f32))
        eps_ln = whole.enter_context(nc.sbuf_tensor("eps_ln", [128, 1], f32))
        prepare(nc, a, locals())
        scan(nc, a, locals())
        experts(nc, a, locals(), out)


def imgs(ap):
    return ap.rearrange("p (b t) -> p b t", b=IMGS)


def now(g, per=1, k=None):
    return g * per + ((per if k is None else k) + 1)


def before(g, per=1):
    return g * per + 1


def prepare(nc, a, env):
    f32, bf16, ALU, ACT, X = (env[k] for k in ("f32", "bf16", "ALU", "ACT", "X"))
    psum, slot, ones, A_all, eps_ln = (env[k] for k in ("psum", "slot", "ones", "A_all", "eps_ln"))
    R2 = env["R2"]
    used = []
    with ExitStack() as ctx:
        def sb(name, shape, dt=f32):
            return ctx.enter_context(nc.sbuf_tensor(name, shape, dt))

        def sem(name):
            handle = nc.alloc_semaphore(name=name)
            used.append(handle)
            return handle

        gamma = sb("gamma", [128, SHIFTS, L])
        count = sb("count", [128, L])
        Wtok = sb("Wtok", [128, SHIFTS, D])
        mlpT, presT = sb("mlpT", [D, DM]), sb("presT", [D, DM])
        flT, inT = sb("flT", [DM, 2, D]), sb("inT", [DM, 2, 2 * D])
        xpT, dtT = sb("xpT", [D, 2, RANK + 2 * D]), sb("dtT", [RANK, 2, D])
        convw = sb("convw", [D, 2, KCONV])
        cols = sb("cols", [D, 7])
        cols64 = sb("cols64", [DM, 4])
        G0, B0 = sb("G0", [D, L]), sb("B0", [D, L])

        img = sb("img", [128, T])
        xw, xc = sb("xw", [128, T]), sb("xc", [128, T])
        s1, s2 = sb("s1", [128, IMGS]), sb("s2", [128, IMGS])
        negmean, m2, var, lnv, rstd = (sb(n, [128, IMGS]) for n in ("negmean", "m2", "var", "lnv", "rstd"))
        patches = sb("patches", [128, SHIFTS, T])
        h0, hc, sq, rs, xln, hx, xn = (sb(n, [D, T]) for n in ("h0", "hc", "sq", "rs", "xln", "hx", "xn"))
        ss, nrm, inv = (sb(n, [D, IMGS]) for n in ("ss", "nrm", "inv"))
        xup, zpre, zf = (sb(n, [DM, T]) for n in ("xup", "zpre", "zf"))
        xin = sb("xin", [DM, 2, T])
        upad = sb("upad", [D, 2, IMGS, L + KCONV - 1])
        sz, conv, u, uD = (sb(n, [D, 2, T]) for n in ("sz", "conv", "u", "uD"))
        dtl = sb("dtl", [RANK, 2, T])
        Bs, Cs, pre = (sb(n, [D, 2, T]) for n in ("Bs", "Cs", "pre"))
        ex, w1, lg, rw, off, base = (sb(n, [D, 2, T]) for n in ("ex", "w1", "lg", "rw", "off", "base"))
        delta, du = conv, w1
        dparts, uparts = sb("dparts", [D, 2, 3, T], bf16), sb("uparts", [D, 2, 3, T], bf16)
        beta = patches
        Alog = Cs[:, 0, 0:2 * D].rearrange("p (d c) -> p d c", d=2)

        weights, consts = sem("weights"), sem("consts")
        carrier, sp_carrier = sem("carrier"), sem("sp_carrier")
        A_exp, A_cut, folded, folded_ps = sem("A_exp"), sem("A_cut"), sem("folded"), sem("folded_ps")
        S = {n: sem(n) for n in (
            "img_loaded sum1 sum1_ps centre sum2_ps var_done lnv_done rstd_done patch_steps token_ps token h0_done "
            "lnmean_ps hc_done sq_done lnvar_ps rs_done xln_done sq3_done ss_done nrm_done inv_done xn_done "
            "hx_done hx_stored up_ps pres_ps xup_done zpre_done zf_done zf_stored").split()}
        S2 = [{n: sem(f"{n}_{d}") for n in (
            "fl_ps xin_done inu_ps inz_ps upad_done sz_done sz_stored conv_steps u_done uD_done uD_stored "
            "dt_ps B_ps dtl_done Bs_done B_stored C_ps Cs_done C_stored pre_ps pre_done mag_done ex_done w1_done "
            "lg_done rw_done off_done delta_steps du_done dsplit d_stored usplit u_stored").split()} for d in "fb"]
        WEIGHTS = 14 * 16

        block = ctx.enter_context(nc.Block())

        @block.sync
        def _(sp):
            for dst, src in (
                (gamma[:], a["gamma"]), (beta[:, :, 0:L], a["beta"]), (count[:], a["count"]), (Wtok[:], a["Wtok"]),
                (mlpT[:], a["mlpT"]), (presT[:], a["presT"]), (flT[:], a["flT"]), (inT[:], a["inT"]),
                (xpT[:], a["xpT"]), (dtT[:], a["dtT"]), (convw[:], a["convw"]), (cols[:], a["cols"]),
                (cols64[:], a["cols64"]), (Alog, a["Alog"]),
            ):
                sp.dma_start(dst, src).then_inc(weights, 16)
            for s in (*S.values(), *S2[0].values(), *S2[1].values()):
                sp.sem_inc(s, 1)

            def load(g):
                sp.wait_ge(S["patch_steps"], before(g, STEPS))
                sp.wait_ge(S["centre"], before(g, CENTRE))
                sp.sem_inc(sp_carrier, 1)
                sp.dma_start(img[:], a["images"][:, bass.ds(g * T, T)]).then_inc(S["img_loaded"], 16)

            def store_front(g):
                sp.wait_ge(S["hx_done"], now(g))
                sp.sem_inc(sp_carrier, 1)
                sp.dma_start(env["hx_d"][bass.ds(g * D, D), :], hx[:]).then_inc(S["hx_stored"], 16)
                sp.wait_ge(S["zf_done"], now(g))
                sp.sem_inc(sp_carrier, 1)
                sp.dma_start(env["zf_d"][bass.ds(g * DM, DM), :], zf[:]).then_inc(S["zf_stored"], 16)

            def store_back(g):
                for d in range(2):
                    s = S2[d]
                    sp.wait_ge(s["uD_done"], now(g))
                    sp.sem_inc(sp_carrier, 1)
                    sp.dma_start(env["uD_d"][bass.ds(g * (2 * D) + d * D, D), :], uD[:, d, :]).then_inc(s["uD_stored"], 16)
                for done, stored, dst, src in (("dsplit", "d_stored", env["delta_d"], dparts),
                                               ("usplit", "u_stored", env["du_d"], uparts)):
                    for d in range(2):
                        sp.wait_ge(S2[d][done], now(g, SPLIT))
                        sp.sem_inc(sp_carrier, 1)
                        for q in range(3):
                            sp.dma_start(dst[bass.ds(g * (2 * D) + (d * D + q * R2), D), :], src[:, d, q, :])\
                              .then_inc(S2[d][stored], 16)

            sp.wait_ge(folded, 3)
            load(0)
            load(1)
            store_front(0)
            with sp.Fori(0, GROUPS - 2) as g:
                load(g + 2)
                store_back(g)
                store_front(g + 1)
            store_back(GROUPS - 2)
            store_front(GROUPS - 1)
            store_back(GROUPS - 1)
            for n in ("hx_stored", "zf_stored"):
                sp.wait_ge(S[n], before(GROUPS, 16))
            for d in range(2):
                for n in ("sz_stored", "uD_stored", "B_stored", "C_stored"):
                    sp.wait_ge(S2[d][n], before(GROUPS, 16))
                for n in ("d_stored", "u_stored"):
                    sp.wait_ge(S2[d][n], before(GROUPS, 48))

        @block.tensor
        def _(pe):
            def product(dst, lhsT, rhs, done, start=True, stop=True):
                for lo, hi in PIECES:
                    last = nc.tensor.matmul(dst[:, lo:hi], lhsT, rhs[:, lo:hi], start=start, stop=stop)
                if done is not None:
                    last.then_inc(done, 1)

            def first_sums(g):
                pe.wait_ge(S2[0]["xin_done"], before(g))
                pe.wait_ge(S["sum1"], now(g, 2))
                nc.tensor.matmul(slot[3][:, 0:IMGS], ones[:], s1[:], start=True, stop=True).then_inc(S["sum1_ps"], 1)

            def second_sums(g):
                pe.wait_ge(S["centre"], now(g, CENTRE))
                nc.tensor.matmul(slot[3][:, 0:IMGS], ones[:], s2[:], start=True, stop=True).then_inc(S["sum2_ps"], 1)

            def tokens(g):
                pe.wait_ge(S2[1]["xin_done"], before(g))
                pe.wait_ge(S["patch_steps"], now(g, STEPS))
                for s in range(SHIFTS):
                    product(slot[2], Wtok[:, s, :], patches[:, s, :], S["token_ps"] if s == SHIFTS - 1 else None,
                            start=s == 0, stop=s == SHIFTS - 1)

            def norms(g):
                pe.wait_ge(S["var_done"], now(g))
                pe.wait_ge(S["h0_done"], now(g))
                product(slot[3], ones[:], h0, S["lnmean_ps"])
                pe.wait_ge(S["sq_done"], now(g))
                product(slot[2], ones[:], sq, S["lnvar_ps"])

            def inputs(g):
                pe.wait_ge(S["xn_done"], now(g))
                product(slot[3][0:DM], mlpT[:], xn, S["up_ps"])
                product(slot[2][0:DM], presT[:], xn, S["pres_ps"])
                pe.wait_ge(S["xup_done"], now(g))
                product(slot[3], flT[:, 0, :], xup, S2[0]["fl_ps"])
                pe.wait_ge(S["zpre_done"], now(g))
                product(slot[2], flT[:, 1, :], xup, S2[1]["fl_ps"])

            def back(g, d, step):
                s, out = S2[d], slot[d]
                if step == "u":
                    pe.wait_ge(s["xin_done"], now(g))
                    pe.wait_ge(s["pre_done"], before(g))
                    product(out, inT[:, d, 0:D], xin[:, d, :], s["inu_ps"])
                elif step == "z":
                    pe.wait_ge(s["upad_done"], now(g))
                    product(out, inT[:, d, D:2 * D], xin[:, d, :], s["inz_ps"])
                elif step == "dt":
                    pe.wait_ge(s["sz_done"], now(g))
                    pe.wait_ge(s["u_done"], now(g))
                    product(out[0:RANK], xpT[:, d, 0:RANK], u[:, d, :], s["dt_ps"])
                elif step == "B":
                    pe.wait_ge(s["dtl_done"], now(g))
                    product(out, xpT[:, d, RANK:RANK + D], u[:, d, :], s["B_ps"])
                elif step == "C":
                    pe.wait_ge(s["Bs_done"], now(g))
                    product(out, xpT[:, d, RANK + D:RANK + 2 * D], u[:, d, :], s["C_ps"])
                else:
                    pe.wait_ge(s["Cs_done"], now(g))
                    product(out, dtT[:, d, :], dtl[:, d, :], s["pre_ps"])

            def both(g, step):
                for d in range(2):
                    back(g, d, step)

            pe.wait_ge(weights, WEIGHTS)
            pe.wait_ge(consts, 3)
            for n, src in enumerate((gamma[:], beta[:, :, 0:L])):
                for s in range(SHIFTS):
                    last = nc.tensor.matmul(psum[:, n * BANK:n * BANK + L], Wtok[:, s, :], src[:, s, :],
                                            start=s == 0, stop=s == SHIFTS - 1)
            last.then_inc(folded_ps, 1)
            pe.wait_ge(folded, 2)
            first_sums(0)
            second_sums(0)
            tokens(0)
            norms(0)
            inputs(0)
            with pe.Fori(0, GROUPS - 1) as g:
                both(g, "u")
                both(g, "z")
                first_sums(g + 1)
                both(g, "dt")
                both(g, "B")
                both(g, "C")
                second_sums(g + 1)
                both(g, "pre")
                tokens(g + 1)
                norms(g + 1)
                inputs(g + 1)
            for step in ("u", "z", "dt", "B", "C", "pre"):
                both(GROUPS - 1, step)

        @block.scalar
        def _(act):
            def image_scale(g):
                act.wait_ge(S["var_done"], now(g))
                act.activation(lnv[:], var[:], ACT.Ln).then_inc(S["lnv_done"], 1)
                act.wait_ge(S["lnv_done"], now(g))
                act.wait_ge(S["h0_done"], before(g))
                act.activation(rstd[:], lnv[:], ACT.Exp, scale=-0.5).then_inc(S["rstd_done"], 1)

            def norms(g):
                act.wait_ge(S["hc_done"], now(g))
                act.wait_ge(S["ss_done"], before(g))
                act.activation(sq[:], hc[:], ACT.Square).then_inc(S["sq_done"], 1)
                act.wait_ge(S["lnvar_ps"], now(g))
                act.wait_ge(S["xln_done"], before(g))
                act.activation(rs[:], slot[2], ACT.Ln, bias=eps_ln[:], scale=1.0 / D).then_inc(S["rs_done"], 1)
                act.wait_ge(S["rs_done"], now(g, 2, 1))
                act.activation(rs[:], rs[:], ACT.Exp, scale=-0.5).then_inc(S["rs_done"], 1)
                act.wait_ge(S["xln_done"], now(g))
                act.activation(sq[:], xln[:], ACT.Square).then_inc(S["sq3_done"], 1)
                act.wait_ge(S["ss_done"], now(g))
                act.activation(nrm[:], ss[:], ACT.Sqrt).then_inc(S["nrm_done"], 1)

            def inputs(g):
                act.wait_ge(S["up_ps"], now(g))
                act.activation(xup[:], slot[3][0:DM], ACT.Identity, bias=cols64[:, 0:1]).then_inc(S["xup_done"], 1)
                act.wait_ge(S["pres_ps"], now(g))
                act.wait_ge(S["zf_done"], before(g))
                act.activation(zpre[:], slot[2][0:DM], ACT.Identity, bias=cols64[:, 1:2]).then_inc(S["zpre_done"], 1)
                for d in range(2):
                    s = S2[d]
                    act.wait_ge(s["fl_ps"], now(g))
                    act.wait_ge(s["inz_ps"], before(g))
                    dst = imgs(xin[:, d, :])
                    act.activation(dst[:, :, ::-1] if d else dst, imgs(slot[3 - d][0:DM]), ACT.Identity,
                                   bias=cols64[:, 2 + d:3 + d]).then_inc(s["xin_done"], 1)

            def u_rows(g, d):
                s = S2[d]
                act.wait_ge(s["inu_ps"], now(g))
                act.wait_ge(s["conv_steps"], before(g, KCONV))
                act.activation(upad[:, d, :, KCONV - 1:], imgs(slot[d]), ACT.Copy).then_inc(s["upad_done"], 1)

            def z_rows(g, d):
                s = S2[d]
                act.wait_ge(s["inz_ps"], now(g))
                act.wait_ge(s["sz_stored"], before(g, 16))
                act.activation(sz[:, d, :], slot[d], ACT.Silu).then_inc(s["sz_done"], 1)
                act.wait_ge(s["sz_done"], now(g))
                act.dma_start(env["sz_d"][bass.ds(g * (2 * D) + d * D, D), :], sz[:, d, :]).then_inc(s["sz_stored"], 16)

            def silu(g, d):
                s = S2[d]
                act.wait_ge(s["conv_steps"], now(g, KCONV))
                act.wait_ge(s["uD_done"], before(g))
                act.wait_ge(s["du_done"], before(g))
                act.activation(u[:, d, :], conv[:, d, :], ACT.Silu).then_inc(s["u_done"], 1)

            def dt_rows(g, d):
                s = S2[d]
                act.wait_ge(s["dt_ps"], now(g))
                act.activation(dtl[:, d, :], slot[d][0:RANK], ACT.Copy).then_inc(s["dtl_done"], 1)

            def state_rows(g, d, product, done, stored, rows, dst):
                s = S2[d]
                act.wait_ge(s[product], now(g))
                act.wait_ge(s[stored], before(g, 16))
                act.activation(rows[:, d, :], slot[d], ACT.Copy).then_inc(s[done], 1)
                act.wait_ge(s[done], now(g))
                act.dma_start(dst[bass.ds(g * (2 * D) + d * D, D), :], rows[:, d, :]).then_inc(s[stored], 16)

            def step_rows(g, d):
                s = S2[d]
                act.wait_ge(s["pre_ps"], now(g))
                act.wait_ge(s["delta_steps"], before(g, DELTA))
                act.activation(pre[:, d, :], slot[d], ACT.Identity, bias=cols[:, 2 + 3 * d:3 + 3 * d]).then_inc(s["pre_done"], 1)

            def softplus(g):
                for d in range(2):
                    act.wait_ge(S2[d]["mag_done"], now(g))
                    act.activation(ex[:, d, :], ex[:, d, :], ACT.Exp, scale=-1.0).then_inc(S2[d]["ex_done"], 1)
                for d in range(2):
                    act.wait_ge(S2[d]["w1_done"], now(g))
                    act.activation(lg[:, d, :], w1[:, d, :], ACT.Ln).then_inc(S2[d]["lg_done"], 1)
                for d in range(2):
                    act.wait_ge(S2[d]["lg_done"], now(g))
                    act.activation(rw[:, d, :], lg[:, d, :], ACT.Exp, scale=-1.0).then_inc(S2[d]["rw_done"], 1)

            def back_start(g):
                for d in range(2):
                    u_rows(g, d)
                for d in range(2):
                    z_rows(g, d)
                for d in range(2):
                    silu(g, d)
                for d in range(2):
                    dt_rows(g, d)
                for d in range(2):
                    state_rows(g, d, "B_ps", "Bs_done", "B_stored", Bs, env["B_d"])
                for d in range(2):
                    state_rows(g, d, "C_ps", "Cs_done", "C_stored", Cs, env["C_d"])
                for d in range(2):
                    step_rows(g, d)

            act.wait_ge(weights, WEIGHTS)
            act.wait_ge(A_cut, 1)
            nc.scalar.activation(A_all[:], Alog, ACT.Exp).then_inc(A_exp, 1)
            image_scale(0)
            norms(0)
            inputs(0)
            with act.Fori(0, GROUPS - 1) as g:
                back_start(g)
                softplus(g)
                image_scale(g + 1)
                norms(g + 1)
                inputs(g + 1)
            back_start(GROUPS - 1)
            softplus(GROUPS - 1)

        @block.gpsimd
        def _(pool):
            def multiply(g):
                pool.wait_ge(S["img_loaded"], now(g, 16))
                pool.wait_ge(S["token_ps"], before(g))
                pool.tensor_tensor(imgs(patches[:, 0, :]), imgs(img[:]),
                                   gamma[:, 0:1, :].broadcast_to([128, IMGS, L]), ALU.mult).then_inc(S["patch_steps"], 1)
                step = 1
                grid = lambda ap: ap.rearrange("p (b i j) -> p b i j", i=GRID, j=GRID)
                for s in range(1, SHIFTS):
                    dr, dc = SHIFT_OF[s]
                    for qr in range(2):
                        for qc in range(2):
                            p = 64 * qr + 32 * qc
                            oi = (1 if qr == 0 else 0) if dr > 0 else (-1 if qr == 1 else 0)
                            oj = (1 if qc == 0 else 0) if dc > 0 else (-1 if qc == 1 else 0)
                            i0, i1 = max(0, -oi), min(GRID, GRID - oi)
                            j0, j1 = max(0, -oj), min(GRID, GRID - oj)
                            dst = grid(patches[p:p + 32, s, :])[:, :, i0:i1, j0:j1]
                            src = grid(img[p:p + 32, :])[:, :, i0 + oi:i1 + oi, j0 + oj:j1 + oj]
                            gam = grid(gamma[p:p + 32, s, :])[:, :, i0:i1, j0:j1]
                            pool.wait_ge(S["patch_steps"], now(g, STEPS, step))
                            pool.tensor_tensor(dst, src, gam.broadcast_to([32, IMGS, i1 - i0, j1 - j0]),
                                               ALU.mult).then_inc(S["patch_steps"], 1)
                            step += 1
                pool.wait_ge(S["patch_steps"], now(g, STEPS))

            def residual(g):
                pool.wait_ge(S["xln_done"], now(g))
                pool.wait_ge(S["hx_stored"], before(g, 16))
                pool.tensor_tensor(hx[:], h0[:], xln[:], ALU.add).then_inc(S["hx_done"], 1)

            def skip(g):
                for d in range(2):
                    s = S2[d]
                    pool.wait_ge(s["u_done"], now(g))
                    pool.wait_ge(s["uD_stored"], before(g, 16))
                    pool.sem_inc(carrier, 1)
                    pool.tensor_scalar(uD[:, d, :], u[:, d, :], cols[:, 3 + 3 * d:4 + 3 * d], None,
                                       ALU.mult).then_inc(s["uD_done"], 1)

            pool.wait_ge(weights, WEIGHTS)
            pool.wait_ge(folded, 3)
            multiply(0)
            residual(0)
            with pool.Fori(0, GROUPS - 1) as g:
                multiply(g + 1)
                skip(g)
                residual(g + 1)
            skip(GROUPS - 1)

        @block.vector
        def _(dve):
            cnt = count[:].unsqueeze(1).broadcast_to([128, IMGS, L])
            image_of = lambda v: v[:].unsqueeze(2).broadcast_to([128, IMGS, L])

            def first_sums(g):
                dve.wait_ge(S["img_loaded"], now(g, 16))
                dve.tensor_tensor(imgs(xw[:]), imgs(img[:]), cnt, ALU.mult).then_inc(S["sum1"], 1)
                dve.wait_ge(S["sum1"], now(g, 2, 1))
                dve.tensor_reduce(s1[:], imgs(xw[:]), X, ALU.add).then_inc(S["sum1"], 1)

            def second_sums(g):
                c = S["centre"]
                dve.wait_ge(S["sum1_ps"], now(g))
                dve.tensor_scalar(negmean[:], slot[3][:, 0:IMGS], -1.0 / AREA, None, ALU.mult).then_inc(c, 1)
                dve.wait_ge(c, now(g, CENTRE, 1))
                dve.tensor_tensor(imgs(xc[:]), imgs(img[:]), image_of(negmean), ALU.add).then_inc(c, 1)
                dve.wait_ge(c, now(g, CENTRE, 2))
                dve.tensor_tensor(imgs(xw[:]), imgs(xc[:]), cnt, ALU.mult).then_inc(c, 1)
                dve.scalar_tensor_tensor(m2[:], negmean[:], PADDED / AREA, negmean[:], ALU.mult, ALU.mult).then_inc(c, 1)
                dve.wait_ge(c, now(g, CENTRE, 4))
                dve.tensor_scalar(m2[:], m2[:], 1e-7, None, ALU.add).then_inc(c, 1)
                dve.tensor_tensor(xw[:], xw[:], xc[:], ALU.mult).then_inc(c, 1)
                dve.wait_ge(c, now(g, CENTRE, 6))
                dve.tensor_reduce(s2[:], imgs(xw[:]), X, ALU.add).then_inc(c, 1)

            def image_variance(g):
                dve.wait_ge(S["sum2_ps"], now(g))
                dve.wait_ge(S["centre"], now(g, CENTRE))
                dve.scalar_tensor_tensor(var[:], slot[3][:, 0:IMGS], 1.0 / AREA, m2[:], ALU.mult, ALU.add)\
                   .then_inc(S["var_done"], 1)

            def tokens(g):
                dve.wait_ge(S["token_ps"], now(g))
                for b in range(IMGS):
                    part = slice(b * L, (b + 1) * L)
                    dve.scalar_tensor_tensor(xc[:, part], G0[:], negmean[:, b:b + 1], slot[2][:, part],
                                             ALU.mult, ALU.add).then_inc(S["token"], 1)
                dve.wait_ge(S["rstd_done"], now(g))
                dve.wait_ge(S["token"], now(g, IMGS))
                dve.wait_ge(S["hx_done"], before(g))
                for b in range(IMGS):
                    part = slice(b * L, (b + 1) * L)
                    last = dve.scalar_tensor_tensor(h0[:, part], xc[:, part], rstd[:, b:b + 1], B0[:],
                                                    ALU.mult, ALU.add)
                last.then_inc(S["h0_done"], 1)

            def centre_tokens(g):
                dve.wait_ge(S["lnmean_ps"], now(g))
                dve.wait_ge(S["h0_done"], now(g))
                dve.scalar_tensor_tensor(hc[:], slot[3], -1.0 / D, h0[:], ALU.mult, ALU.add).then_inc(S["hc_done"], 1)

            def layer_norm(g):
                dve.wait_ge(S["rs_done"], now(g, 2))
                dve.wait_ge(S["hc_done"], now(g))
                dve.tensor_tensor(xln[:], hc[:], rs[:], ALU.mult).then_inc(S["xln_done"], 1)

            def unit_length(g):
                dve.wait_ge(S["sq3_done"], now(g))
                dve.tensor_reduce(ss[:], imgs(sq[:]), X, ALU.add).then_inc(S["ss_done"], 1)
                dve.wait_ge(S["nrm_done"], now(g))
                dve.tensor_scalar(inv[:], nrm[:], 1e-12, None, ALU.max).then_inc(S["inv_done"], 1)
                dve.wait_ge(S["inv_done"], now(g, 2, 1))
                dve.reciprocal(inv[:], inv[:]).then_inc(S["inv_done"], 1)
                dve.wait_ge(S["inv_done"], now(g, 2))
                dve.wait_ge(S["xln_done"], now(g))
                dve.tensor_tensor(imgs(xn[:]), imgs(xln[:]), image_of(inv), ALU.mult).then_inc(S["xn_done"], 1)

            def leaky(g):
                dve.wait_ge(S["zpre_done"], now(g))
                dve.wait_ge(S["zf_stored"], before(g, 16))
                dve.scalar_tensor_tensor(zf[:], zpre[:], 0.01, zpre[:], ALU.mult, ALU.max).then_inc(S["zf_done"], 1)

            def convolve(g, d):
                s = S2[d]
                dve.wait_ge(s["upad_done"], now(g))
                dve.wait_ge(s["dsplit"], before(g, SPLIT))
                c = imgs(conv[:, d, :])
                dve.tensor_scalar(c, upad[:, d, :, 0:L], convw[:, d, 0:1], cols[:, 1 + 3 * d:2 + 3 * d],
                                  ALU.mult, ALU.add).then_inc(s["conv_steps"], 1)
                for k in range(1, KCONV):
                    dve.wait_ge(s["conv_steps"], now(g, KCONV, k))
                    dve.scalar_tensor_tensor(c, upad[:, d, :, k:k + L], convw[:, d, k:k + 1], c,
                                             ALU.mult, ALU.add).then_inc(s["conv_steps"], 1)

            def softplus(g):
                for d in range(2):
                    s = S2[d]
                    dve.wait_ge(s["pre_done"], now(g))
                    dve.scalar_tensor_tensor(ex[:, d, :], pre[:, d, :], -1.0, pre[:, d, :], ALU.mult, ALU.max)\
                       .then_inc(s["mag_done"], 1)
                for d in range(2):
                    s = S2[d]
                    dve.wait_ge(s["ex_done"], now(g))
                    dve.wait_ge(s["usplit"], before(g, SPLIT))
                    dve.tensor_scalar(w1[:, d, :], ex[:, d, :], 1.0, None, ALU.add).then_inc(s["w1_done"], 1)
                for d in range(2):
                    s = S2[d]
                    dve.wait_ge(s["w1_done"], now(g))
                    dve.scalar_tensor_tensor(off[:, d, :], w1[:, d, :], -1.0, ex[:, d, :], ALU.add, ALU.subtract)\
                       .then_inc(s["off_done"], 1)

            def step_sizes(g, d):
                s, t = S2[d], S2[d]["delta_steps"]
                dve.wait_ge(s["lg_done"], now(g))
                dve.scalar_tensor_tensor(base[:, d, :], pre[:, d, :], 0.0, lg[:, d, :], ALU.max, ALU.add).then_inc(t, 1)
                dve.wait_ge(s["rw_done"], now(g))
                dve.wait_ge(s["off_done"], now(g))
                dve.tensor_tensor(off[:, d, :], off[:, d, :], rw[:, d, :], ALU.mult).then_inc(t, 1)
                dve.wait_ge(t, now(g, DELTA, 2))
                dve.tensor_tensor(delta[:, d, :], base[:, d, :], off[:, d, :], ALU.subtract).then_inc(t, 1)
                dve.wait_ge(t, now(g, DELTA, 3))
                dve.tensor_tensor(du[:, d, :], delta[:, d, :], u[:, d, :], ALU.mult).then_inc(s["du_done"], 1)
                dve.wait_ge(s["du_done"], now(g))
                dve.memset(imgs(delta[:, d, :])[:, :, 0:1], 0.0).then_inc(t, 1)

            def split(g, d, row, parts, steps, stored):
                dve.wait_ge(S2[d][stored], before(g, 48))
                rest = base[:, d, :]
                dve.tensor_copy(parts[:, d, 0, :], row[:, d, :]).then_inc(steps, 1)
                dve.wait_ge(steps, now(g, SPLIT, 1))
                dve.tensor_tensor(rest, row[:, d, :], parts[:, d, 0, :], ALU.subtract).then_inc(steps, 1)
                dve.wait_ge(steps, now(g, SPLIT, 2))
                dve.tensor_copy(parts[:, d, 1, :], rest).then_inc(steps, 1)
                dve.wait_ge(steps, now(g, SPLIT, 3))
                dve.tensor_tensor(rest, rest, parts[:, d, 1, :], ALU.subtract).then_inc(steps, 1)
                dve.wait_ge(steps, now(g, SPLIT, 4))
                dve.tensor_copy(parts[:, d, 2, :], rest).then_inc(steps, 1)

            def split_delta(g, d):
                dve.wait_ge(S2[d]["delta_steps"], now(g, DELTA))
                split(g, d, delta, dparts, S2[d]["dsplit"], "d_stored")

            def split_du(g, d):
                dve.wait_ge(S2[d]["dsplit"], now(g, SPLIT))
                split(g, d, du, uparts, S2[d]["usplit"], "u_stored")

            dve.memset(ones[:], 1.0).then_inc(consts, 1)
            dve.memset(eps_ln[:], 1e-5).then_inc(consts, 1)
            dve.memset(upad[:], 0.0).then_inc(consts, 1)
            dve.wait_ge(weights, WEIGHTS)
            dve.tensor_scalar(Alog, Alog, RATE_LOG_CAP, None, ALU.min).then_inc(A_cut, 1)
            dve.wait_ge(A_exp, 1)
            dve.tensor_scalar(A_all[:], A_all[:], -1.0, None, ALU.mult).then_inc(A_cut, 1)
            dve.wait_ge(folded_ps, 1)
            dve.tensor_copy(G0[:], psum[:, 0:L]).then_inc(folded, 1)
            dve.tensor_scalar(B0[:], psum[:, BANK:BANK + L], cols[:, 0:1], None, ALU.add).then_inc(folded, 1)
            dve.memset(patches[:], 0.0).then_inc(folded, 1)
            dve.wait_ge(folded, 3)
            dve.wait_ge(A_cut, 2)
            dve.wait_ge(consts, 3)
            first_sums(0)
            second_sums(0)
            image_variance(0)
            tokens(0)
            centre_tokens(0)
            layer_norm(0)
            unit_length(0)
            leaky(0)
            with dve.Fori(0, GROUPS - 1) as g:
                first_sums(g + 1)
                convolve(g, 0)
                convolve(g, 1)
                second_sums(g + 1)
                image_variance(g + 1)
                softplus(g)
                step_sizes(g, 0)
                step_sizes(g, 1)
                split_delta(g, 0)
                tokens(g + 1)
                split_delta(g, 1)
                centre_tokens(g + 1)
                split_du(g, 0)
                layer_norm(g + 1)
                unit_length(g + 1)
                split_du(g, 1)
                leaky(g + 1)
            for d in range(2):
                convolve(GROUPS - 1, d)
            softplus(GROUPS - 1)
            for d in range(2):
                step_sizes(GROUPS - 1, d)
                split_delta(GROUPS - 1, d)
                split_du(GROUPS - 1, d)

    nc.clear_and_free_semaphores(used)
    nc.all_engine_barrier()


def scan(nc, a, env):
    f32, bf16, ALU, ACT = (env[k] for k in ("f32", "bf16", "ALU", "ACT"))
    psum, A_all, R2 = env["psum"], env["A_all"], env["R2"]
    with ExitStack() as ctx:
        def sb(name, shape, dt=f32):
            return ctx.enter_context(nc.sbuf_tensor(name, shape, dt))

        def sem(name):
            return env["whole"].enter_context(nc.semaphore(name))

        spread32 = sb("spread32", [3 * UNIT, UNIT, 128])
        spread = sb("spread", [3 * UNIT, UNIT, 128], bf16)
        window = sb("window", [128, 2 * UNIT - 1])
        delta = sb("delta_in", [3 * UNIT, 2, T], bf16)
        du = sb("du_in", [3 * UNIT, 2, T], bf16)
        A = sb("A_in", [D, 2, UNIT])
        B, C = sb("B_in", [D, 2, T]), sb("C_in", [D, 2, T])
        H = sb("H", [D, HRING, T])
        P = sb("P", [D, PRING, T])
        ysb = sb("ysb", [UNIT, 2, T])

        sp_carrier = sem("sp_carrier2")
        spread_loaded, spread_cast, window_zero, window_done = (
            sem(n) for n in ("spread_loaded", "spread_cast", "window_zero", "window_done"))
        parts_loaded, A_loaded, B_loaded, C_loaded = (
            [sem(f"{n}_loaded{k}") for k in range(2)] for n in ("parts", "A", "B", "C"))
        decay_bcast = sem("decay_bcast")
        du_bcast = sem("du_bcast")
        decay_exp = sem("decay_exp")
        input_mult = sem("input_mult")
        out_mult = sem("out_mult")
        scanned = sem("scanned")
        reduced = sem("reduced")
        y_out = sem("y_out")
        y_stored = [sem(f"y_stored{k}") for k in range(2)]

        block = ctx.enter_context(nc.Block())

        @block.sync
        def _(sp):
            sp.dma_start(spread32[:], a["spread"]).then_inc(spread_loaded, 16)
            with sp.Fori(0, GROUPS) as g:
                for d in range(2):
                    with sp.Fori(0, 2) as h:
                        for k in range(2):
                            v = g * 8 + (h * 2 + (d * 4 + k))
                            free = g * (8 * UNIT) + (h * (2 * UNIT) + (d * 4 + k + 1) * UNIT)
                            sp.wait_ge(decay_bcast, free)
                            sp.sem_inc(sp_carrier, 1)
                            for q in range(3):
                                for src, dst in ((env["delta_d"], delta), (env["du_d"], du)):
                                    sp.dma_start(dst[q * UNIT:(q + 1) * UNIT, k, :],
                                                 src[bass.ds(v * UNIT + q * R2, UNIT), :]).then_inc(parts_loaded[k], 16)
                            sp.wait_ge(decay_exp, free)
                            sp.sem_inc(sp_carrier, 1)
                            sp.dma_start(A[:, k, :], A_all[:, d, bass.ds(h * (2 * UNIT) + k * UNIT, UNIT)])\
                              .then_inc(A_loaded[k], 16)
                            sp.wait_ge(input_mult, free)
                            sp.sem_inc(sp_carrier, 1)
                            sp.dma_start(B[:, k, :], env["B_d"][bass.ds(g * (2 * D) + d * D, D), :]).then_inc(B_loaded[k], 16)
                            sp.wait_ge(out_mult, free)
                            sp.sem_inc(sp_carrier, 1)
                            sp.dma_start(C[:, k, :], env["C_d"][bass.ds(g * (2 * D) + d * D, D), :]).then_inc(C_loaded[k], 16)

        @block.tensor
        def _(pe):
            nc.tensor.sem_inc(decay_bcast, BODY)
            nc.tensor.sem_inc(reduced, PRING)
            pe.wait_ge(spread_cast, 1)
            pe.wait_ge(window_done, 1)

            def spread_row(base, parts, j, done):
                for lo, hi in PIECES:
                    last = nc.tensor.matmul(psum[:, base + lo:base + hi], spread[:, j % UNIT, :],
                                            parts[:, j // UNIT % 2, lo:hi], start=True, stop=True)
                last.then_inc(done, 1)

            def spread_du(i, j):
                if j % UNIT == 0:
                    pe.wait_ge(parts_loaded[j // UNIT % 2], i * 96 + 96 * (j // BODY + 1))
                pe.wait_ge(input_mult, i * BODY + (j + BODY))
                spread_row(UBASE, du, j, du_bcast)

            def spread_delta(i, j):
                pe.wait_ge(scanned, i * BODY + (j + 1))
                spread_row(ABASE[j % 2], delta, j, decay_bcast)

            def reduce(i, j):
                c = j % UNIT
                pe.wait_ge(out_mult, i * BODY + (j + 1 + BODY))
                if c == 0:
                    pe.wait_ge(y_out, i * 2 + (j // UNIT + 1))
                for lo, hi in PIECES:
                    last = nc.tensor.matmul(psum[0:UNIT, YBASE + lo:YBASE + hi], window[:, UNIT - 1 - c:2 * UNIT - 1 - c],
                                            P[:, j % PRING, lo:hi], start=c == 0, stop=c == UNIT - 1)
                last.then_inc(reduced, 1)

            def body(i, ahead):
                for j in range(BODY):
                    if j + AHEAD < BODY or ahead:
                        spread_du(i, j + AHEAD)
                    reduce(i, j)
                    if j + AHEAD < BODY or ahead:
                        spread_delta(i, j + AHEAD)

            for j in range(AHEAD):
                spread_du(0, j)
                spread_delta(0, j)
            with pe.Fori(0, UNITS // 2 - 1) as i:
                body(i, True)
            body(UNITS // 2 - 1, False)

        @block.scalar
        def _(act):
            nc.scalar.sem_inc(decay_exp, BODY)
            nc.scalar.sem_inc(y_out, 1)
            for k in range(2):
                nc.scalar.sem_inc(y_stored[k], 16)
            act.wait_ge(spread_loaded, 16)
            act.activation(spread[:], spread32[:], ACT.Copy).then_inc(spread_cast, 1)

            def decay(n0, body0, j):
                c, k = j % UNIT, j // UNIT % 2
                if c == 0:
                    act.wait_ge(A_loaded[k], body0 * 16 + 16 * (j // BODY + 1))
                act.wait_ge(decay_bcast, n0 + (j + 1 + BODY))
                row = imgs(psum[:, ABASE[j % 2]:ABASE[j % 2] + T])[:, :, 1:]
                act.activation(row, row, ACT.Exp, scale=A[:, k, c:c + 1]).then_inc(decay_exp, 1)

            def body(i, ahead):
                n0 = i * BODY
                for j in range(BODY):
                    if j + AHEAD < BODY or ahead:
                        decay(n0, i, j + AHEAD)
                    if j % UNIT == UNIT - 1:
                        k = j // UNIT
                        act.wait_ge(reduced, n0 + (j + 1 + PRING))
                        act.wait_ge(y_stored[k], i * 16 + 16)
                        act.activation(ysb[:, k, :], psum[0:UNIT, YBASE:YBASE + T], ACT.Copy).then_inc(y_out, 1)
                        act.wait_ge(y_out, i * 2 + (k + 2))
                        act.dma_start(env["y_d"][bass.ds(i * BODY + k * UNIT, UNIT), :], ysb[:, k, :]).then_inc(y_stored[k], 16)

            for j in range(AHEAD):
                decay(0, 0, j)
            with act.Fori(0, UNITS // 2 - 1) as i:
                body(i, True)
            body(UNITS // 2 - 1, False)
            for k in range(2):
                act.wait_ge(y_stored[k], 16 * (UNITS // 2 + 1))

        @block.vector
        def _(dve):
            nc.vector.sem_inc(input_mult, BODY)
            nc.vector.sem_inc(scanned, 2)
            dve.memset(window[:], 0.0).then_inc(window_zero, 1)
            dve.wait_ge(window_zero, 1)
            dve.memset(window[:, UNIT - 1:UNIT], 1.0).then_inc(window_done, 1)

            def inputs(n0, body0, j):
                c, k = j % UNIT, j // UNIT % 2
                if c == 0:
                    dve.wait_ge(B_loaded[k], body0 * 16 + 16 * (j // BODY + 1))
                dve.wait_ge(du_bcast, n0 + (j + 1))
                dve.wait_ge(out_mult, n0 + (j + 1 + BODY - HRING))
                dve.tensor_tensor(H[:, j % HRING, :], psum[:, UBASE:UBASE + T], B[:, k, :],
                                  ALU.mult).then_inc(input_mult, 1)

            def body(i, ahead):
                n0 = i * BODY
                for j in range(BODY):
                    if j + 1 < BODY or ahead:
                        inputs(n0, i, j + 1)
                    dve.wait_ge(decay_exp, n0 + (j + 1 + BODY))
                    dve.wait_ge(input_mult, n0 + (j + 1 + BODY))
                    h = H[:, j % HRING, :]
                    dve.tensor_tensor_scan(h, psum[:, ABASE[j % 2]:ABASE[j % 2] + T], h, 0.0, ALU.mult, ALU.add)\
                       .then_inc(scanned, 1)

            inputs(0, 0, 0)
            with dve.Fori(0, UNITS // 2 - 1) as i:
                body(i, True)
            body(UNITS // 2 - 1, False)

        @block.gpsimd
        def _(pool):
            nc.gpsimd.sem_inc(out_mult, BODY)
            with pool.Fori(0, UNITS // 2) as i:
                n0 = i * BODY
                for j in range(BODY):
                    k = j // UNIT
                    if j % UNIT == 0:
                        pool.wait_ge(C_loaded[k], i * 16 + 16)
                    pool.wait_ge(scanned, n0 + (j + 3))
                    pool.wait_ge(reduced, n0 + (j + 1))
                    pool.tensor_tensor(P[:, j % PRING, :], H[:, j % HRING, :], C[:, k, :], ALU.mult)\
                        .then_inc(out_mult, 1)


def experts(nc, a, env, out):
    f32, bf16, ALU, ACT, X = (env[k] for k in ("f32", "bf16", "ALU", "ACT", "X"))
    slot, ones, eps_ln = (env[k] for k in ("slot", "ones", "eps_ln"))
    EXPERT_OUT, HEAD = slot[2], slot[3]
    with ExitStack() as ctx:
        def sb(name, shape, dt=f32):
            return ctx.enter_context(nc.sbuf_tensor(name, shape, dt))

        def sem(name):
            return ctx.enter_context(nc.semaphore(name + "_3"))

        outpT, outT = sb("outpT", [D, 2, DM]), sb("outT", [DM, D])
        Ws, bs = sb("Ws", [D, E]), sb("bs", [128, NC, E])
        W1, W2 = sb("W1", [D, E, F]), sb("W2", [128, E, FC, D])
        b1, b2, outb = sb("b1", [128, E, FC]), sb("b2", [D, E]), sb("outb", [D, 1])
        ident, rank = sb("ident", [128, 128]), sb("rank", [128, NC, E])
        pick32 = sb("pick32", [E + 1, E + 1, 128])
        pick = sb("pick", [E, E, 128], bf16)
        y, uD, sz = (sb(n, [D, 2, T]) for n in ("y_r", "uD_r", "sz_r"))
        zf, hx = sb("zf_r", [DM, T]), sb("hx_r", [D, T])
        yu, gated, fus = sb("yu", [D, 2, T]), sb("gated", [D, 2, T]), sb("fus", [DM, T])
        hc, sq, lnr, rs = (sb(n, [D, T]) for n in ("hc2", "sq2", "lnr2", "rs2"))
        h1, xt = sb("h1", [D, 2, T]), sb("xt", [D, 2, T])
        lg, eq = sb("logits", [128, NC, E]), sb("eq", [128, NC, E])
        gate = sb("gate", [128, NC, E + 1])
        top, tot = sb("top", [128, NC]), sb("tot", [128, NC])
        gateT32, gateT = sb("gateT32", [E + 1, T]), sb("gateT", [E, T], bf16)
        chosen = sb("chosen", [128, 2, E, T], bf16)
        prob = sb("prob", [128, 2, T])
        acc = sb("acc", [D, T])
        hid = sb("hid", [128, HIDRING, T])
        tmp = sb("tmp", [D, 2, T])

        sp_carrier = sem("sp_carrier3")
        weights = sem("weights3")
        loaded, yu_done, gated_done = sem("loaded"), sem("yu_done"), sem("gated_done")
        mix_ps, fus_done, mixed_ps, h1_done = sem("mix_ps"), sem("fus_done"), sem("mixed_ps"), sem("h1_done")
        mean_ps, hc_done, sq_done, var_ps = sem("mean_ps"), sem("hc_done"), sem("sq_done"), sem("var_ps")
        lnr_done, rs_done, xt_done = sem("lnr_done"), sem("rs_done"), sem("xt_done")
        logits_ps, router, gateexp_done = sem("logits_ps"), sem("router"), sem("gateexp_done")
        gate_done, gateT_ps, gateT_done = sem("gate_done"), sem("gateT_ps"), sem("gateT_done")
        pick_done = sem("pick_done")
        gb_ps, gb_done = sem("gb_ps"), sem("gb_done")
        hid_ps, hid_done = sem("hid_ps"), sem("hid_done")
        y_ps = sem("y_ps")
        tmp_done = sem("tmp_done")
        acc_done = sem("acc_done")
        stored = [sem(f"stored{p}") for p in range(2)]
        block = ctx.enter_context(nc.Block())

        LOADED = 16 * 8
        WEIGHTS = 16 * (11 + NC)
        ROWS = E * FC
        BODIES = GROUPS // 2

        @block.sync
        def _(sp):
            for dst, src in (
                (outpT[:], a["outpT"]), (outT[:], a["outT"]), (Ws[:], a["Ws"]), (W1[:], a["W1"]), (W2[:], a["W2"]),
                (b1[:], a["b1"]), (b2[:], a["b2"]), (outb[:], a["outb"]), (ident[:], a["ident"]),
                (rank[:], a["rank"]), (pick32[:], a["pick"]),
            ):
                sp.dma_start(dst, src).then_inc(weights, 16)
            for c in range(NC):
                sp.dma_start(bs[:, c, :], a["bs"].broadcast_to([128, E])).then_inc(weights, 16)
            for s in (yu_done, gated_done, fus_done, h1_done, mix_ps):
                sp.sem_inc(s, 1)
            with sp.Fori(0, GROUPS) as g:
                for done in (yu_done, gated_done, fus_done, h1_done):
                    sp.wait_ge(done, g + 1)
                sp.sem_inc(sp_carrier, 1)
                for d in range(2):
                    for dst, src in ((y, env["y_d"]), (uD, env["uD_d"]), (sz, env["sz_d"])):
                        sp.dma_start(dst[:, d, :], src[bass.ds(g * (2 * D) + d * D, D), :]).then_inc(loaded, 16)
                sp.dma_start(zf[:], env["zf_d"][bass.ds(g * DM, DM), :]).then_inc(loaded, 16)
                sp.dma_start(hx[:], env["hx_d"][bass.ds(g * D, D), :]).then_inc(loaded, 16)

        @block.gpsimd
        def _(pool):
            with pool.Fori(0, GROUPS) as g:
                pool.wait_ge(loaded, g * LOADED + LOADED)
                pool.wait_ge(gated_done, g + 1)
                pool.tensor_tensor(yu[:], y[:], uD[:], ALU.add).then_inc(yu_done, 1)

        @block.tensor
        def _(pe):
            def product(dst, lhsT, rhs, done, start=True, stop=True):
                for lo, hi in PIECES:
                    last = nc.tensor.matmul(dst[:, lo:hi], lhsT, rhs[:, lo:hi], start=start, stop=stop)
                if done is not None:
                    last.then_inc(done, 1)

            def head(g, p, piece):
                if piece == 0:
                    pe.wait_ge(gb_done, g * SPREADS + 1)
                    pe.wait_ge(gated_done, g + 2)
                    product(HEAD[0:DM], outpT[:, 0, :], gated[:, 0, :], None, stop=False)
                    product(HEAD[0:DM], outpT[:, 1, :], gated[:, 1, :], mix_ps, start=False)
                elif piece == 1:
                    pe.wait_ge(fus_done, g + 2)
                    product(HEAD, outT[:], fus, mixed_ps)
                elif piece == 2:
                    pe.wait_ge(h1_done, g + 2)
                    product(HEAD, ones[:], h1[:, p, :], mean_ps)
                elif piece == 3:
                    pe.wait_ge(sq_done, g + 1)
                    product(HEAD, ones[:], sq, var_ps)
                elif piece == 4:
                    pe.wait_ge(xt_done, g + 1)
                    for c, (lo, hi) in enumerate(CHUNKS):
                        last = nc.tensor.matmul(HEAD[0:hi - lo, c * E:(c + 1) * E], xt[:, p, lo:hi], Ws[:],
                                                start=True, stop=True)
                    last.then_inc(logits_ps, 1)
                elif piece == 5:
                    pe.wait_ge(gate_done, g + 1)
                    for c, (lo, hi) in enumerate(CHUNKS):
                        last = nc.tensor.transpose(HEAD[0:E + 1, lo:hi], gate[0:hi - lo, c, :], ident[0:hi - lo, 0:hi - lo])
                    last.then_inc(gateT_ps, 1)
                elif piece == 6:
                    pe.wait_ge(gateT_done, g + 1)
                    product(HEAD, pick32[:, E, :], gateT32, gb_ps)
                else:
                    e = piece - 7
                    pe.wait_ge(gb_done, g * SPREADS + (e + 2))
                    product(HEAD, pick[:, e, :], gateT, gb_ps)

            def down(g, n):
                e, f = divmod(n, FC)
                pe.wait_ge(hid_done, g * ROWS + (n + 2))
                if f == 0:
                    pe.wait_ge(tmp_done, g * E + (e + 1))
                product(EXPERT_OUT, W2[:, e, f, :], hid[:, n % HIDRING, :], y_ps, start=f == 0, stop=f == FC - 1)

            def run_experts(g, p, following):
                for n in range(ROWS):
                    e, f = divmod(n, FC)
                    pe.wait_ge(hid_done, g * ROWS + n)
                    product(slot[n % 2], W1[:, e, f * 128:(f + 1) * 128], xt[:, p, :], hid_ps)
                    if n >= 1:
                        down(g, n - 1)
                    if following is not None and n in PE_HEAD:
                        head(following, 1 - p, PE_HEAD.index(n))
                down(g, ROWS - 1)

            pe.wait_ge(weights, WEIGHTS)
            pe.wait_ge(pick_done, 1)
            for piece in range(len(PE_HEAD)):
                head(0, 0, piece)
            with pe.Fori(0, BODIES - 1) as i:
                run_experts(i * 2, 0, i * 2 + 1)
                run_experts(i * 2 + 1, 1, i * 2 + 2)
            run_experts(GROUPS - 2, 0, GROUPS - 1)
            run_experts(GROUPS - 1, 1, None)

        @block.scalar
        def _(act):
            def head(g, p, piece):
                if piece == 0:
                    act.wait_ge(hc_done, g + 1)
                    act.activation(sq[:], hc[:], ACT.Square).then_inc(sq_done, 1)
                elif piece == 1:
                    act.wait_ge(var_ps, g + 1)
                    act.activation(lnr[:], HEAD, ACT.Ln, bias=eps_ln[:], scale=1.0 / D).then_inc(lnr_done, 1)
                    act.wait_ge(lnr_done, g + 1)
                    act.activation(rs[:], lnr[:], ACT.Exp, scale=-0.5).then_inc(rs_done, 1)
                elif piece == 2:
                    act.wait_ge(router, g * ROUTER + 3)
                    act.activation(lg[:], lg[:], ACT.Exp).then_inc(gateexp_done, 1)
                elif piece == 3:
                    act.wait_ge(gateT_ps, g + 1)
                    act.activation(gateT32[:], HEAD[0:E + 1], ACT.Copy)
                    act.activation(gateT[:], HEAD[0:E], ACT.Copy).then_inc(gateT_done, 1)
                else:
                    n = piece - 4
                    act.wait_ge(gb_ps, g * SPREADS + (n + 1))
                    act.activation(chosen[:, p, n - 1, :] if n else prob[:, p, :], HEAD, ACT.Copy).then_inc(gb_done, 1)

            def store(g, i, p):
                act.wait_ge(acc_done, g * ACC + ACC)
                act.dma_start(out[:, bass.ds(g * T, T)], h1[:, p, :]).then_inc(stored[p], 16)

            def run_experts(g, p, following):
                for n in range(ROWS):
                    e, f = divmod(n, FC)
                    act.wait_ge(hid_ps, g * ROWS + (n + 1))
                    act.wait_ge(y_ps, g * ROWS + (n + 1))
                    act.activation(hid[:, n % HIDRING, :], slot[n % 2], ACT.Gelu, bias=b1[:, e, f:f + 1])\
                       .then_inc(hid_done, 1)
                    if following is not None and n in ACT_HEAD:
                        head(following, 1 - p, ACT_HEAD.index(n))

            act.wait_ge(weights, WEIGHTS)
            act.activation(pick[:], pick32[0:E, 0:E, :], ACT.Copy).then_inc(pick_done, 1)
            act.sem_inc(gb_done, 1)
            act.sem_inc(hid_done, 1)
            for p in range(2):
                act.sem_inc(stored[p], 16)
            for piece in range(len(ACT_HEAD)):
                head(0, 0, piece)
            with act.Fori(0, BODIES - 1) as i:
                for p in range(2):
                    run_experts(i * 2 + p, p, i * 2 + (p + 1))
                    store(i * 2 + p, i, p)
            run_experts(GROUPS - 2, 0, GROUPS - 1)
            store(GROUPS - 2, BODIES - 1, 0)
            run_experts(GROUPS - 1, 1, None)
            store(GROUPS - 1, BODIES - 1, 1)
            for p in range(2):
                act.wait_ge(stored[p], 16 * BODIES + 16)

        @block.vector
        def _(dve):
            spread_of = lambda v: v[:].unsqueeze(2).broadcast_to([128, NC, E])

            def head(g, i, p, piece):
                if piece == 0:
                    dve.wait_ge(yu_done, g + 2)
                    dve.wait_ge(mix_ps, g + 1)
                    dve.tensor_tensor(gated[:, 0, :], yu[:, 0, :], sz[:, 0, :], ALU.mult)
                    dve.tensor_tensor(imgs(gated[:, 1, :])[:, :, ::-1], imgs(yu[:, 1, :]), imgs(sz[:, 1, :]), ALU.mult)\
                       .then_inc(gated_done, 1)
                    dve.wait_ge(mix_ps, g + 2)
                    dve.tensor_tensor(fus[:], HEAD[0:DM], zf[:], ALU.mult).then_inc(fus_done, 1)
                elif piece == 1:
                    dve.wait_ge(mixed_ps, g + 1)
                    dve.wait_ge(stored[p], i * 16 + 16)
                    dve.scalar_tensor_tensor(h1[:, p, :], HEAD, outb[:], hx[:], ALU.add, ALU.add).then_inc(h1_done, 1)
                elif piece == 2:
                    dve.wait_ge(mean_ps, g + 1)
                    dve.wait_ge(h1_done, g + 2)
                    dve.scalar_tensor_tensor(hc[:], HEAD, -1.0 / D, h1[:, p, :], ALU.mult, ALU.add).then_inc(hc_done, 1)
                elif piece == 3:
                    dve.wait_ge(rs_done, g + 1)
                    dve.wait_ge(hc_done, g + 1)
                    dve.tensor_tensor(xt[:, p, :], hc[:], rs[:], ALU.mult).then_inc(xt_done, 1)
                elif piece == 4:
                    dve.wait_ge(logits_ps, g + 1)
                    dve.tensor_tensor(lg[:].rearrange("p c e -> p (c e)"), HEAD[:, 0:NC * E],
                                      bs[:].rearrange("p c e -> p (c e)"), ALU.add).then_inc(router, 1)
                    dve.wait_ge(router, g * ROUTER + 1)
                    dve.tensor_reduce(top[:], lg[:], X, ALU.max).then_inc(router, 1)
                    dve.wait_ge(router, g * ROUTER + 2)
                    dve.tensor_tensor(lg[:], lg[:], spread_of(top), ALU.subtract).then_inc(router, 1)
                else:
                    dve.wait_ge(gateexp_done, g + 1)
                    dve.tensor_reduce(tot[:], lg[:], X, ALU.add).then_inc(router, 1)
                    dve.wait_ge(router, g * ROUTER + 4)
                    dve.reciprocal(tot[:], tot[:]).then_inc(router, 1)
                    dve.wait_ge(router, g * ROUTER + 5)
                    dve.tensor_tensor(lg[:], lg[:], spread_of(tot), ALU.mult).then_inc(router, 1)
                    dve.wait_ge(router, g * ROUTER + 6)
                    dve.tensor_reduce(gate[:, :, E:E + 1], lg[:], X, ALU.max).then_inc(router, 1)
                    dve.wait_ge(router, g * ROUTER + 7)
                    dve.tensor_tensor(eq[:], lg[:], gate[:, :, E:E + 1].broadcast_to([128, NC, E]), ALU.is_equal)\
                       .then_inc(router, 1)
                    dve.wait_ge(router, g * ROUTER + 8)
                    dve.tensor_tensor(eq[:], eq[:], rank[:], ALU.mult).then_inc(router, 1)
                    dve.wait_ge(router, g * ROUTER + 9)
                    dve.tensor_reduce(top[:], eq[:], X, ALU.max).then_inc(router, 1)
                    dve.wait_ge(router, g * ROUTER + 10)
                    dve.tensor_tensor(gate[:, :, 0:E], eq[:], spread_of(top), ALU.is_equal).then_inc(gate_done, 1)

            def run_experts(g, i, p, following):
                if following is not None:
                    head(following, i + p, 1 - p, 0)
                    head(following, i + p, 1 - p, 1)
                for e in range(E):
                    if e == 0:
                        dve.wait_ge(gb_done, g * SPREADS + (SPREADS + 1))
                    dve.wait_ge(y_ps, g * ROWS + (FC * e + FC + HIDRING))
                    out_e = tmp[:, e % 2, :] if e else acc[:]
                    dve.scalar_tensor_tensor(out_e, EXPERT_OUT, b2[:, e:e + 1], chosen[:, p, e, :],
                                             ALU.add, ALU.mult).then_inc(tmp_done, 1)
                    if e:
                        dve.wait_ge(tmp_done, g * E + (e + 2))
                        if e > 1:
                            dve.wait_ge(acc_done, g * ACC + (e - 1))
                        dve.tensor_tensor(acc[:], acc[:], out_e, ALU.add).then_inc(acc_done, 1)
                    if following is not None:
                        for piece in DVE_HEAD[e]:
                            head(following, i + p, 1 - p, piece)
                dve.wait_ge(acc_done, g * ACC + (E - 1))
                dve.tensor_tensor(acc[:], acc[:], prob[:, p, :], ALU.mult).then_inc(acc_done, 1)
                dve.wait_ge(acc_done, g * ACC + E)
                dve.tensor_tensor(h1[:, p, :], h1[:, p, :], acc[:], ALU.add).then_inc(acc_done, 1)

            dve.sem_inc(tmp_done, 1)
            dve.sem_inc(y_ps, HIDRING)
            dve.wait_ge(weights, WEIGHTS)
            for piece in range(6):
                head(0, 0, 0, piece)
            with dve.Fori(0, BODIES - 1) as i:
                run_experts(i * 2, i, 0, i * 2 + 1)
                run_experts(i * 2 + 1, i, 1, i * 2 + 2)
            run_experts(GROUPS - 2, BODIES - 1, 0, GROUPS - 1)
            run_experts(GROUPS - 1, BODIES - 1, 1, None)


SPREADS = E + 1
PE_HEAD = [1, 3, 5, 7, 11, 17] + list(range(19, 19 + SPREADS))
ACT_HEAD = [5, 7, 12, 17] + list(range(19, 19 + SPREADS))
DVE_HEAD = [[2], [3], [4], [5], [], [], [], []]
ROUTER = 10
ACC = E + 1
HIDRING = 4


def patch_rows(x):
    n = x.shape[0]
    x = x.reshape(n, CH, GRID, 2, HALF, GRID, 2, HALF)
    return x.transpose(3, 6, 1, 4, 7, 0, 2, 5).reshape(128, n, L)


def swap_halves(rows):
    return rows.reshape((2, 2, 32) + rows.shape[1:])[::-1, ::-1].reshape(rows.shape)


def layout(v):
    def shifts_first(t):
        rows = patch_rows(t.reshape(SHIFTS, CH, SIDE, SIDE))
        return np.concatenate([rows[:, :1], swap_halves(rows[:, 1:])], axis=1)

    W = v["L0_tok_W"].reshape(D, SHIFTS, CH, 2, HALF, 2, HALF).transpose(3, 5, 2, 4, 6, 1, 0).reshape(128, SHIFTS, D)
    W = np.concatenate([W[:, :1], swap_halves(W[:, 1:])], axis=1)
    at = lambda n: v["L0_attn_" + n]
    both = lambda n: np.stack([at("f_" + n), at("b_" + n)])
    ffn = lambda n: v["L0_ffn_" + n]
    spread = np.tile(np.eye(UNIT, dtype=np.float32), (3, 1))[:, :, None] * np.ones((1, 1, 128), np.float32)
    pick = np.eye(E + 1, dtype=np.float32)[:, :, None] * np.ones((1, 1, 128), np.float32)
    arrays = {
        "images": patch_rows(v["x"]).reshape(128, BATCH * L),
        "gamma": shifts_first(v["L0_tok_gamma"]), "beta": shifts_first(v["L0_tok_beta"]),
        "count": patch_rows(np.broadcast_to(keep_count(), (1, CH, SIDE, SIDE)))[:, 0],
        "Wtok": W, "mlpT": at("mlp_w").T, "presT": at("mlpres_w").T,
        "flT": np.pad(np.stack([at("fl_w").T, at("bl_w").T], axis=1), ((0, 0), (0, 0), (0, D - DM))),
        "inT": both("in_w").transpose(2, 0, 1), "xpT": both("xproj_w").transpose(2, 0, 1),
        "dtT": both("dt_w").transpose(2, 0, 1), "convw": both("conv_w").transpose(1, 0, 2),
        "cols": np.stack([v["L0_tok_b"], at("f_conv_b"), at("f_dt_b"), at("f_D"),
                          at("b_conv_b"), at("b_dt_b"), at("b_D")], axis=1),
        "cols64": np.stack([at("mlp_b"), at("mlpres_b"), at("fl_b"), at("bl_b")], axis=1),
        "Alog": both("Alog").transpose(2, 0, 1),
        "spread": spread,
        "outpT": both("outp_w").transpose(2, 0, 1), "outT": at("out_w").T, "outb": at("out_b")[:, None],
        "Ws": ffn("Ws"), "bs": ffn("bs")[None], "W1": ffn("W1").transpose(1, 0, 2),
        "W2": ffn("W2").reshape(E, FC, 128, D).transpose(2, 0, 1, 3),
        "b1": ffn("b1").reshape(E, FC, 128).transpose(2, 0, 1), "b2": ffn("b2").T,
        "ident": np.eye(128, dtype=np.float32),
        "rank": np.broadcast_to(np.arange(E, 0, -1, dtype=np.float32), (128, NC, E)),
        "pick": pick,
    }
    return {n: np.ascontiguousarray(x) for n, x in arrays.items()}


def kernel(**inputs):
    import concourse.bacc as bacc
    from concourse.bass_utils import run_bass_kernel_spmd

    nc = bacc.Bacc("TRN2", target_bir_lowering=False, num_devices=1)
    arrays = layout({n: np.asarray(x) for n, x in inputs.items()})
    args = {n: nc.dram_tensor(n + "_in", x.shape, mybir.dt.from_np(x.dtype), kind="ExternalInput").ap()
            for n, x in arrays.items()}
    out = nc.dram_tensor("out", (D, BATCH * L), mybir.dt.float32, kind="ExternalOutput").ap()
    build(nc, args, out)
    r = run_bass_kernel_spmd(nc, [{n + "_in": x for n, x in arrays.items()}], core_ids=[0])
    return np.ascontiguousarray(r.results[0]["out"].reshape(D, BATCH, L).transpose(1, 2, 0))
```

```python
from contextlib import ExitStack

import numpy as np

import concourse.bass as bass
from concourse import mybir

BATCH, CH, SIDE, PATCH, HALF = 128, 2, 104, 8, 4
GRID = SIDE // PATCH
L = GRID * GRID
D = 128
DM = 64
RANK = 16
KCONV = 4
IMGS = 4
GROUPS = BATCH // IMGS
T = IMGS * L
SHIFTS = 5
AREA = SHIFTS * CH * SIDE * SIDE
E, F = 8, 512
FC = F // 128
BANK = 512
PIECES = ((0, BANK), (BANK, T))
CHUNKS = [(c, min(c + 128, T)) for c in range(0, T, 128)]
NC = len(CHUNKS)
SHIFT_OF = (None, (4, -4), (4, 4), (-4, -4), (-4, 4))

UNIT = 32
UNITS = GROUPS * 2 * (D // UNIT)
BODY = 2 * UNIT
AHEAD = 4
RATE_LOG_CAP = 78.0
STEPS = 1 + 4 * (SHIFTS - 1)
CENTRE, DELTA, DSPLIT, SPLIT = 7, 3, 6, 5
HRING, PRING = 8, 4
YBASE = 6 * BANK
ABASE = (0, 2 * BANK)
UBASE = 4 * BANK


def keep_count():
    n = np.ones((SIDE, SIDE), np.float32)
    for dr, dc in SHIFT_OF[1:]:
        r, c = np.arange(SIDE) - dr, np.arange(SIDE) - dc
        n += ((r >= 0) & (r < SIDE))[:, None] & ((c >= 0) & (c < SIDE))[None, :]
    return n


PADDED = AREA - CH * int(keep_count().sum())


def build(nc, a, out):
    f32, bf16 = mybir.dt.float32, mybir.dt.bfloat16
    ALU, ACT = mybir.AluOpType, mybir.ActivationFunctionType
    X = mybir.AxisListType.X

    def dram(name, rows, cols, dt=f32):
        return nc.dram_tensor(name, [rows, cols], dt).ap()

    R2 = GROUPS * 2 * D
    delta_d = dram("delta_parts", 3 * R2, T, bf16)
    du_d = dram("du_parts", 3 * R2, T, bf16)
    B_d, C_d = dram("B_rows", R2, T), dram("C_rows", R2, T)
    uD_d, sz_d, y_d = dram("uD_rows", R2, T), dram("silu_z", R2, T), dram("y_rows", R2, T)
    zf_d = dram("branch_z", GROUPS * DM, T)
    hx_d = dram("residual", GROUPS * D, T)

    with ExitStack() as whole:
        psum = whole.enter_context(nc.psum_tensor("psum", [128, 8 * BANK], f32))
        slot = [psum[:, 2 * BANK * s:2 * BANK * s + T] for s in range(4)]
        A_all = whole.enter_context(nc.sbuf_tensor("A_all", [D, 2, D], f32))
        ones = whole.enter_context(nc.sbuf_tensor("ones", [128, 128], f32))
        eps_ln = whole.enter_context(nc.sbuf_tensor("eps_ln", [128, 1], f32))
        prepare(nc, a, locals())
        scan(nc, a, locals())
        experts(nc, a, locals(), out)


def imgs(ap):
    return ap.rearrange("p (b t) -> p b t", b=IMGS)


def now(g, per=1, k=None):
    return g * per + ((per if k is None else k) + 1)


def before(g, per=1):
    return g * per + 1


def prepare(nc, a, env):
    f32, bf16, ALU, ACT, X = (env[k] for k in ("f32", "bf16", "ALU", "ACT", "X"))
    psum, slot, ones, A_all, eps_ln = (env[k] for k in ("psum", "slot", "ones", "A_all", "eps_ln"))
    R2 = env["R2"]
    used = []
    with ExitStack() as ctx:
        def sb(name, shape, dt=f32):
            return ctx.enter_context(nc.sbuf_tensor(name, shape, dt))

        def sem(name):
            handle = nc.alloc_semaphore(name=name)
            used.append(handle)
            return handle

        gamma = sb("gamma", [128, SHIFTS, L])
        count = sb("count", [128, L])
        Wtok = sb("Wtok", [128, SHIFTS, D])
        mlpT, presT = sb("mlpT", [D, DM]), sb("presT", [D, DM])
        flT, inT = sb("flT", [DM, 2, D]), sb("inT", [DM, 2, 2 * D])
        xpT, dtT = sb("xpT", [D, 2, RANK + 2 * D]), sb("dtT", [RANK, 2, D])
        convw = sb("convw", [D, 2, KCONV])
        cols = sb("cols", [D, 7])
        cols64 = sb("cols64", [DM, 4])
        G0, B0 = sb("G0", [D, L]), sb("B0", [D, L])

        img = sb("img", [128, T])
        xw, xc = sb("xw", [128, T]), sb("xc", [128, T])
        s1, s2 = sb("s1", [128, IMGS]), sb("s2", [128, IMGS])
        negmean, m2, var, lnv, rstd = (sb(n, [128, IMGS]) for n in ("negmean", "m2", "var", "lnv", "rstd"))
        patches = sb("patches", [128, SHIFTS, T])
        h0, hc, sq, rs, xln, hx, xn = (sb(n, [D, T]) for n in ("h0", "hc", "sq", "rs", "xln", "hx", "xn"))
        ss, nrm, inv = (sb(n, [D, IMGS]) for n in ("ss", "nrm", "inv"))
        xup, zpre, zf = (sb(n, [DM, T]) for n in ("xup", "zpre", "zf"))
        xin = sb("xin", [DM, 2, T])
        upad = sb("upad", [D, 2, IMGS, L + KCONV - 1])
        sz, conv, u, uD = (sb(n, [D, 2, T]) for n in ("sz", "conv", "u", "uD"))
        dtl = sb("dtl", [RANK, 2, T])
        Bs, Cs, pre = (sb(n, [D, 2, T]) for n in ("Bs", "Cs", "pre"))
        ex, w1, lg, rw, off, base = (sb(n, [D, 2, T]) for n in ("ex", "w1", "lg", "rw", "off", "base"))
        delta, du = conv, w1
        dparts, uparts = sb("dparts", [D, 2, 3, T], bf16), sb("uparts", [D, 2, 3, T], bf16)
        beta = patches
        Alog = Cs[:, 0, 0:2 * D].rearrange("p (d c) -> p d c", d=2)

        weights, consts = sem("weights"), sem("consts")
        sp_carrier = sem("sp_carrier")
        A_exp, A_cut, folded, folded_ps = sem("A_exp"), sem("A_cut"), sem("folded"), sem("folded_ps")
        S = {n: sem(n) for n in (
            "img_loaded counted sum1 sum1_ps centre sum2_ps var_done lnv_done rstd_done patch_steps token_ps token h0_done "
            "lnmean_ps hc_done sq_done lnvar_ps rs_done xln_done sq3_done ss_done nrm_done inv_done xn_done "
            "hx_done hx_stored up_ps pres_ps xup_done zpre_done zf_done zf_stored").split()}
        S2 = [{n: sem(f"{n}_{d}") for n in (
            "fl_ps xin_done inu_ps inz_ps upad_done sz_done sz_stored conv_steps u_done uD_done uD_stored "
            "dt_ps B_ps dtl_done Bs_done B_stored C_ps Cs_done C_stored pre_ps pre_done mag_done ex_done w1_done "
            "lg_done rw_done off_done delta_steps du_done dsplit d_stored usplit u_stored").split()} for d in "fb"]
        WEIGHTS = 14 * 16

        block = ctx.enter_context(nc.Block())

        @block.sync
        def _(sp):
            for dst, src in (
                (gamma[:], a["gamma"]), (beta[:, :, 0:L], a["beta"]), (count[:], a["count"]), (Wtok[:], a["Wtok"]),
                (mlpT[:], a["mlpT"]), (presT[:], a["presT"]), (flT[:], a["flT"]), (inT[:], a["inT"]),
                (xpT[:], a["xpT"]), (dtT[:], a["dtT"]), (convw[:], a["convw"]), (cols[:], a["cols"]),
                (cols64[:], a["cols64"]), (Alog, a["Alog"]),
            ):
                sp.dma_start(dst, src).then_inc(weights, 16)
            for s in (*S.values(), *S2[0].values(), *S2[1].values()):
                sp.sem_inc(s, 1)

            def load(g):
                sp.wait_ge(S["patch_steps"], before(g, STEPS))
                sp.wait_ge(S["centre"], before(g, CENTRE))
                sp.sem_inc(sp_carrier, 1)
                sp.dma_start(img[:], a["images"][:, bass.ds(g * T, T)]).then_inc(S["img_loaded"], 16)

            def store_front(g):
                sp.wait_ge(S["hx_done"], now(g))
                sp.sem_inc(sp_carrier, 1)
                sp.dma_start(env["hx_d"][bass.ds(g * D, D), :], hx[:]).then_inc(S["hx_stored"], 16)
                sp.wait_ge(S["zf_done"], now(g))
                sp.sem_inc(sp_carrier, 1)
                sp.dma_start(env["zf_d"][bass.ds(g * DM, DM), :], zf[:]).then_inc(S["zf_stored"], 16)

            def store_back(g):
                for d in range(2):
                    s = S2[d]
                    sp.wait_ge(s["uD_done"], now(g))
                    sp.sem_inc(sp_carrier, 1)
                    sp.dma_start(env["uD_d"][bass.ds(g * (2 * D) + d * D, D), :], uD[:, d, :]).then_inc(s["uD_stored"], 16)
                for done, count, stored, dst, src in (("dsplit", DSPLIT, "d_stored", env["delta_d"], dparts),
                                                      ("usplit", SPLIT, "u_stored", env["du_d"], uparts)):
                    for d in range(2):
                        sp.wait_ge(S2[d][done], now(g, count))
                        sp.sem_inc(sp_carrier, 1)
                        for q in range(3):
                            sp.dma_start(dst[bass.ds(g * (2 * D) + (d * D + q * R2), D), :], src[:, d, q, :])\
                              .then_inc(S2[d][stored], 16)

            sp.wait_ge(folded, 3)
            load(0)
            load(1)
            load(2)
            store_front(0)
            with sp.Fori(0, GROUPS - 3) as g:
                load(g + 3)
                store_back(g)
                store_front(g + 1)
            for g in range(GROUPS - 3, GROUPS - 1):
                store_back(g)
                store_front(g + 1)
            store_back(GROUPS - 1)
            for n in ("hx_stored", "zf_stored"):
                sp.wait_ge(S[n], before(GROUPS, 16))
            for d in range(2):
                for n in ("sz_stored", "uD_stored", "B_stored", "C_stored"):
                    sp.wait_ge(S2[d][n], before(GROUPS, 16))
                for n in ("d_stored", "u_stored"):
                    sp.wait_ge(S2[d][n], before(GROUPS, 48))

        @block.tensor
        def _(pe):
            def product(dst, lhsT, rhs, done, start=True, stop=True):
                for lo, hi in PIECES:
                    last = nc.tensor.matmul(dst[:, lo:hi], lhsT, rhs[:, lo:hi], start=start, stop=stop)
                if done is not None:
                    last.then_inc(done, 1)

            def first_sums(g):
                pe.wait_ge(S["hc_done"], before(g))
                pe.wait_ge(S["sum1"], now(g))
                nc.tensor.matmul(slot[3][:, 0:IMGS], ones[:], s1[:], start=True, stop=True).then_inc(S["sum1_ps"], 1)

            def second_sums(g):
                pe.wait_ge(S["centre"], now(g, CENTRE))
                nc.tensor.matmul(slot[3][:, 0:IMGS], ones[:], s2[:], start=True, stop=True).then_inc(S["sum2_ps"], 1)

            def tokens(g):
                pe.wait_ge(S2[1]["xin_done"], before(g))
                pe.wait_ge(S["patch_steps"], now(g, STEPS))
                for s in range(SHIFTS):
                    product(slot[2], Wtok[:, s, :], patches[:, s, :], S["token_ps"] if s == SHIFTS - 1 else None,
                            start=s == 0, stop=s == SHIFTS - 1)

            def token_mean(g):
                pe.wait_ge(S2[0]["xin_done"], before(g))
                pe.wait_ge(S["h0_done"], now(g))
                product(slot[3], ones[:], h0, S["lnmean_ps"])

            def token_variance(g):
                pe.wait_ge(S["sq_done"], now(g))
                product(slot[2], ones[:], sq, S["lnvar_ps"])

            def inputs(g, pre):
                if pre is not None:
                    pe.wait_ge(S["var_done"], now(pre))
                pe.wait_ge(S["xn_done"], now(g))
                product(slot[3][0:DM], mlpT[:], xn, S["up_ps"])
                product(slot[2][0:DM], presT[:], xn, S["pres_ps"])
                pe.wait_ge(S["xup_done"], now(g))
                product(slot[3], flT[:, 0, :], xup, S2[0]["fl_ps"])
                pe.wait_ge(S["zpre_done"], now(g))
                product(slot[2], flT[:, 1, :], xup, S2[1]["fl_ps"])

            def back(g, d, step):
                s, out = S2[d], slot[d]
                if step == "u":
                    pe.wait_ge(s["xin_done"], now(g))
                    pe.wait_ge(s["Cs_done"], before(g))
                    product(out, inT[:, d, 0:D], xin[:, d, :], s["inu_ps"])
                elif step == "z":
                    pe.wait_ge(s["upad_done"], now(g))
                    product(out, inT[:, d, D:2 * D], xin[:, d, :], s["inz_ps"])
                elif step == "dt":
                    pe.wait_ge(s["sz_done"], now(g))
                    pe.wait_ge(s["u_done"], now(g))
                    product(out[0:RANK], xpT[:, d, 0:RANK], u[:, d, :], s["dt_ps"])
                elif step == "pre":
                    pe.wait_ge(s["dtl_done"], now(g))
                    product(out, dtT[:, d, :], dtl[:, d, :], s["pre_ps"])
                elif step == "B":
                    pe.wait_ge(s["pre_done"], now(g))
                    product(out, xpT[:, d, RANK:RANK + D], u[:, d, :], s["B_ps"])
                else:
                    pe.wait_ge(s["Bs_done"], now(g))
                    product(out, xpT[:, d, RANK + D:RANK + 2 * D], u[:, d, :], s["C_ps"])

            def both(g, step):
                if g is not None:
                    for d in range(2):
                        back(g, d, step)

            def turn(g, mid, pre):
                both(g, "u")
                both(g, "z")
                if mid is not None:
                    tokens(mid)
                both(g, "dt")
                both(g, "pre")
                if mid is not None:
                    token_mean(mid)
                both(g, "B")
                if pre is not None:
                    first_sums(pre)
                both(g, "C")
                if mid is not None:
                    token_variance(mid)
                if pre is not None:
                    second_sums(pre)
                if mid is not None:
                    inputs(mid, pre)

            pe.wait_ge(weights, WEIGHTS)
            pe.wait_ge(consts, 3)
            for n, src in enumerate((gamma[:], beta[:, :, 0:L])):
                for s in range(SHIFTS):
                    last = nc.tensor.matmul(psum[:, n * BANK:n * BANK + L], Wtok[:, s, :], src[:, s, :],
                                            start=s == 0, stop=s == SHIFTS - 1)
            last.then_inc(folded_ps, 1)
            pe.wait_ge(folded, 2)
            turn(None, None, 0)
            turn(None, 0, 1)
            with pe.Fori(0, GROUPS - 2) as g:
                turn(g, g + 1, g + 2)
            turn(GROUPS - 2, GROUPS - 1, None)
            turn(GROUPS - 1, None, None)

        @block.scalar
        def _(act):
            def image_log(g):
                act.wait_ge(S["var_done"], now(g))
                act.activation(lnv[:], var[:], ACT.Ln).then_inc(S["lnv_done"], 1)

            def image_scale(g):
                act.wait_ge(S["lnv_done"], now(g))
                act.wait_ge(S["h0_done"], before(g))
                act.activation(rstd[:], lnv[:], ACT.Exp, scale=-0.5).then_inc(S["rstd_done"], 1)

            def square(g):
                act.wait_ge(S["hc_done"], now(g))
                act.wait_ge(S["ss_done"], before(g))
                act.activation(sq[:], hc[:], ACT.Square).then_inc(S["sq_done"], 1)

            def token_log(g):
                act.wait_ge(S["lnvar_ps"], now(g))
                act.wait_ge(S["xln_done"], before(g))
                act.activation(rs[:], slot[2], ACT.Ln, bias=eps_ln[:], scale=1.0 / D).then_inc(S["rs_done"], 1)

            def token_scale(g):
                act.wait_ge(S["rs_done"], now(g, 2, 1))
                act.activation(rs[:], rs[:], ACT.Exp, scale=-0.5).then_inc(S["rs_done"], 1)

            def lengths(g):
                act.wait_ge(S["xln_done"], now(g))
                act.activation(sq[:], xln[:], ACT.Square).then_inc(S["sq3_done"], 1)
                act.wait_ge(S["ss_done"], now(g))
                act.activation(nrm[:], ss[:], ACT.Sqrt).then_inc(S["nrm_done"], 1)

            def inputs(g):
                act.wait_ge(S["up_ps"], now(g))
                act.activation(xup[:], slot[3][0:DM], ACT.Identity, bias=cols64[:, 0:1]).then_inc(S["xup_done"], 1)
                act.wait_ge(S["pres_ps"], now(g))
                act.wait_ge(S["zf_done"], before(g))
                act.activation(zpre[:], slot[2][0:DM], ACT.Identity, bias=cols64[:, 1:2]).then_inc(S["zpre_done"], 1)
                for d in range(2):
                    s = S2[d]
                    act.wait_ge(s["fl_ps"], now(g))
                    act.wait_ge(s["inz_ps"], before(g))
                    dst = imgs(xin[:, d, :])
                    act.activation(dst[:, :, ::-1] if d else dst, imgs(slot[3 - d][0:DM]), ACT.Identity,
                                   bias=cols64[:, 2 + d:3 + d]).then_inc(s["xin_done"], 1)

            def u_rows(g, d):
                s = S2[d]
                act.wait_ge(s["inu_ps"], now(g))
                act.wait_ge(s["conv_steps"], before(g, KCONV))
                act.activation(upad[:, d, :, KCONV - 1:], imgs(slot[d]), ACT.Copy).then_inc(s["upad_done"], 1)

            def z_rows(g, d):
                s = S2[d]
                act.wait_ge(s["inz_ps"], now(g))
                act.wait_ge(s["sz_stored"], before(g, 16))
                act.activation(sz[:, d, :], slot[d], ACT.Silu).then_inc(s["sz_done"], 1)
                act.wait_ge(s["sz_done"], now(g))
                act.dma_start(env["sz_d"][bass.ds(g * (2 * D) + d * D, D), :], sz[:, d, :]).then_inc(s["sz_stored"], 16)

            def silu(g, d):
                s = S2[d]
                act.wait_ge(s["conv_steps"], now(g, KCONV))
                act.wait_ge(s["uD_done"], before(g))
                act.wait_ge(s["du_done"], before(g))
                act.activation(u[:, d, :], conv[:, d, :], ACT.Silu).then_inc(s["u_done"], 1)

            def skip(g, d):
                s = S2[d]
                act.wait_ge(s["u_done"], now(g))
                act.wait_ge(s["uD_stored"], before(g, 16))
                act.activation(uD[:, d, :], u[:, d, :], ACT.Copy, scale=cols[:, 3 + 3 * d:4 + 3 * d])\
                   .then_inc(s["uD_done"], 1)

            def dt_rows(g, d):
                s = S2[d]
                act.wait_ge(s["dt_ps"], now(g))
                act.activation(dtl[:, d, :], slot[d][0:RANK], ACT.Copy).then_inc(s["dtl_done"], 1)

            def state_rows(g, d, product, done, stored, rows, dst):
                s = S2[d]
                act.wait_ge(s[product], now(g))
                act.wait_ge(s[stored], before(g, 16))
                act.activation(rows[:, d, :], slot[d], ACT.Copy).then_inc(s[done], 1)
                act.wait_ge(s[done], now(g))
                act.dma_start(dst[bass.ds(g * (2 * D) + d * D, D), :], rows[:, d, :]).then_inc(s[stored], 16)

            def step_rows(g, d):
                s = S2[d]
                act.wait_ge(s["pre_ps"], now(g))
                act.wait_ge(s["delta_steps"], before(g, DELTA))
                act.activation(ex[:, d, :], slot[d], ACT.Abs, bias=cols[:, 2 + 3 * d:3 + 3 * d]).then_inc(s["mag_done"], 1)
                act.activation(pre[:, d, :], slot[d], ACT.Identity, bias=cols[:, 2 + 3 * d:3 + 3 * d]).then_inc(s["pre_done"], 1)

            def turn(g, mid, pre):
                both = range(2) if g is not None else ()
                for d in both:
                    u_rows(g, d)
                for d in both:
                    z_rows(g, d)
                for d in both:
                    silu(g, d)
                for d in both:
                    dt_rows(g, d)
                for d in both:
                    step_rows(g, d)
                for d in both:
                    state_rows(g, d, "B_ps", "Bs_done", "B_stored", Bs, env["B_d"])
                for d in both:
                    state_rows(g, d, "C_ps", "Cs_done", "C_stored", Cs, env["C_d"])
                if mid is not None:
                    square(mid)
                for d in both:
                    act.wait_ge(S2[d]["mag_done"], now(g))
                    act.activation(ex[:, d, :], ex[:, d, :], ACT.Exp, scale=-1.0).then_inc(S2[d]["ex_done"], 1)
                for d in both:
                    act.wait_ge(S2[d]["w1_done"], now(g))
                    act.activation(lg[:, d, :], w1[:, d, :], ACT.Ln).then_inc(S2[d]["lg_done"], 1)
                if mid is not None:
                    token_log(mid)
                if pre is not None:
                    image_log(pre)
                if mid is not None:
                    token_scale(mid)
                for d in both:
                    act.wait_ge(S2[d]["lg_done"], now(g))
                    act.activation(rw[:, d, :], lg[:, d, :], ACT.Exp, scale=-1.0).then_inc(S2[d]["rw_done"], 1)
                if pre is not None:
                    image_scale(pre)
                if mid is not None:
                    lengths(mid)
                for d in both:
                    skip(g, d)
                if mid is not None:
                    inputs(mid)

            act.wait_ge(weights, WEIGHTS)
            act.wait_ge(A_cut, 1)
            nc.scalar.activation(A_all[:], Alog, ACT.Exp).then_inc(A_exp, 1)
            turn(None, None, 0)
            turn(None, 0, 1)
            with act.Fori(0, GROUPS - 2) as g:
                turn(g, g + 1, g + 2)
            turn(GROUPS - 2, GROUPS - 1, None)
            turn(GROUPS - 1, None, None)

        @block.gpsimd
        def _(pool):
            def multiply(g):
                pool.wait_ge(S["img_loaded"], now(g, 16))
                pool.wait_ge(S["token_ps"], before(g))
                pool.tensor_tensor(imgs(patches[:, 0, :]), imgs(img[:]),
                                   gamma[:, 0:1, :].broadcast_to([128, IMGS, L]), ALU.mult).then_inc(S["patch_steps"], 1)
                step = 1
                grid = lambda ap: ap.rearrange("p (b i j) -> p b i j", i=GRID, j=GRID)
                for s in range(1, SHIFTS):
                    dr, dc = SHIFT_OF[s]
                    for qr in range(2):
                        for qc in range(2):
                            p = 64 * qr + 32 * qc
                            oi = (1 if qr == 0 else 0) if dr > 0 else (-1 if qr == 1 else 0)
                            oj = (1 if qc == 0 else 0) if dc > 0 else (-1 if qc == 1 else 0)
                            i0, i1 = max(0, -oi), min(GRID, GRID - oi)
                            j0, j1 = max(0, -oj), min(GRID, GRID - oj)
                            dst = grid(patches[p:p + 32, s, :])[:, :, i0:i1, j0:j1]
                            src = grid(img[p:p + 32, :])[:, :, i0 + oi:i1 + oi, j0 + oj:j1 + oj]
                            gam = grid(gamma[p:p + 32, s, :])[:, :, i0:i1, j0:j1]
                            pool.wait_ge(S["patch_steps"], now(g, STEPS, step))
                            pool.tensor_tensor(dst, src, gam.broadcast_to([32, IMGS, i1 - i0, j1 - j0]),
                                               ALU.mult).then_inc(S["patch_steps"], 1)
                            step += 1
                pool.wait_ge(S["patch_steps"], now(g, STEPS))

            def counts(g):
                pool.wait_ge(S["img_loaded"], now(g, 16))
                pool.wait_ge(S["centre"], before(g, CENTRE))
                pool.tensor_tensor(imgs(xw[:]), imgs(img[:]), count[:].unsqueeze(1).broadcast_to([128, IMGS, L]),
                                   ALU.mult).then_inc(S["counted"], 1)

            def inputs(g, d):
                s = S2[d]
                pool.wait_ge(s["delta_steps"], now(g, DELTA))
                pool.tensor_tensor(du[:, d, :], delta[:, d, :], u[:, d, :], ALU.mult).then_inc(s["du_done"], 1)

            def residual(g):
                pool.wait_ge(S["xln_done"], now(g))
                pool.wait_ge(S["hx_stored"], before(g, 16))
                pool.tensor_tensor(hx[:], h0[:], xln[:], ALU.add).then_inc(S["hx_done"], 1)

            pool.wait_ge(weights, WEIGHTS)
            pool.wait_ge(folded, 3)
            counts(0)
            multiply(0)
            counts(1)
            multiply(1)
            residual(0)
            with pool.Fori(0, GROUPS - 2) as g:
                counts(g + 2)
                multiply(g + 2)
                residual(g + 1)
                inputs(g, 0)
                inputs(g, 1)
            residual(GROUPS - 1)
            for g in (GROUPS - 2, GROUPS - 1):
                inputs(g, 0)
                inputs(g, 1)

        @block.vector
        def _(dve):
            cnt = count[:].unsqueeze(1).broadcast_to([128, IMGS, L])
            image_of = lambda v: v[:].unsqueeze(2).broadcast_to([128, IMGS, L])

            def first_sums(g):
                dve.wait_ge(S["counted"], now(g))
                dve.tensor_reduce(s1[:], imgs(xw[:]), X, ALU.add).then_inc(S["sum1"], 1)

            def second_sums(g):
                c = S["centre"]
                dve.wait_ge(S["sum1_ps"], now(g))
                dve.tensor_scalar(negmean[:], slot[3][:, 0:IMGS], -1.0 / AREA, None, ALU.mult).then_inc(c, 1)
                dve.wait_ge(c, now(g, CENTRE, 1))
                dve.tensor_tensor(imgs(xc[:]), imgs(img[:]), image_of(negmean), ALU.add).then_inc(c, 1)
                dve.wait_ge(c, now(g, CENTRE, 2))
                dve.tensor_tensor(imgs(xw[:]), imgs(xc[:]), cnt, ALU.mult).then_inc(c, 1)
                dve.scalar_tensor_tensor(m2[:], negmean[:], PADDED / AREA, negmean[:], ALU.mult, ALU.mult).then_inc(c, 1)
                dve.wait_ge(c, now(g, CENTRE, 4))
                dve.tensor_scalar(m2[:], m2[:], 1e-7, None, ALU.add).then_inc(c, 1)
                dve.tensor_tensor(xw[:], xw[:], xc[:], ALU.mult).then_inc(c, 1)
                dve.wait_ge(c, now(g, CENTRE, 6))
                dve.tensor_reduce(s2[:], imgs(xw[:]), X, ALU.add).then_inc(c, 1)

            def image_variance(g):
                dve.wait_ge(S["sum2_ps"], now(g))
                dve.wait_ge(S["centre"], now(g, CENTRE))
                dve.scalar_tensor_tensor(var[:], slot[3][:, 0:IMGS], 1.0 / AREA, m2[:], ALU.mult, ALU.add)\
                   .then_inc(S["var_done"], 1)

            def tokens(g):
                dve.wait_ge(S["token_ps"], now(g))
                for b in range(IMGS):
                    part = slice(b * L, (b + 1) * L)
                    dve.scalar_tensor_tensor(xc[:, part], G0[:], negmean[:, b:b + 1], slot[2][:, part],
                                             ALU.mult, ALU.add).then_inc(S["token"], 1)
                dve.wait_ge(S["rstd_done"], now(g))
                dve.wait_ge(S["token"], now(g, IMGS))
                dve.wait_ge(S["hx_done"], before(g))
                for b in range(IMGS):
                    part = slice(b * L, (b + 1) * L)
                    last = dve.scalar_tensor_tensor(h0[:, part], xc[:, part], rstd[:, b:b + 1], B0[:],
                                                    ALU.mult, ALU.add)
                last.then_inc(S["h0_done"], 1)

            def centre_tokens(g):
                dve.wait_ge(S["lnmean_ps"], now(g))
                dve.wait_ge(S["h0_done"], now(g))
                dve.scalar_tensor_tensor(hc[:], slot[3], -1.0 / D, h0[:], ALU.mult, ALU.add).then_inc(S["hc_done"], 1)

            def layer_norm(g):
                dve.wait_ge(S["rs_done"], now(g, 2))
                dve.wait_ge(S["hc_done"], now(g))
                dve.tensor_tensor(xln[:], hc[:], rs[:], ALU.mult).then_inc(S["xln_done"], 1)

            def lengths(g):
                dve.wait_ge(S["sq3_done"], now(g))
                dve.tensor_reduce(ss[:], imgs(sq[:]), X, ALU.add).then_inc(S["ss_done"], 1)

            def unit_length(g):
                dve.wait_ge(S["nrm_done"], now(g))
                dve.tensor_scalar(inv[:], nrm[:], 1e-12, None, ALU.max).then_inc(S["inv_done"], 1)
                dve.wait_ge(S["inv_done"], now(g, 2, 1))
                dve.reciprocal(inv[:], inv[:]).then_inc(S["inv_done"], 1)
                dve.wait_ge(S["inv_done"], now(g, 2))
                dve.wait_ge(S["xln_done"], now(g))
                dve.tensor_tensor(imgs(xn[:]), imgs(xln[:]), image_of(inv), ALU.mult).then_inc(S["xn_done"], 1)

            def leaky(g):
                dve.wait_ge(S["zpre_done"], now(g))
                dve.wait_ge(S["zf_stored"], before(g, 16))
                dve.scalar_tensor_tensor(zf[:], zpre[:], 0.01, zpre[:], ALU.mult, ALU.max).then_inc(S["zf_done"], 1)

            def convolve(g, d):
                s = S2[d]
                dve.wait_ge(s["upad_done"], now(g))
                dve.wait_ge(s["du_done"], before(g))
                dve.wait_ge(s["dsplit"], before(g, DSPLIT))
                c = imgs(conv[:, d, :])
                dve.tensor_scalar(c, upad[:, d, :, 0:L], convw[:, d, 0:1], cols[:, 1 + 3 * d:2 + 3 * d],
                                  ALU.mult, ALU.add).then_inc(s["conv_steps"], 1)
                for k in range(1, KCONV):
                    dve.wait_ge(s["conv_steps"], now(g, KCONV, k))
                    dve.scalar_tensor_tensor(c, upad[:, d, :, k:k + L], convw[:, d, k:k + 1], c,
                                             ALU.mult, ALU.add).then_inc(s["conv_steps"], 1)

            def softplus(g):
                for d in range(2):
                    s = S2[d]
                    dve.wait_ge(s["ex_done"], now(g))
                    dve.wait_ge(s["usplit"], before(g, SPLIT))
                    dve.tensor_scalar(w1[:, d, :], ex[:, d, :], 1.0, None, ALU.add).then_inc(s["w1_done"], 1)
                for d in range(2):
                    s = S2[d]
                    dve.wait_ge(s["w1_done"], now(g))
                    dve.scalar_tensor_tensor(off[:, d, :], w1[:, d, :], -1.0, ex[:, d, :], ALU.add, ALU.subtract)\
                       .then_inc(s["off_done"], 1)

            def step_base(g, d):
                s, t = S2[d], S2[d]["delta_steps"]
                dve.wait_ge(s["pre_done"], now(g))
                dve.wait_ge(s["lg_done"], now(g))
                dve.scalar_tensor_tensor(base[:, d, :], pre[:, d, :], 0.0, lg[:, d, :], ALU.max, ALU.add).then_inc(t, 1)

            def step_sizes(g, d):
                s, t = S2[d], S2[d]["delta_steps"]
                dve.wait_ge(s["rw_done"], now(g))
                dve.wait_ge(s["off_done"], now(g))
                dve.tensor_tensor(off[:, d, :], off[:, d, :], rw[:, d, :], ALU.mult).then_inc(t, 1)
                dve.wait_ge(t, now(g, DELTA, 2))
                dve.tensor_tensor(delta[:, d, :], base[:, d, :], off[:, d, :], ALU.subtract).then_inc(t, 1)

            def split(g, d, row, parts, steps, stored, count):
                dve.wait_ge(S2[d][stored], before(g, 48))
                rest = base[:, d, :]
                dve.tensor_copy(parts[:, d, 0, :], row[:, d, :]).then_inc(steps, 1)
                dve.wait_ge(steps, now(g, count, 1))
                dve.tensor_tensor(rest, row[:, d, :], parts[:, d, 0, :], ALU.subtract).then_inc(steps, 1)
                dve.wait_ge(steps, now(g, count, 2))
                dve.tensor_copy(parts[:, d, 1, :], rest).then_inc(steps, 1)
                dve.wait_ge(steps, now(g, count, 3))
                dve.tensor_tensor(rest, rest, parts[:, d, 1, :], ALU.subtract).then_inc(steps, 1)
                dve.wait_ge(steps, now(g, count, 4))
                dve.tensor_copy(parts[:, d, 2, :], rest).then_inc(steps, 1)

            def split_delta(g, d):
                dve.wait_ge(S2[d]["delta_steps"], now(g, DELTA))
                steps = S2[d]["dsplit"]
                split(g, d, delta, dparts, steps, "d_stored", DSPLIT)
                dve.wait_ge(steps, now(g, DSPLIT, SPLIT))
                first = dparts[:, d, :, :].rearrange("p q (b t) -> p q b t", b=IMGS)[:, :, :, 0:1]
                dve.memset(first, 0.0).then_inc(steps, 1)

            def split_du(g, d):
                dve.wait_ge(S2[d]["dsplit"], now(g, DSPLIT))
                dve.wait_ge(S2[d]["du_done"], now(g))
                split(g, d, du, uparts, S2[d]["usplit"], "u_stored", SPLIT)

            def turn(g, mid, pre, last):
                if g is not None:
                    convolve(g, 0)
                    convolve(g, 1)
                if pre is not None:
                    first_sums(pre)
                if mid is not None:
                    tokens(mid)
                if last is not None:
                    split_du(last, 0)
                if mid is not None:
                    centre_tokens(mid)
                if pre is not None:
                    second_sums(pre)
                if last is not None:
                    split_du(last, 1)
                if pre is not None:
                    image_variance(pre)
                if g is not None:
                    softplus(g)
                    step_base(g, 0)
                    step_base(g, 1)
                if mid is not None:
                    layer_norm(mid)
                if g is not None:
                    step_sizes(g, 0)
                if mid is not None:
                    lengths(mid)
                if g is not None:
                    step_sizes(g, 1)
                if mid is not None:
                    unit_length(mid)
                if g is not None:
                    split_delta(g, 0)
                    split_delta(g, 1)
                if mid is not None:
                    leaky(mid)

            dve.memset(ones[:], 1.0).then_inc(consts, 1)
            dve.memset(eps_ln[:], 1e-5).then_inc(consts, 1)
            dve.memset(upad[:], 0.0).then_inc(consts, 1)
            dve.wait_ge(weights, WEIGHTS)
            dve.tensor_scalar(Alog, Alog, RATE_LOG_CAP, None, ALU.min).then_inc(A_cut, 1)
            dve.wait_ge(A_exp, 1)
            dve.tensor_scalar(A_all[:], A_all[:], -1.0, None, ALU.mult).then_inc(A_cut, 1)
            dve.wait_ge(folded_ps, 1)
            dve.tensor_copy(G0[:], psum[:, 0:L]).then_inc(folded, 1)
            dve.tensor_scalar(B0[:], psum[:, BANK:BANK + L], cols[:, 0:1], None, ALU.add).then_inc(folded, 1)
            dve.memset(patches[:], 0.0).then_inc(folded, 1)
            dve.wait_ge(folded, 3)
            dve.wait_ge(A_cut, 2)
            dve.wait_ge(consts, 3)
            turn(None, None, 0, None)
            turn(None, 0, 1, None)
            turn(0, 1, 2, None)
            with dve.Fori(0, GROUPS - 3) as i:
                turn(i + 1, i + 2, i + 3, i)
            turn(GROUPS - 2, GROUPS - 1, None, GROUPS - 3)
            turn(GROUPS - 1, None, None, GROUPS - 2)
            for d in range(2):
                split_du(GROUPS - 1, d)

    nc.clear_and_free_semaphores(used)
    nc.all_engine_barrier()


def scan(nc, a, env):
    f32, bf16, ALU, ACT = (env[k] for k in ("f32", "bf16", "ALU", "ACT"))
    psum, A_all, R2 = env["psum"], env["A_all"], env["R2"]
    with ExitStack() as ctx:
        def sb(name, shape, dt=f32):
            return ctx.enter_context(nc.sbuf_tensor(name, shape, dt))

        def sem(name):
            return env["whole"].enter_context(nc.semaphore(name))

        spread32 = sb("spread32", [3 * UNIT, UNIT, 128])
        spread = sb("spread", [3 * UNIT, UNIT, 128], bf16)
        window = sb("window", [128, 2 * UNIT - 1])
        delta = sb("delta_in", [3 * UNIT, 2, T], bf16)
        du = sb("du_in", [3 * UNIT, 2, T], bf16)
        A = sb("A_in", [D, 2, UNIT])
        B, C = sb("B_in", [D, 2, T]), sb("C_in", [D, 2, T])
        H = sb("H", [D, HRING, T])
        P = sb("P", [D, PRING, T])
        ysb = sb("ysb", [2 * UNIT, T])

        sp_carrier = sem("sp_carrier2")
        spread_loaded, spread_cast, window_zero, window_done = (
            sem(n) for n in ("spread_loaded", "spread_cast", "window_zero", "window_done"))
        parts_loaded, A_loaded, B_loaded, C_loaded = (
            [sem(f"{n}_loaded{k}") for k in range(2)] for n in ("parts", "A", "B", "C"))
        decay_bcast = sem("decay_bcast")
        du_bcast = sem("du_bcast")
        decay_exp = sem("decay_exp")
        input_mult = sem("input_mult")
        out_mult = sem("out_mult")
        scanned = sem("scanned")
        reduced = sem("reduced")
        y_out = sem("y_out")
        y_stored = sem("y_stored")

        block = ctx.enter_context(nc.Block())

        @block.sync
        def _(sp):
            sp.dma_start(spread32[:], a["spread"]).then_inc(spread_loaded, 16)
            with sp.Fori(0, GROUPS) as g:
                for d in range(2):
                    with sp.Fori(0, 2) as h:
                        for k in range(2):
                            v = g * 8 + (h * 2 + (d * 4 + k))
                            free = g * (8 * UNIT) + (h * (2 * UNIT) + (d * 4 + k + 1) * UNIT)
                            sp.wait_ge(decay_bcast, free)
                            sp.sem_inc(sp_carrier, 1)
                            for q in range(3):
                                for src, dst in ((env["delta_d"], delta), (env["du_d"], du)):
                                    sp.dma_start(dst[q * UNIT:(q + 1) * UNIT, k, :],
                                                 src[bass.ds(v * UNIT + q * R2, UNIT), :]).then_inc(parts_loaded[k], 16)
                            sp.wait_ge(decay_exp, free)
                            sp.sem_inc(sp_carrier, 1)
                            sp.dma_start(A[:, k, :], A_all[:, d, bass.ds(h * (2 * UNIT) + k * UNIT, UNIT)])\
                              .then_inc(A_loaded[k], 16)
                            sp.wait_ge(input_mult, free)
                            sp.sem_inc(sp_carrier, 1)
                            sp.dma_start(B[:, k, :], env["B_d"][bass.ds(g * (2 * D) + d * D, D), :]).then_inc(B_loaded[k], 16)
                            sp.wait_ge(out_mult, free)
                            sp.sem_inc(sp_carrier, 1)
                            sp.dma_start(C[:, k, :], env["C_d"][bass.ds(g * (2 * D) + d * D, D), :]).then_inc(C_loaded[k], 16)

        @block.tensor
        def _(pe):
            nc.tensor.sem_inc(decay_bcast, BODY)
            nc.tensor.sem_inc(reduced, PRING)
            pe.wait_ge(spread_cast, 1)
            pe.wait_ge(window_done, 1)

            def spread_row(base, parts, j, done):
                for lo, hi in PIECES:
                    last = nc.tensor.matmul(psum[:, base + lo:base + hi], spread[:, j % UNIT, :],
                                            parts[:, j // UNIT % 2, lo:hi], start=True, stop=True)
                last.then_inc(done, 1)

            def spread_du(i, j):
                if j % UNIT == 0:
                    pe.wait_ge(parts_loaded[j // UNIT % 2], i * 96 + 96 * (j // BODY + 1))
                pe.wait_ge(input_mult, i * BODY + (j + BODY))
                spread_row(UBASE, du, j, du_bcast)

            def spread_delta(i, j):
                pe.wait_ge(scanned, i * BODY + (j + 1))
                spread_row(ABASE[j % 2], delta, j, decay_bcast)

            def reduce(i, j):
                q, c = j % 2, j // 2
                pe.wait_ge(out_mult, i * BODY + (j + 1 + BODY))
                if j == 0:
                    pe.wait_ge(y_out, i + 1)
                for lo, hi in PIECES:
                    last = nc.tensor.matmul(psum[q * UNIT:(q + 1) * UNIT, YBASE + lo:YBASE + hi],
                                            window[:, UNIT - 1 - c:2 * UNIT - 1 - c],
                                            P[:, j % PRING, lo:hi], start=c == 0, stop=c == UNIT - 1)
                last.then_inc(reduced, 1)

            def body(i, ahead):
                for j in range(BODY):
                    if j + AHEAD < BODY or ahead:
                        spread_du(i, j + AHEAD)
                    if j % 2:
                        reduce(i, j - 1)
                        reduce(i, j)
                    if j + AHEAD < BODY or ahead:
                        spread_delta(i, j + AHEAD)

            for j in range(AHEAD):
                spread_du(0, j)
                spread_delta(0, j)
            with pe.Fori(0, UNITS // 2 - 1) as i:
                body(i, True)
            body(UNITS // 2 - 1, False)

        @block.scalar
        def _(act):
            nc.scalar.sem_inc(decay_exp, BODY)
            nc.scalar.sem_inc(y_out, 1)
            nc.scalar.sem_inc(y_stored, 32)
            act.wait_ge(spread_loaded, 16)
            act.activation(spread[:], spread32[:], ACT.Copy).then_inc(spread_cast, 1)

            def decay(n0, body0, j):
                c, k = j % UNIT, j // UNIT % 2
                if c == 0:
                    act.wait_ge(A_loaded[k], body0 * 16 + 16 * (j // BODY + 1))
                act.wait_ge(decay_bcast, n0 + (j + 1 + BODY))
                row = imgs(psum[:, ABASE[j % 2]:ABASE[j % 2] + T])[:, :, 1:]
                act.activation(row, row, ACT.Exp, scale=A[:, k, c:c + 1]).then_inc(decay_exp, 1)

            def body(i, ahead):
                n0 = i * BODY
                for j in range(BODY):
                    if j + AHEAD < BODY or ahead:
                        decay(n0, i, j + AHEAD)
                act.wait_ge(reduced, n0 + (BODY + PRING))
                act.wait_ge(y_stored, i * 32 + 32)
                act.activation(ysb[:], psum[0:2 * UNIT, YBASE:YBASE + T], ACT.Copy).then_inc(y_out, 1)
                act.wait_ge(y_out, i + 2)
                rows = env["y_d"][bass.ds(i * BODY, BODY), :].rearrange("(c q) t -> q c t", q=2)
                for q in range(2):
                    act.dma_start(rows[q], ysb[q * UNIT:(q + 1) * UNIT, :]).then_inc(y_stored, 16)

            for j in range(AHEAD):
                decay(0, 0, j)
            with act.Fori(0, UNITS // 2 - 1) as i:
                body(i, True)
            body(UNITS // 2 - 1, False)
            act.wait_ge(y_stored, 32 * (UNITS // 2 + 1))

        @block.vector
        def _(dve):
            nc.vector.sem_inc(input_mult, BODY)
            nc.vector.sem_inc(scanned, 2)
            dve.memset(window[:], 0.0).then_inc(window_zero, 1)
            dve.wait_ge(window_zero, 1)
            dve.memset(window[:, UNIT - 1:UNIT], 1.0).then_inc(window_done, 1)

            def inputs(n0, body0, j):
                c, k = j % UNIT, j // UNIT % 2
                if c == 0:
                    dve.wait_ge(B_loaded[k], body0 * 16 + 16 * (j // BODY + 1))
                dve.wait_ge(du_bcast, n0 + (j + 1))
                dve.wait_ge(out_mult, n0 + (j + 1 + BODY - HRING))
                dve.tensor_tensor(H[:, j % HRING, :], psum[:, UBASE:UBASE + T], B[:, k, :],
                                  ALU.mult).then_inc(input_mult, 1)

            def body(i, ahead):
                n0 = i * BODY
                for j in range(BODY):
                    if j + 1 < BODY or ahead:
                        inputs(n0, i, j + 1)
                    dve.wait_ge(decay_exp, n0 + (j + 1 + BODY))
                    dve.wait_ge(input_mult, n0 + (j + 1 + BODY))
                    h = H[:, j % HRING, :]
                    dve.tensor_tensor_scan(h, psum[:, ABASE[j % 2]:ABASE[j % 2] + T], h, 0.0, ALU.mult, ALU.add)\
                       .then_inc(scanned, 1)

            inputs(0, 0, 0)
            with dve.Fori(0, UNITS // 2 - 1) as i:
                body(i, True)
            body(UNITS // 2 - 1, False)

        @block.gpsimd
        def _(pool):
            nc.gpsimd.sem_inc(out_mult, BODY)
            with pool.Fori(0, UNITS // 2) as i:
                n0 = i * BODY
                for j in range(BODY):
                    k = j // UNIT
                    if j % UNIT == 0:
                        pool.wait_ge(C_loaded[k], i * 16 + 16)
                    pool.wait_ge(scanned, n0 + (j + 3))
                    pool.wait_ge(reduced, n0 + (j + 1))
                    pool.tensor_tensor(P[:, j % PRING, :], H[:, j % HRING, :], C[:, k, :], ALU.mult)\
                        .then_inc(out_mult, 1)


def experts(nc, a, env, out):
    f32, bf16, ALU, ACT, X = (env[k] for k in ("f32", "bf16", "ALU", "ACT", "X"))
    slot, ones, eps_ln = (env[k] for k in ("slot", "ones", "eps_ln"))
    EXPERT_OUT, HEAD = slot[2], slot[3]
    with ExitStack() as ctx:
        def sb(name, shape, dt=f32):
            return ctx.enter_context(nc.sbuf_tensor(name, shape, dt))

        def sem(name):
            return ctx.enter_context(nc.semaphore(name + "_3"))

        outpT, outT = sb("outpT", [D, 2, DM]), sb("outT", [DM, D])
        Ws, bs = sb("Ws", [D, E]), sb("bs", [128, NC, E])
        W1, W2 = sb("W1", [D, E, F]), sb("W2", [128, E, FC, D])
        b1, b2, outb = sb("b1", [128, E, FC]), sb("b2", [D, E]), sb("outb", [D, 1])
        ident, rank = sb("ident", [128, 128]), sb("rank", [128, NC, E])
        pick32 = sb("pick32", [E + 1, E + 1, 128])
        pick = sb("pick", [E, E, 128], bf16)
        y, uD, sz = (sb(n, [D, 2, T]) for n in ("y_r", "uD_r", "sz_r"))
        zf, hx = sb("zf_r", [DM, T]), sb("hx_r", [D, T])
        yu, gated, fus = sb("yu", [D, 2, T]), sb("gated", [D, 2, T]), sb("fus", [DM, T])
        hc, sq, root, rs = (sb(n, [D, T]) for n in ("hc2", "sq2", "root2", "rs2"))
        h1, xt = sb("h1", [D, 2, T]), sb("xt", [D, 2, T])
        lg, eq = sb("logits", [128, NC, E]), sb("eq", [128, NC, E])
        gate = sb("gate", [128, NC, E + 1])
        top, tot = sb("top", [128, NC]), sb("tot", [128, NC])
        gateT32, gateT = sb("gateT32", [E + 1, T]), sb("gateT", [E, T], bf16)
        chosen = sb("chosen", [128, 2, E, T], bf16)
        prob = sb("prob", [128, 2, T])
        acc = sb("acc", [D, T])
        hid = sb("hid", [128, HIDRING, T])
        tmp = sb("tmp", [D, 2, T])

        sp_carrier = sem("sp_carrier3")
        weights = sem("weights3")
        loaded, yu_done, gated_done = sem("loaded"), sem("yu_done"), sem("gated_done")
        mix_ps, fus_done, mixed_ps, h1_done = sem("mix_ps"), sem("fus_done"), sem("mixed_ps"), sem("h1_done")
        mean_ps, hc_done, sq_done, var_ps = sem("mean_ps"), sem("hc_done"), sem("sq_done"), sem("var_ps")
        root_done, rs_done, xt_done = sem("root_done"), sem("rs_done"), sem("xt_done")
        logits_ps, router, gateexp_done = sem("logits_ps"), sem("router"), sem("gateexp_done")
        gate_done, gateT_ps, gateT_done = sem("gate_done"), sem("gateT_ps"), sem("gateT_done")
        pick_done = sem("pick_done")
        gb_ps, gb_done = sem("gb_ps"), sem("gb_done")
        hid_ps, hid_done = sem("hid_ps"), sem("hid_done")
        y_ps = sem("y_ps")
        tmp_done = sem("tmp_done")
        acc_done = sem("acc_done")
        stored = [sem(f"stored{p}") for p in range(2)]
        block = ctx.enter_context(nc.Block())

        LOADED = 16 * 8
        WEIGHTS = 16 * (11 + NC)
        ROWS = E * FC
        BODIES = GROUPS // 2

        @block.sync
        def _(sp):
            for dst, src in (
                (outpT[:], a["outpT"]), (outT[:], a["outT"]), (Ws[:], a["Ws"]), (W1[:], a["W1"]), (W2[:], a["W2"]),
                (b1[:], a["b1"]), (b2[:], a["b2"]), (outb[:], a["outb"]), (ident[:], a["ident"]),
                (rank[:], a["rank"]), (pick32[:], a["pick"]),
            ):
                sp.dma_start(dst, src).then_inc(weights, 16)
            for c in range(NC):
                sp.dma_start(bs[:, c, :], a["bs"].broadcast_to([128, E])).then_inc(weights, 16)
            for s in (yu_done, gated_done, fus_done, h1_done, mix_ps):
                sp.sem_inc(s, 1)
            with sp.Fori(0, GROUPS) as g:
                for done in (yu_done, gated_done, fus_done, h1_done):
                    sp.wait_ge(done, g + 1)
                sp.sem_inc(sp_carrier, 1)
                for d in range(2):
                    for dst, src in ((y, env["y_d"]), (uD, env["uD_d"]), (sz, env["sz_d"])):
                        sp.dma_start(dst[:, d, :], src[bass.ds(g * (2 * D) + d * D, D), :]).then_inc(loaded, 16)
                sp.dma_start(zf[:], env["zf_d"][bass.ds(g * DM, DM), :]).then_inc(loaded, 16)
                sp.dma_start(hx[:], env["hx_d"][bass.ds(g * D, D), :]).then_inc(loaded, 16)

        @block.gpsimd
        def _(pool):
            with pool.Fori(0, GROUPS) as g:
                pool.wait_ge(loaded, g * LOADED + LOADED)
                pool.wait_ge(gated_done, g + 1)
                pool.tensor_tensor(yu[:], y[:], uD[:], ALU.add).then_inc(yu_done, 1)

        @block.tensor
        def _(pe):
            def product(dst, lhsT, rhs, done, start=True, stop=True):
                for lo, hi in PIECES:
                    last = nc.tensor.matmul(dst[:, lo:hi], lhsT, rhs[:, lo:hi], start=start, stop=stop)
                if done is not None:
                    last.then_inc(done, 1)

            def head(g, p, piece):
                if piece == 0:
                    pe.wait_ge(gb_done, g * SPREADS + 1)
                    pe.wait_ge(gated_done, g + 2)
                    product(HEAD[0:DM], outpT[:, 0, :], gated[:, 0, :], None, stop=False)
                    product(HEAD[0:DM], outpT[:, 1, :], gated[:, 1, :], mix_ps, start=False)
                elif piece == 1:
                    pe.wait_ge(fus_done, g + 2)
                    product(HEAD, outT[:], fus, mixed_ps)
                elif piece == 2:
                    pe.wait_ge(h1_done, g + 2)
                    product(HEAD, ones[:], h1[:, p, :], mean_ps)
                elif piece == 3:
                    pe.wait_ge(sq_done, g + 1)
                    product(HEAD, ones[:], sq, var_ps)
                elif piece == 4:
                    pe.wait_ge(xt_done, g + 1)
                    for c, (lo, hi) in enumerate(CHUNKS):
                        last = nc.tensor.matmul(HEAD[0:hi - lo, c * E:(c + 1) * E], xt[:, p, lo:hi], Ws[:],
                                                start=True, stop=True)
                    last.then_inc(logits_ps, 1)
                elif piece == 5:
                    pe.wait_ge(gate_done, g + 1)
                    for c, (lo, hi) in enumerate(CHUNKS):
                        last = nc.tensor.transpose(HEAD[0:E + 1, lo:hi], gate[0:hi - lo, c, :], ident[0:hi - lo, 0:hi - lo])
                    last.then_inc(gateT_ps, 1)
                elif piece == 6:
                    pe.wait_ge(gateT_done, g + 1)
                    product(HEAD, pick32[:, E, :], gateT32, gb_ps)
                else:
                    e = piece - 7
                    pe.wait_ge(gb_done, g * SPREADS + (e + 2))
                    product(HEAD, pick[:, e, :], gateT, gb_ps)

            def down(g, n):
                e, f = divmod(n, FC)
                pe.wait_ge(hid_done, g * ROWS + (n + 2))
                if f == 0:
                    pe.wait_ge(tmp_done, g * E + (e + 1))
                product(EXPERT_OUT, W2[:, e, f, :], hid[:, n % HIDRING, :], y_ps, start=f == 0, stop=f == FC - 1)

            def run_experts(g, p, following):
                for n in range(ROWS):
                    e, f = divmod(n, FC)
                    pe.wait_ge(hid_done, g * ROWS + n)
                    product(slot[n % 2], W1[:, e, f * 128:(f + 1) * 128], xt[:, p, :], hid_ps)
                    if n >= 1:
                        down(g, n - 1)
                    if following is not None and n in PE_HEAD:
                        head(following, 1 - p, PE_HEAD.index(n))
                down(g, ROWS - 1)

            pe.wait_ge(weights, WEIGHTS)
            pe.wait_ge(pick_done, 1)
            for piece in range(len(PE_HEAD)):
                head(0, 0, piece)
            with pe.Fori(0, BODIES - 1) as i:
                run_experts(i * 2, 0, i * 2 + 1)
                run_experts(i * 2 + 1, 1, i * 2 + 2)
            run_experts(GROUPS - 2, 0, GROUPS - 1)
            run_experts(GROUPS - 1, 1, None)

        @block.scalar
        def _(act):
            def head(g, p, piece):
                if piece == 0:
                    act.wait_ge(hc_done, g + 1)
                    act.activation(sq[:], hc[:], ACT.Square).then_inc(sq_done, 1)
                elif piece == 1:
                    act.wait_ge(var_ps, g + 1)
                    act.wait_ge(rs_done, g + 1)
                    act.activation(root[:], HEAD, ACT.Sqrt, bias=eps_ln[:], scale=1.0 / D).then_inc(root_done, 1)
                elif piece == 2:
                    act.wait_ge(router, g * ROUTER + 3)
                    act.activation(lg[:], lg[:], ACT.Exp).then_inc(gateexp_done, 1)
                elif piece == 3:
                    act.wait_ge(gateT_ps, g + 1)
                    act.activation(gateT32[:], HEAD[0:E + 1], ACT.Copy)
                    act.activation(gateT[:], HEAD[0:E], ACT.Copy).then_inc(gateT_done, 1)
                else:
                    n = piece - 4
                    act.wait_ge(gb_ps, g * SPREADS + (n + 1))
                    act.activation(chosen[:, p, n - 1, :] if n else prob[:, p, :], HEAD, ACT.Copy).then_inc(gb_done, 1)

            def store(g, i, p):
                act.wait_ge(acc_done, g * ACC + ACC)
                act.dma_start(out[:, bass.ds(g * T, T)], h1[:, p, :]).then_inc(stored[p], 16)

            def run_experts(g, p, following, earlier):
                for n in range(ROWS):
                    e, f = divmod(n, FC)
                    act.wait_ge(hid_ps, g * ROWS + (n + 1))
                    act.wait_ge(y_ps, g * ROWS + (n + 1))
                    act.activation(hid[:, n % HIDRING, :], slot[n % 2], ACT.Gelu, bias=b1[:, e, f:f + 1])\
                       .then_inc(hid_done, 1)
                    if n == STORE and earlier is not None:
                        store(*earlier)
                    if following is not None and n in ACT_HEAD:
                        head(following, 1 - p, ACT_HEAD.index(n))

            act.wait_ge(weights, WEIGHTS)
            act.activation(pick[:], pick32[0:E, 0:E, :], ACT.Copy).then_inc(pick_done, 1)
            act.sem_inc(gb_done, 1)
            act.sem_inc(hid_done, 1)
            for p in range(2):
                act.sem_inc(stored[p], 16)
            for piece in range(len(ACT_HEAD)):
                head(0, 0, piece)
            run_experts(0, 0, 1, None)
            with act.Fori(0, BODIES - 1) as i:
                run_experts(i * 2 + 1, 1, i * 2 + 2, (i * 2, i, 0))
                run_experts(i * 2 + 2, 0, i * 2 + 3, (i * 2 + 1, i, 1))
            run_experts(GROUPS - 1, 1, None, (GROUPS - 2, BODIES - 1, 0))
            store(GROUPS - 1, BODIES - 1, 1)
            for p in range(2):
                act.wait_ge(stored[p], 16 * BODIES + 16)

        @block.vector
        def _(dve):
            spread_of = lambda v: v[:].unsqueeze(2).broadcast_to([128, NC, E])

            def head(g, i, p, piece):
                if piece == 0:
                    dve.wait_ge(yu_done, g + 2)
                    dve.wait_ge(mix_ps, g + 1)
                    dve.tensor_tensor(gated[:, 0, :], yu[:, 0, :], sz[:, 0, :], ALU.mult)
                    dve.tensor_tensor(imgs(gated[:, 1, :])[:, :, ::-1], imgs(yu[:, 1, :]), imgs(sz[:, 1, :]), ALU.mult)\
                       .then_inc(gated_done, 1)
                    dve.wait_ge(mix_ps, g + 2)
                    dve.tensor_tensor(fus[:], HEAD[0:DM], zf[:], ALU.mult).then_inc(fus_done, 1)
                elif piece == 1:
                    dve.wait_ge(mixed_ps, g + 1)
                    dve.wait_ge(stored[p], i * 16 + 16)
                    dve.scalar_tensor_tensor(h1[:, p, :], HEAD, outb[:], hx[:], ALU.add, ALU.add).then_inc(h1_done, 1)
                elif piece == 2:
                    dve.wait_ge(mean_ps, g + 1)
                    dve.wait_ge(h1_done, g + 2)
                    dve.scalar_tensor_tensor(hc[:], HEAD, -1.0 / D, h1[:, p, :], ALU.mult, ALU.add).then_inc(hc_done, 1)
                elif piece == 3:
                    dve.wait_ge(root_done, g + 1)
                    dve.reciprocal(rs[:], root[:]).then_inc(rs_done, 1)
                    dve.wait_ge(rs_done, g + 2)
                    dve.wait_ge(hc_done, g + 1)
                    dve.tensor_tensor(xt[:, p, :], hc[:], rs[:], ALU.mult).then_inc(xt_done, 1)
                elif piece == 4:
                    dve.wait_ge(logits_ps, g + 1)
                    dve.tensor_tensor(lg[:].rearrange("p c e -> p (c e)"), HEAD[:, 0:NC * E],
                                      bs[:].rearrange("p c e -> p (c e)"), ALU.add).then_inc(router, 1)
                    dve.wait_ge(router, g * ROUTER + 1)
                    dve.tensor_reduce(top[:], lg[:], X, ALU.max).then_inc(router, 1)
                    dve.wait_ge(router, g * ROUTER + 2)
                    dve.tensor_tensor(lg[:], lg[:], spread_of(top), ALU.subtract).then_inc(router, 1)
                else:
                    dve.wait_ge(gateexp_done, g + 1)
                    dve.tensor_reduce(tot[:], lg[:], X, ALU.add).then_inc(router, 1)
                    dve.wait_ge(router, g * ROUTER + 4)
                    dve.reciprocal(tot[:], tot[:]).then_inc(router, 1)
                    dve.wait_ge(router, g * ROUTER + 5)
                    dve.tensor_tensor(lg[:], lg[:], spread_of(tot), ALU.mult).then_inc(router, 1)
                    dve.wait_ge(router, g * ROUTER + 6)
                    dve.tensor_reduce(gate[:, :, E:E + 1], lg[:], X, ALU.max).then_inc(router, 1)
                    dve.wait_ge(router, g * ROUTER + 7)
                    dve.tensor_tensor(eq[:], lg[:], gate[:, :, E:E + 1].broadcast_to([128, NC, E]), ALU.is_equal)\
                       .then_inc(router, 1)
                    dve.wait_ge(router, g * ROUTER + 8)
                    dve.tensor_tensor(eq[:], eq[:], rank[:], ALU.mult).then_inc(router, 1)
                    dve.wait_ge(router, g * ROUTER + 9)
                    dve.tensor_reduce(top[:], eq[:], X, ALU.max).then_inc(router, 1)
                    dve.wait_ge(router, g * ROUTER + 10)
                    dve.tensor_tensor(gate[:, :, 0:E], eq[:], spread_of(top), ALU.is_equal).then_inc(gate_done, 1)

            def run_experts(g, i, p, following):
                if following is not None:
                    head(following, i + p, 1 - p, 0)
                for e in range(E):
                    if e == 0:
                        dve.wait_ge(gb_done, g * SPREADS + (SPREADS + 1))
                    dve.wait_ge(y_ps, g * ROWS + (FC * e + FC + HIDRING))
                    out_e = tmp[:, e % 2, :] if e else acc[:]
                    dve.scalar_tensor_tensor(out_e, EXPERT_OUT, b2[:, e:e + 1], chosen[:, p, e, :],
                                             ALU.add, ALU.mult).then_inc(tmp_done, 1)
                    if e:
                        dve.wait_ge(tmp_done, g * E + (e + 2))
                        if e > 1:
                            dve.wait_ge(acc_done, g * ACC + (e - 1))
                        dve.tensor_tensor(acc[:], acc[:], out_e, ALU.add).then_inc(acc_done, 1)
                    if following is not None:
                        for piece in DVE_HEAD[e]:
                            head(following, i + p, 1 - p, piece)
                dve.wait_ge(acc_done, g * ACC + (E - 1))
                dve.tensor_tensor(acc[:], acc[:], prob[:, p, :], ALU.mult).then_inc(acc_done, 1)
                dve.wait_ge(acc_done, g * ACC + E)
                dve.tensor_tensor(h1[:, p, :], h1[:, p, :], acc[:], ALU.add).then_inc(acc_done, 1)

            dve.sem_inc(tmp_done, 1)
            dve.sem_inc(rs_done, 1)
            dve.sem_inc(y_ps, HIDRING)
            dve.wait_ge(weights, WEIGHTS)
            for piece in range(6):
                head(0, 0, 0, piece)
            with dve.Fori(0, BODIES - 1) as i:
                run_experts(i * 2, i, 0, i * 2 + 1)
                run_experts(i * 2 + 1, i, 1, i * 2 + 2)
            run_experts(GROUPS - 2, BODIES - 1, 0, GROUPS - 1)
            run_experts(GROUPS - 1, BODIES - 1, 1, None)


SPREADS = E + 1
PE_HEAD = [2, 4, 6, 8, 15, 22] + list(range(23, 23 + SPREADS))
ACT_HEAD = [7, 9, 16, 22] + list(range(23, 23 + SPREADS))
DVE_HEAD = [[1, 2], [], [3], [4], [5], [], [], []]
STORE = 2
ROUTER = 10
ACC = E + 1
HIDRING = 4


def patch_rows(x):
    n = x.shape[0]
    x = x.reshape(n, CH, GRID, 2, HALF, GRID, 2, HALF)
    return x.transpose(3, 6, 1, 4, 7, 0, 2, 5).reshape(128, n, L)


def swap_halves(rows):
    return rows.reshape((2, 2, 32) + rows.shape[1:])[::-1, ::-1].reshape(rows.shape)


def layout(v):
    def shifts_first(t):
        rows = patch_rows(t.reshape(SHIFTS, CH, SIDE, SIDE))
        return np.concatenate([rows[:, :1], swap_halves(rows[:, 1:])], axis=1)

    W = v["L0_tok_W"].reshape(D, SHIFTS, CH, 2, HALF, 2, HALF).transpose(3, 5, 2, 4, 6, 1, 0).reshape(128, SHIFTS, D)
    W = np.concatenate([W[:, :1], swap_halves(W[:, 1:])], axis=1)
    at = lambda n: v["L0_attn_" + n]
    both = lambda n: np.stack([at("f_" + n), at("b_" + n)])
    ffn = lambda n: v["L0_ffn_" + n]
    spread = np.tile(np.eye(UNIT, dtype=np.float32), (3, 1))[:, :, None] * np.ones((1, 1, 128), np.float32)
    pick = np.eye(E + 1, dtype=np.float32)[:, :, None] * np.ones((1, 1, 128), np.float32)
    arrays = {
        "images": patch_rows(v["x"]).reshape(128, BATCH * L),
        "gamma": shifts_first(v["L0_tok_gamma"]), "beta": shifts_first(v["L0_tok_beta"]),
        "count": patch_rows(np.broadcast_to(keep_count(), (1, CH, SIDE, SIDE)))[:, 0],
        "Wtok": W, "mlpT": at("mlp_w").T, "presT": at("mlpres_w").T,
        "flT": np.pad(np.stack([at("fl_w").T, at("bl_w").T], axis=1), ((0, 0), (0, 0), (0, D - DM))),
        "inT": both("in_w").transpose(2, 0, 1), "xpT": both("xproj_w").transpose(2, 0, 1),
        "dtT": both("dt_w").transpose(2, 0, 1), "convw": both("conv_w").transpose(1, 0, 2),
        "cols": np.stack([v["L0_tok_b"], at("f_conv_b"), at("f_dt_b"), at("f_D"),
                          at("b_conv_b"), at("b_dt_b"), at("b_D")], axis=1),
        "cols64": np.stack([at("mlp_b"), at("mlpres_b"), at("fl_b"), at("bl_b")], axis=1),
        "Alog": both("Alog").transpose(2, 0, 1),
        "spread": spread,
        "outpT": both("outp_w").transpose(2, 0, 1), "outT": at("out_w").T, "outb": at("out_b")[:, None],
        "Ws": ffn("Ws"), "bs": ffn("bs")[None], "W1": ffn("W1").transpose(1, 0, 2),
        "W2": ffn("W2").reshape(E, FC, 128, D).transpose(2, 0, 1, 3),
        "b1": ffn("b1").reshape(E, FC, 128).transpose(2, 0, 1), "b2": ffn("b2").T,
        "ident": np.eye(128, dtype=np.float32),
        "rank": np.broadcast_to(np.arange(E, 0, -1, dtype=np.float32), (128, NC, E)),
        "pick": pick,
    }
    return {n: np.ascontiguousarray(x) for n, x in arrays.items()}


def kernel(**inputs):
    import concourse.bacc as bacc
    from concourse.bass_utils import run_bass_kernel_spmd

    nc = bacc.Bacc("TRN2", target_bir_lowering=False, num_devices=1)
    arrays = layout({n: np.asarray(x) for n, x in inputs.items()})
    args = {n: nc.dram_tensor(n + "_in", x.shape, mybir.dt.from_np(x.dtype), kind="ExternalInput").ap()
            for n, x in arrays.items()}
    out = nc.dram_tensor("out", (D, BATCH * L), mybir.dt.float32, kind="ExternalOutput").ap()
    build(nc, args, out)
    r = run_bass_kernel_spmd(nc, [{n + "_in": x for n, x in arrays.items()}], core_ids=[0])
    return np.ascontiguousarray(r.results[0]["out"].reshape(D, BATCH, L).transpose(1, 2, 0))
```
